# Optimizing a Trainium2 kernel written in Bass

```python
import numpy as np
import jax
import jax.numpy as jnp

def _softmax(x, axis=-1):
    return jax.nn.softmax(x, axis=axis)

def _gelu(x):
    return jax.nn.gelu(x, approximate=True)

def _silu(x):
    return jax.nn.silu(x)

def _sigmoid(x):
    return jax.nn.sigmoid(x)

def _layernorm(x, axis=-1, eps=1e-05):
    m = jnp.mean(x, axis=axis, keepdims=True)
    v = jnp.var(x, axis=axis, keepdims=True)
    return (x - m) / jnp.sqrt(v + eps)

def _scatter_add(tgt, idx, src, axis=0):
    return tgt.at[idx].add(src)

def _segment_sum(src, seg, n):
    return jax.ops.segment_sum(src, seg, n)
kernel_name = 'mk_adj_ffn_d1_adj_r2_343eee'

def setup_inputs(seed: int=0):
    np.random.seed(seed)
    _w = jnp.asarray

    def _rec_inputs():
        import jax
        import jax.numpy as jnp
        _gk = jax.random.key(seed)
        x = -8.015e-05 + 0.9999 * jax.random.normal(jax.random.fold_in(_gk, 1), (128, 128, 128), jnp.float32)
        _a = jax.random.bernoulli(jax.random.fold_in(_gk, 2), 0.03125, (128, 128, 128))
        _a = jnp.logical_or(_a, jnp.swapaxes(_a, -1, -2))
        _a = jnp.logical_or(_a, jnp.eye(128, dtype=bool))
        _af = _a.astype(jnp.float32)
        _af = _af * jax.random.uniform(jax.random.fold_in(_gk, 3), (128, 128, 128), jnp.float32, 0.05, 0.999837)
        adj = _af
        return (x, adj)
    x, adj = _rec_inputs()

    def _L0_gnn_setup():
        import jax, jax.numpy as jnp
        import numpy as np
        GROUPS = [list(range(25)), [0, 1, 2, 3, 4, 5, 6, 7, 8], [0, 9, 10, 11, 12, 13, 14], [6, 7, 8, 12, 13, 14], [3, 4, 5, 9, 10, 11]]
        B, N, D_IN, D_HID = (4096, 25, 128, 256)

        def _graph_conv(x, adj, W, b):
            n = adj.shape[-1]
            A = adj + jnp.eye(n, dtype=adj.dtype)
            deg = jnp.sum(A, axis=-1)
            deg_safe = jnp.where(deg == 0, 1.0, deg)
            dinv = jnp.where(deg == 0, 0.0, deg_safe ** (-0.5))
            norm_adj = dinv[:, :, None] * A * dinv[:, None, :]
            support = jnp.einsum('bnd,de->bne', x, W)
            out = jnp.einsum('bnm,bme->bne', norm_adj, support) + b
            return jax.nn.relu(out)
        key = jax.random.key(seed)
        ks = jax.random.split(key, 7)
        s1 = float(np.sqrt(6.0 / (D_IN + D_HID)))
        s2 = float(np.sqrt(6.0 / (D_HID + D_IN)))
        return {'x': jax.random.normal(ks[0], (B, N, D_IN), dtype=jnp.float32), 'adj': jax.random.uniform(ks[1], (B, N, N), dtype=jnp.float32), 'W1': jax.random.uniform(ks[2], (5, D_IN, D_HID), jnp.float32, -s1, s1), 'b1': jnp.zeros((5, D_HID), dtype=jnp.float32), 'W2': jax.random.uniform(ks[3], (5, D_HID, D_IN), jnp.float32, -s2, s2), 'b2': jnp.zeros((5, D_IN), dtype=jnp.float32), 'fusion_w': jnp.ones((5,), dtype=jnp.float32)}
    _L0_gnn_all = _L0_gnn_setup()
    _L0_gnn_in = {k: v for k, v in _L0_gnn_all.items() if k in ('W1', 'b1', 'W2', 'b2', 'fusion_w')}
    del _L0_gnn_all

    def _L0_ffn_setup():
        import jax, jax.numpy as jnp
        import numpy as np
        TOP_K = 2
        LN_EPS = 1e-05
        key = jax.random.key(seed)
        ks = jax.random.split(key, 8)
        B, S, D, E, H = (16, 512, 128, 8, 512)
        x = jax.random.normal(ks[0], (B, S, D), dtype=jnp.float32)
        Wr = jax.random.normal(ks[1], (D, E), dtype=jnp.float32) * 0.1
        br = jnp.zeros((E,), dtype=jnp.float32)
        ln_g = jnp.ones((E, D), dtype=jnp.float32)
        ln_b = jnp.zeros((E, D), dtype=jnp.float32)
        W1 = jax.random.normal(ks[2], (E, D, H), dtype=jnp.float32) * (1.0 / np.sqrt(D))
        b1 = jnp.zeros((E, H), dtype=jnp.float32)
        W2 = jax.random.normal(ks[3], (E, H, D), dtype=jnp.float32) * (1.0 / np.sqrt(H))
        b2 = jnp.zeros((E, D), dtype=jnp.float32)
        return {'x': x, 'Wr': Wr, 'br': br, 'ln_g': ln_g, 'ln_b': ln_b, 'W1': W1, 'b1': b1, 'W2': W2, 'b2': b2}
    _L0_ffn_all = _L0_ffn_setup()
    _L0_ffn_in = {k: v for k, v in _L0_ffn_all.items() if k in ('Wr', 'br', 'ln_g', 'ln_b', 'W1', 'b1', 'W2', 'b2')}
    del _L0_ffn_all
    return {'x': x, 'adj': adj, 'L0_gnn_W1': _L0_gnn_in['W1'], 'L0_gnn_b1': _L0_gnn_in['b1'], 'L0_gnn_W2': _L0_gnn_in['W2'], 'L0_gnn_b2': _L0_gnn_in['b2'], 'L0_gnn_fusion_w': _L0_gnn_in['fusion_w'], 'L0_ffn_Wr': _L0_ffn_in['Wr'], 'L0_ffn_br': _L0_ffn_in['br'], 'L0_ffn_ln_g': _L0_ffn_in['ln_g'], 'L0_ffn_ln_b': _L0_ffn_in['ln_b'], 'L0_ffn_W1': _L0_ffn_in['W1'], 'L0_ffn_b1': _L0_ffn_in['b1'], 'L0_ffn_W2': _L0_ffn_in['W2'], 'L0_ffn_b2': _L0_ffn_in['b2']}

def reference(x, adj, L0_gnn_W1, L0_gnn_b1, L0_gnn_W2, L0_gnn_b2, L0_gnn_fusion_w, L0_ffn_Wr, L0_ffn_br, L0_ffn_ln_g, L0_ffn_ln_b, L0_ffn_W1, L0_ffn_b1, L0_ffn_W2, L0_ffn_b2):
    import jax
    import jax.numpy as jnp

    def _L0_gnn_ref(x, adj, W1, b1, W2, b2, fusion_w):
        import jax, jax.numpy as jnp
        import numpy as np
        GROUPS = [list(range(25)), [0, 1, 2, 3, 4, 5, 6, 7, 8], [0, 9, 10, 11, 12, 13, 14], [6, 7, 8, 12, 13, 14], [3, 4, 5, 9, 10, 11]]
        B, N, D_IN, D_HID = (4096, 25, 128, 256)

        def _graph_conv(x, adj, W, b):
            n = adj.shape[-1]
            A = adj + jnp.eye(n, dtype=adj.dtype)
            deg = jnp.sum(A, axis=-1)
            deg_safe = jnp.where(deg == 0, 1.0, deg)
            dinv = jnp.where(deg == 0, 0.0, deg_safe ** (-0.5))
            norm_adj = dinv[:, :, None] * A * dinv[:, None, :]
            support = jnp.einsum('bnd,de->bne', x, W)
            out = jnp.einsum('bnm,bme->bne', norm_adj, support) + b
            return jax.nn.relu(out)
        norm_w = jax.nn.softmax(fusion_w)
        fused = jnp.zeros_like(x)
        for g, idx_list in enumerate(GROUPS):
            idx = jnp.asarray(idx_list)
            x_g = x[:, idx, :]
            adj_g = adj[:, idx][:, :, idx]
            h = _graph_conv(x_g, adj_g, W1[g], b1[g])
            out_g = _graph_conv(h, adj_g, W2[g], b2[g])
            fused = fused.at[:, idx, :].add(norm_w[g] * out_g)
        return fused

    def _L0_ffn_ref(x, Wr, br, ln_g, ln_b, W1, b1, W2, b2):
        import jax, jax.numpy as jnp
        import numpy as np
        TOP_K = 2
        LN_EPS = 1e-05
        B, S, D = x.shape
        N = B * S
        xt = x.reshape(N, D)
        logits = xt @ Wr + br
        probs = jax.nn.softmax(logits, axis=-1)
        top_p, top_idx = jax.lax.top_k(probs, TOP_K)
        weights = top_p / top_p.sum(axis=-1, keepdims=True)
        mu = xt.mean(axis=-1, keepdims=True)
        var = ((xt - mu) ** 2).mean(axis=-1, keepdims=True)
        xn = (xt - mu) * jax.lax.rsqrt(var + LN_EPS)
        xe = xn[None, :, :] * ln_g[:, None, :] + ln_b[:, None, :]
        h = jax.nn.gelu(jnp.einsum('end,edh->enh', xe, W1) + b1[:, None, :], approximate=False)
        y = jnp.einsum('enh,ehd->end', h, W2) + b2[:, None, :]
        y_tok = jnp.transpose(y, (1, 0, 2))
        sel = jnp.take_along_axis(y_tok, top_idx[:, :, None], axis=1)
        out = (weights[:, :, None] * sel).sum(axis=1)
        return out.reshape(B, S, D)
    x = x + _L0_gnn_ref(_layernorm(x, axis=-1), adj, L0_gnn_W1, L0_gnn_b1, L0_gnn_W2, L0_gnn_b2, L0_gnn_fusion_w)
    x = x + _L0_ffn_ref(_layernorm(x, axis=-1), L0_ffn_Wr, L0_ffn_br, L0_ffn_ln_g, L0_ffn_ln_b, L0_ffn_W1, L0_ffn_b1, L0_ffn_W2, L0_ffn_b2)
    return x

_drawn_inputs = setup_inputs


def setup_inputs(seed=0):
    import zlib

    import numpy as np

    out = dict(_drawn_inputs(seed))
    spreads = {'L0_gnn_b1': (0.0, 0.45),
     'L0_gnn_b2': (0.0, 0.34),
     'L0_gnn_fusion_w': (1.0, 0.6),
     'L0_ffn_br': (0.0, 0.1),
     'L0_ffn_ln_g': (1.0, 0.2),
     'L0_ffn_ln_b': (0.0, 0.1),
     'L0_ffn_b1': (0.0, 0.1),
     'L0_ffn_b2': (0.0, 0.1)}
    factors = {}
    for name, (base, spread) in spreads.items():
        noise = np.random.default_rng([zlib.crc32(name.encode()), seed]).standard_normal(out[name].shape)
        drawn = base * np.exp(spread * noise) if base else spread * noise
        out[name] = jnp.asarray(drawn.astype(out[name].dtype))
    for name, factor in factors.items():
        out[name] = (out[name] * factor).astype(out[name].dtype)
    return out
```

```python
from contextlib import ExitStack

import concourse.bass as bass
import numpy as np
from concourse import mybir

ALU = mybir.AluOpType
ACT = mybir.ActivationFunctionType
AX_X = mybir.AxisListType.X
F32 = mybir.dt.float32
F16 = mybir.dt.float16
BF16 = mybir.dt.bfloat16
I32 = mybir.dt.int32

B = N = D = 128
GROUPS = [[(0, 25)], [(0, 9)], [(0, 1), (9, 6)], [(6, 3), (12, 3)], [(3, 3), (9, 3)]]
SIZE = [sum(c for _, c in r) for r in GROUPS]
BATCHES = [4, 8, 16, 16, 16]
OFF = [sum(SIZE[:g]) for g in range(6)]
OFF2 = [sum(s * s for s in SIZE[:g]) for g in range(6)]
NG = SIZE[0]
COLS = OFF[5]
HID = 256
ROWS = [BATCHES[g] * SIZE[g] for g in range(5)]
QUADS = [(g, q) for g in range(5) for q in range(B // BATCHES[g] // 4)]
NQ = len(QUADS)

E, H = 8, 512
HC = H // 128
PAIRS = E * (E - 1) // 2
CH = 32
CHUNKS = [32, 64, 96, 0]
GRP = CH // 4
MEAN, NBIAS, RSTD, WA, WB, TOKEN = 0, 128, 129, 130, 131, 132
ROW = 133
REGION = B * N // 128 + 1
DUMMY = PAIRS * REGION
TILES = B * N // 128 + PAIRS
RING = 6
AHEAD = 2
TABLE = TILES + AHEAD
EPS = 1e-5
S64 = 64.0
S4096 = S64 * S64
NOWHERE = 1 << 20
NEG = -1e30


def build(nc, x, adj, gW1, gb1, gW2, gb2, fusion, Wr, br, ln_g, ln_b, W1, b1, W2, b2, out):
    with ExitStack() as ctx:
        def sb(name, shape, dt=F32):
            return ctx.enter_context(nc.sbuf_tensor(name, shape, dt))

        def sem(name):
            return ctx.enter_context(nc.semaphore(name))

        xg_dram = [nc.dram_tensor(f"xg{g}", [B, SIZE[g] * D], F32).ap() for g in range(5)]
        nt_dram = [nc.dram_tensor(f"nt{g}", [B, SIZE[g] ** 2], F32).ap() for g in range(5)]
        go_dram = [nc.dram_tensor(f"go{g}", [B, SIZE[g] * D], F32).ap() for g in range(5)]
        pay_dram = nc.dram_tensor("pay_rows", [(DUMMY + 1) * 128, ROW], F32).ap()
        out_rows = out.rearrange("b n d -> (b n) d")

        bank = [ctx.enter_context(nc.psum_tensor(f"bank{i}", [128, 512], F32)) for i in range(8)]

        pay = sb("pay", [128, N, ROW])
        slot = sb("slot", [128, N], I32)
        deg = sb("deg", [128, 6, COLS])
        gw1 = sb("gw1", [128, 5, HID])
        gw2 = sb("gw2", [128, 5, 2, D])
        gb1s = sb("gb1s", [128, 5, 2])
        wb2 = sb("wb2", [128, 5, D])
        fus = sb("fus", [128, 5])
        fstat = sb("fstat", [128, 4])
        mask = [sb(f"mask{g}", [128, BATCHES[g]]) for g in range(4)]
        xpack = sb("xpack", [128, 2, 4, D])
        npack = sb("npack", [128, 2, 4, NG])
        bd = sb("bd", [128, 2, 4, 128])
        zs = sb("zs", [128, 2, 512])
        hs = sb("hs", [128, 2, 2, 4 * max(ROWS)])
        ss = sb("ss", [128, 2, 4, D])
        gpre = sb("gpre", [128, 4, D])
        gpost = sb("gpost", [128, 2, 4, D])
        stat = sb("stat", [128, CH, 6])
        ln = sb("ln", [128, 6, CH])
        y = sb("y", [128, 2, 4, D])
        yT = sb("yT", [128, 2, 512])
        wr = sb("wr", [128, E])
        brb = sb("brb", [128, E])
        rev = sb("rev", [128, E])
        logit = sb("logit", [128, CH, E])
        small = sb("small", [128, 16, CH])
        pairs = sb("pairs", [128, PAIRS])
        onehot = sb("onehot", [128, PAIRS, CH], BF16)
        running = sb("running", [128, PAIRS, CH], BF16)
        restart = sb("restart", [128, PAIRS, CH], BF16)
        rank = sb("rank", [128, PAIRS, CH])
        scratch = rank[:, :, :].rearrange("p a n -> p (a n)")
        pick = scratch[:, 0:CH * E].rearrange("p (n e) -> p n e", e=E)
        score = scratch[:, CH * E:2 * CH * E].rearrange("p (n e) -> p n e", e=E)
        inpair = scratch[0:PAIRS, 0:TABLE]
        ahead = scratch[0:PAIRS, TABLE:2 * TABLE]
        seen = sb("seen", [128, 5, PAIRS], BF16)
        ones16 = sb("ones16", [128, 128], BF16)
        below = sb("below", [128, 128], BF16)
        ident = sb("ident", [128, 128])
        vrow = sb("vrow", [1, 3, PAIRS])
        one = sb("one", [1, 1])
        tri = sb("tri", [PAIRS, PAIRS])
        tline = sb("tline", [PAIRS, TABLE])
        tcnt = sb("tcnt", [PAIRS, 8])
        tint = sb("tint", [PAIRS, 2], I32)
        tadd = sb("tadd", [1, 4, TABLE])
        table = sb("table", [1, 3, TABLE], I32)
        padrow = sb("padrow", [1, 2, PAIRS])
        padint = sb("padint", [1, PAIRS], I32)
        padding = sb("padding", [128, ROW])
        stage = sb("stage", [128, E * H * 2])
        w1f = stage[:, 0:E * H].rearrange("p (e h) -> p e h", e=E)
        w2f = stage[:, E * H:2 * E * H].rearrange("p (e c d) -> p e c d", e=E, c=HC)
        gl = stage[:, 0:COLS * D].rearrange("p (i d) -> p i d", d=D)
        split_w = sb("split_w", [128, 2 * E * H])
        w1s = split_w[:, 0:E * H].bitcast(F16).rearrange("p (e t h) -> p e t h", e=E, t=2)
        w2s = split_w[:, E * H:2 * E * H].bitcast(F16).rearrange("p (e t h) -> p e t h", e=E, t=2)
        xn = split_w[:, 0:NG * D].rearrange("p (i d) -> p i d", d=D)
        at0 = NG * D
        adjs = split_w[:, at0:at0 + NG * NG]
        at0 += NG * NG
        acomp = split_w[:, at0:at0 + OFF2[5]]
        at0 += OFF2[5]
        nt_sb = split_w[:, at0:at0 + OFF2[5]]
        lng = sb("lng", [128, E])
        lnb = sb("lnb", [128, E])
        g64 = sb("g64", [128, E])
        b1s = sb("b1s", [128, E * HC])
        b1t = sb("b1t", [128, E * HC])
        b2s = sb("b2s", [128, E * D], F16)
        b2f = zs[0:33, :, :].rearrange("p a n -> p (a n)")
        b2hi = bd[0:33, 0, :, :].rearrange("p k n -> p (k n)").bitcast(F16)
        ones64 = sb("ones64", [128, 128], F16)
        epsc = sb("epsc", [128, 1])

        flat = pay[:, :, :].rearrange("p n r -> p (n r)")
        at = [0]

        def take(words, dt=F32):
            v = flat[:, at[0]:at[0] + words]
            at[0] += words
            return v if dt == F32 else v.bitcast(dt)

        prow = [take(ROW) for _ in range(RING)]
        orow = [take(D) for _ in range(RING)]
        at[0] += at[0] % 2
        xnt = [take(D) for _ in range(2)]
        xh = [take(D // 2, F16) for _ in range(2)]
        xl = [take(D // 2, F16) for _ in range(2)]
        hid = [take(H) for _ in range(4)]
        hh = [take(H // 2, F16) for _ in range(4)]
        hl = [take(H // 2, F16) for _ in range(4)]

        in_graph = sem("in_graph")
        in_adj = sem("in_adj")
        in_gw = sem("in_gw")
        in_chunk = [sem(f"in_chunk{c}") for c in range(4)]
        in_router = sem("in_router")
        in_experts = sem("in_experts")
        in_b2 = sem("in_b2")
        xg_out = sem("xg_out")
        nt_out = sem("nt_out")
        in_pack = [sem(f"in_pack{i}") for i in range(2)]
        go_out = [sem(f"go_out{i}") for i in range(2)]
        in_gl = sem("in_gl")
        pads_out = sem("pads_out")
        consts = sem("consts")
        zeros = sem("zeros")
        vec = sem("vec")
        act_own = sem("act_own")
        xn_done = sem("xn_done")
        var_ready = sem("var_ready")
        root_ready = sem("root_ready")
        deg_ready = sem("deg_ready")
        nt_done = sem("nt_done")
        fmax_ready = sem("fmax_ready")
        fexp_ready = sem("fexp_ready")
        bd_ready = sem("bd_ready")
        z_ready = sem("z_ready")
        zs_ready = sem("zs_ready")
        h_ready = sem("h_ready")
        hs_ready = sem("hs_ready")
        s_ready = sem("s_ready")
        ss_ready = sem("ss_ready")
        o_ready = sem("o_ready")
        gpre_ready = sem("gpre_ready")
        gpost_ready = sem("gpost_ready")
        gl_added = sem("gl_added")
        ln_ready = sem("ln_ready")
        y_ready = sem("y_ready")
        yt_ready = sem("yt_ready")
        yT_ready = sem("yT_ready")
        logits_ready = sem("logits_ready")
        logits_taken = sem("logits_taken")
        gap_ready = sem("gap_ready")
        exp_ready = sem("exp_ready")
        hot_ready = sem("hot_ready")
        rank_ready = sem("rank_ready")
        rank_taken = sem("rank_taken")
        slots_ready = sem("slots_ready")
        rows_out = sem("rows_out")
        seen_ready = sem("seen_ready")
        w_high = sem("w_high")
        w_done = sem("w_done")
        b1_ready = sem("b1_ready")
        b2_done = sem("b2_done")
        cnt_ready = sem("cnt_ready")
        ntile_ready = sem("ntile_ready")
        tincl_ready = sem("tincl_ready")
        vcol_ready = sem("vcol_ready")
        member_ready = sem("member_ready")
        trow_ready = sem("trow_ready")
        table_ready = sem("table_ready")
        in_tile = [sem(f"in_tile{i}") for i in range(RING)]
        out_tile = [sem(f"out_tile{i}") for i in range(RING)]
        xn_ready = sem("xn_ready")
        xt_ready = sem("xt_ready")
        xh_ready = sem("xh_ready")
        xl_ready = sem("xl_ready")
        hid_ready = sem("hid_ready")
        gelu_ready = sem("gelu_ready")
        hh_ready = sem("hh_ready")
        split_ready = sem("split_ready")
        e_ready = sem("e_ready")
        half_ready = sem("half_ready")
        row_ready = sem("row_ready")
        row_seen = sem("row_seen")

        block = ctx.enter_context(nc.Block())

        def node_view(t, first, count):
            return t[:, first:first + count, 0:D]

        @block.sync
        def _(sp):
            sp.dma_start(pay[:, 0:16, 0:D], x[:, 0:16, :]).then_inc(in_graph, 16)
            sp.dma_start(pay[:, 16:NG, 0:D], x[:, 16:NG, :]).then_inc(in_graph, 16)
            sp.dma_start(adjs[:, :].rearrange("p (i j) -> p i j", j=NG), adj[:, 0:NG, 0:NG]).then_inc(in_adj, 16)
            c0 = CHUNKS[0]
            sp.dma_start(pay[:, c0:c0 + CH, 0:D], x[:, c0:c0 + CH, :]).then_inc(in_chunk[0], 16)
            sp.dma_start(wr[:, :], Wr).then_inc(in_router, 16)
            sp.dma_start(brb[:, :], br.rearrange("(o e) -> o e", o=1).to_broadcast([128, E])).then_inc(in_router, 16)
            sp.dma_start(gw1[:, :, :], gW1.rearrange("g d h -> d g h")).then_inc(in_gw, 16)
            sp.dma_start(gw2[:, :, :, :], gW2.rearrange("g (c p) d -> p g c d", c=2)).then_inc(in_gw, 16)
            with nc.allow_non_contiguous_dma(reason="small bias columns"):
                sp.dma_start(gb1s[:, :, :], gb1.rearrange("g (c p) -> p g c", c=2)).then_inc(in_gw, 16)
            sp.dma_start(wb2[:, :, :].rearrange("p g d -> p (g d)"),
                         gb2.rearrange("(o g) d -> o (g d)", o=1).to_broadcast([128, 5 * D])).then_inc(in_gw, 16)
            sp.dma_start(fus[:, :], fusion.rearrange("(o g) -> o g", o=1).to_broadcast([128, 5])).then_inc(in_gw, 16)
            sp.wait_ge(xn_done, 1)
            for g in range(5):
                to = 0
                for first, count in GROUPS[g]:
                    sp.dma_start(xg_dram[g][:, to * D:(to + count) * D],
                                 xn[:, first:first + count, :].rearrange("p i d -> p (i d)")).then_inc(xg_out, 16)
                    to += count
            sp.wait_ge(nt_done, 1)
            for g in range(5):
                sp.dma_start(nt_dram[g], nt_sb[:, OFF2[g]:OFF2[g + 1]]).then_inc(nt_out, 16)
            for c in (1, 2):
                c0 = CHUNKS[c]
                sp.dma_start(pay[:, c0:c0 + CH, 0:D], x[:, c0:c0 + CH, :]).then_inc(in_chunk[c], 16)
            sp.dma_start(pay[:, NG:CH, 0:D], x[:, NG:CH, :]).then_inc(in_chunk[3], 16)
            sp.dma_start(w1f, W1.rearrange("e d h -> d e h")).then_inc(in_experts, 16)
            for c in range(HC):
                sp.dma_start(w2f[:, :, c, :], W2[:, c * 128:(c + 1) * 128, :].rearrange("e p d -> p e d")).then_inc(in_experts, 16)
            with nc.allow_non_contiguous_dma(reason="small columns of scales and biases"):
                sp.dma_start(lng[:, :], ln_g.rearrange("e d -> d e")).then_inc(in_experts, 16)
                sp.dma_start(lnb[:, :], ln_b.rearrange("e d -> d e")).then_inc(in_experts, 16)
                sp.dma_start(b1t[:, :], b1.rearrange("e (c p) -> p (e c)", c=HC)).then_inc(in_experts, 16)
            sp.wait_ge(xg_out, 16 * sum(len(r) for r in GROUPS))
            sp.wait_ge(nt_out, 16 * 5)

            def load_pack(i):
                g, q = QUADS[i]
                p = ROWS[g]
                if i >= 2:
                    sp.wait_ge(z_ready, i - 1)
                    sp.wait_ge(bd_ready, i - 1)
                rows = xg_dram[g].rearrange("b (i d) -> (b i) d", d=D)[q * 4 * p:(q + 1) * 4 * p, :]
                sp.dma_start(xpack[0:p, i % 2, :, :], rows.rearrange("(k p) d -> p k d", k=4)).then_inc(in_pack[i % 2], 16)
                rows = nt_dram[g].rearrange("b (m n) -> (b m) n", n=SIZE[g])[q * 4 * p:(q + 1) * 4 * p, :]
                sp.dma_start(npack[0:p, i % 2, :, 0:SIZE[g]], rows.rearrange("(k p) n -> p k n", k=4))\
                    .then_inc(in_pack[i % 2], 16)

            load_pack(0)
            load_pack(1)
            for i, (g, q) in enumerate(QUADS):
                p = ROWS[g]
                if i + 2 < NQ:
                    load_pack(i + 2)
                sp.wait_ge(gpost_ready, i + 1)
                rows = go_dram[g].rearrange("b (i d) -> (b i) d", d=D)[q * 4 * p:(q + 1) * 4 * p, :]
                sp.dma_start(rows.rearrange("(k p) d -> p k d", k=4), gpost[0:p, i % 2, :, :])\
                    .then_inc(go_out[i % 2], 16)
            sp.wait_ge(o_ready, NQ)
            for r in (0, 32):
                sp.dma_start(b2f[r:r + 1, :], b2.rearrange("(o e) d -> o (e d)", o=1)).then_inc(in_b2, 16)
            for i in range(2):
                sp.wait_ge(go_out[i], 16 * (NQ // 2))
            sp.wait_ge(w_done, 1)
            sp.wait_ge(b1_ready, 1)
            for g in range(5):
                sp.dma_start(gl[:, OFF[g]:OFF[g + 1], :].rearrange("p i d -> p (i d)"), go_dram[g]).then_inc(in_gl, 16)
            sp.wait_ge(consts, 1)
            sp.dma_start(pay_dram[DUMMY * 128:(DUMMY + 1) * 128, :], padding[:, :]).then_inc(pads_out, 16)
            sp.wait_ge(table_ready, 1)
            for p in range(PAIRS):
                r = sp.value_load(padint[0:1, p:p + 1], min_val=0, max_val=DUMMY * 128 - 128)
                sp.dma_start(pay_dram[bass.ds(r, 128), :], padding[:, :]).then_inc(pads_out, 16)
            sp.wait_ge(pads_out, 16 * (PAIRS + 1))
            sp.wait_ge(rows_out, 16 * N)

            def load_tile(t, s, round_):
                r = sp.value_load(table[0:1, 2, bass.ds(t, 1)], min_val=0, max_val=DUMMY)
                r = sp.snap(r * 128)
                if round_ is not None:
                    sp.wait_ge(out_tile[s], round_ * 16)
                sp.dma_start(prow[s], pay_dram[bass.ds(r, 128), :]).then_inc(in_tile[s], 16)

            for t in range(RING):
                load_tile(t, t, None)
            with sp.Fori(1, TILES // RING) as i:
                for s in range(RING):
                    load_tile(i * RING + s, s, i)
            for t in range(TILES, TABLE):
                load_tile(t, t - TILES, TILES // RING)
            for s in range(RING):
                sp.wait_ge(out_tile[s], TILES // RING * 16)


        @block.gpsimd
        def _(pool):
            nc.gpsimd.memset(padding[:, :], 0.0).then_inc(zeros, 1)
            nc.gpsimd.memset(ones16[:, :], 1.0).then_inc(zeros, 1)
            nc.gpsimd.memset(ident[:, :], 0.0).then_inc(zeros, 1)
            nc.gpsimd.memset(below[:, :], 0.0).then_inc(zeros, 1)
            nc.gpsimd.memset(tri[:, :], 1.0).then_inc(zeros, 1)
            for g in range(4):
                nc.gpsimd.memset(mask[g][:, :], 1.0).then_inc(zeros, 1)
            nc.gpsimd.memset(epsc[:, :], EPS).then_inc(zeros, 1)
            nc.gpsimd.memset(ones64[:, :], S64).then_inc(zeros, 1)
            nc.gpsimd.memset(b2s[:, :], 0.0).then_inc(zeros, 1)
            nc.gpsimd.memset(one[:, :], 1.0).then_inc(zeros, 1)
            nc.gpsimd.memset(seen[:, 0, :], 0.0).then_inc(zeros, 1)
            nc.gpsimd.memset(restart[:, :, :], 1.0).then_inc(zeros, 1)
            pool.wait_ge(zeros, 15)
            nc.gpsimd.memset(restart[:, :, 0:1], 0.0)
            nc.gpsimd.iota(padding[:, TOKEN:TOKEN + 1].bitcast(I32), pattern=[[0, 1]], base=NOWHERE, channel_multiplier=0)
            nc.gpsimd.affine_select(out=ident[:, :], in_=ident[:, :], compare_op=ALU.not_equal, fill=1.0, base=0,
                                    pattern=[[-1, 128]], channel_multiplier=1)
            nc.gpsimd.affine_select(out=below[:, :], in_=below[:, :], compare_op=ALU.is_gt, fill=-1.0, base=0,
                                    pattern=[[1, 128]], channel_multiplier=-1)
            nc.gpsimd.affine_select(out=tri[:, :], in_=tri[:, :], compare_op=ALU.is_ge, fill=0.0, base=0,
                                    pattern=[[1, PAIRS]], channel_multiplier=-1)
            for g in range(4):
                nc.gpsimd.affine_select(out=mask[g][:, :], in_=mask[g][:, :], compare_op=ALU.is_ge, fill=0.0,
                                        base=0, pattern=[[-SIZE[g], BATCHES[g]]], channel_multiplier=1).then_inc(zeros, 1)
            pool.wait_ge(zeros, 19)
            for g in range(4):
                nc.gpsimd.affine_select(out=mask[g][:, :], in_=mask[g][:, :], compare_op=ALU.is_ge, fill=0.0,
                                        base=SIZE[g] - 1, pattern=[[SIZE[g], BATCHES[g]]], channel_multiplier=-1)
            nc.gpsimd.iota(pay[:, :, TOKEN:TOKEN + 1].bitcast(I32), pattern=[[1, N], [0, 1]], base=0, channel_multiplier=N)
            for dst, pattern, base, mult in (
                (rev[:, :], [[-1, E]], E, 0), (pairs[:, :], [[1, PAIRS]], 0, 0),
                (tline[:, :], [[1, TABLE]], 0, 0), (vrow[:, 2, :], [[REGION, PAIRS]], -2 * DUMMY, 0),
                (tadd[:, 2, :], [[1, TABLE]], 2 * DUMMY, 0), (padrow[:, 0, :], [[REGION * 128, PAIRS]], 0, 0),
            ):
                nc.gpsimd.iota(dst, pattern=pattern, base=base, channel_multiplier=mult,
                               allow_small_or_imprecise_dtypes=True)
            first = 0
            for a in range(E - 1):
                k = E - 1 - a
                nc.gpsimd.memset(vrow[:, 0, first:first + k], float(a))
                nc.gpsimd.iota(vrow[:, 1, first:first + k], pattern=[[1, k]], base=a + 1, channel_multiplier=0,
                               allow_small_or_imprecise_dtypes=True)
                first += k
            nc.gpsimd.memset(tadd[:, 0:2, :], 0.0).then_inc(consts, 1)
            for c in range(4):
                pool.wait_ge(slots_ready, c + 1)
                for n in range(CHUNKS[c], CHUNKS[c] + CH):
                    nc.gpsimd.indirect_dma_start(
                        out=pay_dram, out_offset=bass.IndirectOffsetOnAxis(ap=slot[:, n:n + 1], axis=0),
                        in_=pay[:, n, :], in_offset=None).then_inc(rows_out, 16)

            last_token = pool.to_reg(B * N - 1)

            def scatter(t, s):
                pool.wait_ge(row_ready, t + 1)
                pool.sem_inc(row_seen, 1)
                nc.gpsimd.indirect_dma_start(
                    out=out_rows, out_offset=bass.IndirectOffsetOnAxis(ap=prow[s][:, TOKEN:TOKEN + 1].bitcast(I32), axis=0),
                    in_=orow[s], in_offset=None, bounds_check=last_token, oob_is_err=False).then_inc(out_tile[s], 16)

            for t in range(RING):
                scatter(t, t)
            with pool.Fori(1, TILES // RING) as i:
                for s in range(RING):
                    scatter(i * RING + s, s)

        def expert_high(act):
            act.wait_ge(in_experts, 16 * (1 + HC + 3))
            nc.scalar.activation(g64[:, :], lng[:, :], ACT.Copy, scale=S64).then_inc(w_high, 1)
            act.wait_ge(w_high, 1)
            for e in range(E):
                nc.scalar.activation(w1s[:, e, 0, :], w1f[:, e, :], ACT.Copy, scale=g64[:, e:e + 1])
                nc.scalar.activation(w2s[:, e, 0, :], w2f[:, e, :, :].rearrange("p c d -> p (c d)"), ACT.Copy,
                                     scale=S64).then_inc(w_high, 1)

        @block.scalar
        def _(act):
            own = [0]

            def link(ins):
                own[0] += 1
                ins.then_inc(act_own, 1)
                act.wait_ge(act_own, own[0])

            act.wait_ge(consts, 1)
            act.wait_ge(var_ready, 1)
            nc.scalar.activation(ln[:, 1, 0:NG], ln[:, 0, 0:NG], ACT.Sqrt, bias=epsc[:, :]).then_inc(root_ready, 1)
            act.wait_ge(deg_ready, 1)
            nc.scalar.activation(deg[:, 3, :], deg[:, 2, :], ACT.Sqrt).then_inc(root_ready, 1)

            def root1(c):
                act.wait_ge(var_ready, 2 + 2 * c)
                nc.scalar.activation(ln[:, 1, :], ln[:, 0, :], ACT.Sqrt, bias=epsc[:, :]).then_inc(root_ready, 1)

            def root2(c):
                act.wait_ge(var_ready, 3 + 2 * c)
                nc.scalar.activation(ln[:, 4, :], ln[:, 3, :], ACT.Sqrt, bias=epsc[:, :]).then_inc(root_ready, 1)

            def normalise(c):
                act.wait_ge(ln_ready, c + 1)
                for j in range(GRP):
                    k = GRP * c + j
                    if k >= 2:
                        act.wait_ge(yt_ready, k - 1)
                    for n in range(4):
                        m = 4 * j + n
                        last = nc.scalar.activation(y[:, k % 2, n, :], pay[:, CHUNKS[c] + m, 0:D], ACT.Identity,
                                                    bias=ln[:, 5, m:m + 1], scale=ln[:, 2, m:m + 1])
                    last.then_inc(y_ready, 1)
                    if j >= 1:
                        take_yT(k - 1)
                take_yT(GRP * c + GRP - 1)

            def take_yT(k):
                act.wait_ge(yt_ready, k + 1)
                if k >= 2:
                    act.wait_ge(logits_ready, k - 1)
                nc.scalar.activation(yT[:, k % 2, :], bank[5 + k % 2][:, :], ACT.Copy).then_inc(yT_ready, 1)

            def gap_exp(c):
                act.wait_ge(gap_ready, c + 1)
                nc.scalar.activation(small[:, 6, :], small[:, 5, :], ACT.Exp).then_inc(exp_ready, 1)

            root1(0)
            root2(0)
            normalise(0)
            gap_exp(0)
            act.wait_ge(fmax_ready, 1)
            nc.scalar.activation(fus[:, :], fus[:, :], ACT.Exp, bias=fstat[:, 0:1], accum_out=fstat[:, 1:2])\
                .then_inc(fexp_ready, 1)

            def quad(i):
                g, q = QUADS[i]
                p4 = 4 * ROWS[g]
                act.wait_ge(h_ready, i + 1)
                if i >= 2:
                    act.wait_ge(s_ready, i - 1)
                for c in range(2):
                    last = nc.scalar.activation(hs[:, i % 2, c, 0:p4], bank[1 + c][:, 0:p4], ACT.Relu,
                                                bias=gb1s[:, g, c:c + 1])
                last.then_inc(hs_ready, 1)
                if i >= 1:
                    post(i - 1)

            def post(i):
                g, q = QUADS[i]
                p = ROWS[g]
                act.wait_ge(gpre_ready, i + 1)
                if i >= 2:
                    act.wait_ge(go_out[i % 2], 16 * (i // 2))
                nc.scalar.activation(gpost[0:p, i % 2, :, :], gpre[0:p, :, :], ACT.Relu).then_inc(gpost_ready, 1)

            act.wait_ge(in_gw, 16 * 5)
            for i in range(NQ):
                quad(i)
                for c, first in ((1, 0), (2, 8)):
                    if i == first + 1:
                        root1(c)
                    if i == first + 2:
                        root2(c)
                    if i == first + 3:
                        normalise(c)
                    if i == first + 5:
                        gap_exp(c)
                if i == 15:
                    expert_high(act)
            post(NQ - 1)
            root1(3)
            root2(3)
            normalise(3)
            gap_exp(3)

            def high_x(t, s):
                act.wait_ge(xt_ready, t + 1)
                nc.scalar.activation(xh[s % 2], bank[s % 2][:, 0:128], ACT.Copy).then_inc(xh_ready, 1)

            def gelu(t, s, k):
                u = 2 * t + k
                v = (2 * s + k) % 4
                e = act.value_load(table[0:1, k, bass.ds(t, 1)], min_val=0, max_val=E - 1)
                act.wait_ge(hid_ready, u + 1)
                for c in range(HC):
                    last = nc.scalar.activation(hid[v][:, c * 128:(c + 1) * 128], bank[2 + v][:, c * 128:(c + 1) * 128],
                                                ACT.Gelu, bias=b1s[:, bass.ds(e * HC + c, 1)], scale=1.0 / S4096)
                last.then_inc(gelu_ready, 1)

            act.wait_ge(table_ready, 1)
            act.wait_ge(rows_out, 16 * N)
            high_x(0, 0)
            for t in range(RING):
                high_x(t + 1, t + 1)
                for k in range(2):
                    if 2 * t + k >= 4:
                        act.wait_ge(split_ready, 2 * t + k - 3)
                    gelu(t, t, k)
            with act.Fori(1, TILES // RING) as i:
                for s in range(RING):
                    t = i * RING + s
                    high_x(t + 1, s + 1)
                    for k in range(2):
                        act.wait_ge(split_ready, 2 * t + k - 3)
                        gelu(t, s, k)

        @block.tensor
        def _(pe):
            pe.wait_ge(consts, 1)
            pe.wait_ge(in_router, 32)

            def transposes(k):
                pe.wait_ge(y_ready, k + 1)
                if k >= 2:
                    pe.wait_ge(yT_ready, k - 1)
                if k % GRP < 2 and k >= GRP:
                    pe.wait_ge(rank_taken, k // GRP)
                for n in range(4):
                    last = nc.tensor.transpose(bank[5 + k % 2][:, n * 128:(n + 1) * 128], y[:, k % 2, n, :], ident[:, :])
                last.then_inc(yt_ready, 1)

            def logits(k):
                pe.wait_ge(yT_ready, k + 1)
                if k % GRP == 0 and k >= GRP:
                    pe.wait_ge(logits_taken, k // GRP)
                for n in range(4):
                    col = (4 * (k % GRP) + n) * E
                    last = nc.tensor.matmul(bank[7][:, col:col + E], yT[:, k % 2, n * 128:(n + 1) * 128], wr[:, :],
                                            start=True, stop=True)
                last.then_inc(logits_ready, 1)

            def route(c):
                for j in range(GRP):
                    transposes(GRP * c + j)
                    if j >= 1:
                        logits(GRP * c + j - 1)
                logits(GRP * c + GRP - 1)

            def ranks(c):
                pe.wait_ge(hot_ready, c + 1)
                half = PAIRS // 2
                for b in range(2):
                    s = slice(b * half, (b + 1) * half)
                    o = bank[5 + b][:, 0:half * CH].rearrange("p (a n) -> p a n", n=CH)
                    nc.tensor.matmul(o, below[:, :], onehot[:, s, :], start=True, stop=False)
                    nc.tensor.matmul(o, ones16[:, :], running[:, s, :], start=False, stop=False)
                    last = nc.tensor.matmul(o, ones16[:, :],
                                            seen[:, c, s].rearrange("p (a o) -> p a o", o=1).to_broadcast([128, half, CH]),
                                            start=False, stop=True)
                last.then_inc(rank_ready, 1)

            def z(i):
                g, q = QUADS[i]
                p = ROWS[g]
                pe.wait_ge(bd_ready, i + 1)
                if i >= 1:
                    pe.wait_ge(zs_ready, i)
                for k in range(4):
                    last = nc.tensor.matmul(bank[0][:, k * p:(k + 1) * p], xpack[0:p, i % 2, k, :], bd[0:p, i % 2, k, 0:p],
                                            start=True, stop=True)
                last.then_inc(z_ready, 1)

            def h(i):
                g, q = QUADS[i]
                p4 = 4 * ROWS[g]
                pe.wait_ge(zs_ready, i + 1)
                if i >= 1:
                    pe.wait_ge(hs_ready, i)
                for c in range(2):
                    last = nc.tensor.matmul(bank[1 + c][:, 0:p4], gw1[:, g, c * 128:(c + 1) * 128], zs[:, i % 2, 0:p4],
                                            start=True, stop=True)
                last.then_inc(h_ready, 1)

            def s_(i):
                g, q = QUADS[i]
                p = ROWS[g]
                pe.wait_ge(hs_ready, i + 1)
                if i >= 1:
                    pe.wait_ge(ss_ready, i)
                for k in range(4):
                    for c in range(2):
                        last = nc.tensor.matmul(bank[3][0:p, k * D:(k + 1) * D], hs[:, i % 2, c, k * p:(k + 1) * p],
                                                gw2[:, g, c, :], start=(c == 0), stop=(c == 1))
                last.then_inc(s_ready, 1)

            def o(i):
                g, q = QUADS[i]
                p = ROWS[g]
                pe.wait_ge(ss_ready, i + 1)
                if i >= 1:
                    pe.wait_ge(gpre_ready, i)
                for k in range(4):
                    last = nc.tensor.matmul(bank[4][0:p, k * D:(k + 1) * D], bd[0:p, i % 2, k, 0:p], ss[0:p, i % 2, k, :],
                                            start=True, stop=True)
                last.then_inc(o_ready, 1)

            route(0)
            ranks(0)
            pe.wait_ge(in_gw, 16 * 5)
            z(0)
            for i in range(NQ):
                h(i)
                if i >= 1:
                    o(i - 1)
                if i + 1 < NQ:
                    z(i + 1)
                s_(i)
                for c, first in ((1, 0), (2, 8)):
                    if i == first + 3:
                        route(c)
                    if i == first + 6:
                        ranks(c)
            o(NQ - 1)
            pe.wait_ge(in_experts, 16 * (1 + HC + 3))
            for e in range(E):
                for c in range(HC):
                    last = nc.tensor.matmul(bank[0][:, e * HC + c:e * HC + c + 1], w1f[:, e, c * 128:(c + 1) * 128],
                                            lnb[:, e:e + 1], start=True, stop=True)
            last.then_inc(b1_ready, 1)
            route(3)
            ranks(3)
            pe.wait_ge(seen_ready, 4)
            nc.tensor.matmul(bank[1][0:PAIRS, 0:1], seen[:, 4, :], ones16[:, 0:1], start=True, stop=True)
            nc.tensor.matmul(bank[2][0:1, 0:PAIRS], ones16[:, 0:1], seen[:, 4, :], start=True, stop=True).then_inc(cnt_ready, 1)
            pe.wait_ge(ntile_ready, 1)
            nc.tensor.matmul(bank[3][0:PAIRS, 0:1], tri[:, :], tcnt[:, 1:2], start=True, stop=True)
            for k in range(3):
                last = nc.tensor.matmul(bank[3][0:PAIRS, 1 + k:2 + k], vrow[:, k, :], one[:, :], start=True, stop=True)
            last.then_inc(tincl_ready, 1)
            pe.wait_ge(member_ready, 1)
            for k in range(3):
                last = nc.tensor.matmul(bank[4][0:1, k * TABLE:(k + 1) * TABLE], tcnt[:, 4 + k:5 + k], inpair[:, :],
                                        start=True, stop=True)
            last.then_inc(trow_ready, 1)

            def turn(t, s):
                pe.wait_ge(xn_ready, t + 1)
                nc.tensor.transpose(bank[s % 2][:, 0:128], xnt[s % 2], ident[:, :]).then_inc(xt_ready, 1)

            def first_layer(t, s, k, e):
                v = (2 * s + k) % 4
                for c in range(HC):
                    o = bank[2 + v][:, c * 128:(c + 1) * 128]
                    w = [w1s[:, bass.ds(e, 1), part, c * 128:(c + 1) * 128].rearrange("p o h -> p (o h)") for part in range(2)]
                    nc.tensor.matmul(o, w[0], xh[s % 2], start=True, stop=False)
                    nc.tensor.matmul(o, w[0], xl[s % 2], start=False, stop=False)
                    last = nc.tensor.matmul(o, w[1], xh[s % 2], start=False, stop=True)
                last.then_inc(hid_ready, 1)

            def second_layer(s, k, e):
                v = (2 * s + k) % 4
                o = bank[6 + s % 2][:, k * 128:(k + 1) * 128]
                nc.tensor.matmul(o, ones64[:, :], b2s[:, bass.ds(e * D, D)], start=True, stop=False)
                for c in range(HC):
                    w = [w2s[:, bass.ds(e, 1), part, c * D:(c + 1) * D].rearrange("p o d -> p (o d)") for part in range(2)]
                    a, b = hh[v][:, c * 128:(c + 1) * 128], hl[v][:, c * 128:(c + 1) * 128]
                    nc.tensor.matmul(o, a, w[0], start=False, stop=False)
                    nc.tensor.matmul(o, a, w[1], start=False, stop=False)
                    last = nc.tensor.matmul(o, b, w[0], start=False, stop=(c == HC - 1))
                last.then_inc(e_ready, 1)

            def expert(t, k):
                return pe.value_load(table[0:1, k, bass.ds(t, 1)], min_val=0, max_val=E - 1)

            pe.wait_ge(table_ready, 1)
            pe.wait_ge(b2_done, 1)
            turn(0, 0)
            for t in range(RING):
                turn(t + 1, t + 1)
                for k in range(2):
                    u = 2 * t + k
                    pe.wait_ge(xl_ready, t + 1)
                    if u >= 4:
                        pe.wait_ge(gelu_ready, u - 3)
                    first_layer(t, t, k, expert(t, k))
                    if t >= 1:
                        pe.wait_ge(split_ready, u - 1)
                        if t >= 3:
                            pe.wait_ge(row_ready, t - 2)
                        second_layer(t - 1, k, expert(t - 1, k))
            with pe.Fori(1, TILES // RING) as i:
                for s in range(RING):
                    t = i * RING + s
                    turn(t + 1, s + 1)
                    for k in range(2):
                        e = expert(t, k)
                        pe.wait_ge(xl_ready, t + 1)
                        pe.wait_ge(gelu_ready, 2 * t + k - 3)
                        first_layer(t, s, k, e)
                        e = expert(t - 1, k)
                        pe.wait_ge(split_ready, 2 * t + k - 1)
                        pe.wait_ge(row_ready, t - 2)
                        second_layer(s - 1, k, e)
            for k in range(2):
                pe.wait_ge(split_ready, 2 * TILES - 1 + k)
                pe.wait_ge(row_ready, TILES - 2)
                second_layer(TILES - 1, k, expert(TILES - 1, k))

        @block.vector
        def _(dve):
            own = [0]
            V = nc.vector

            def link(ins):
                own[0] += 1
                ins.then_inc(vec, 1)
                dve.wait_ge(vec, own[0])

            dve.wait_ge(consts, 1)

            def moments(first, count):
                for j in range(count):
                    last = V.bn_stats(stat[:, j, :], pay[:, first + j, 0:D])
                link(last)
                me, mo, qe, qo = (stat[:, 0:count, k] for k in (1, 4, 2, 5))
                V.tensor_tensor(small[:, 0, 0:count], me, mo, ALU.subtract)
                V.tensor_tensor(small[:, 1, 0:count], me, mo, ALU.add)
                link(V.tensor_tensor(small[:, 2, 0:count], qe, qo, ALU.add))
                link(V.scalar_tensor_tensor(out=small[:, 3, 0:count], in0=small[:, 0, 0:count], scalar=D / 4.0,
                                            in1=small[:, 0, 0:count], op0=ALU.mult, op1=ALU.mult))
                link(V.tensor_tensor(small[:, 4, 0:count], small[:, 2, 0:count], small[:, 3, 0:count], ALU.add))
                V.tensor_scalar(ln[:, 0, 0:count], small[:, 4, 0:count], 1.0 / D, None, ALU.mult).then_inc(var_ready, 1)

            dve.wait_ge(in_graph, 32)
            moments(0, NG)
            dve.wait_ge(root_ready, 1)
            link(V.reciprocal(ln[:, 2, 0:NG], ln[:, 1, 0:NG]))
            link(V.scalar_tensor_tensor(out=ln[:, 5, 0:NG], in0=small[:, 1, 0:NG], scalar=-0.5, in1=ln[:, 2, 0:NG],
                                        op0=ALU.mult, op1=ALU.mult))
            for j in range(NG):
                last = V.tensor_scalar(xn[:, j, :], pay[:, j, 0:D], ln[:, 2, j:j + 1], ln[:, 5, j:j + 1],
                                       ALU.mult, ALU.add)
            last.then_inc(xn_done, 1)
            dve.wait_ge(in_adj, 16)
            link(V.tensor_scalar(adjs[:, 0:NG * NG:NG + 1], adjs[:, 0:NG * NG:NG + 1], 1.0, None, ALU.add))
            whole = adjs[:, :].rearrange("p (i j) -> p i j", j=NG)

            def square(g, t=acomp):
                return t[:, OFF2[g]:OFF2[g + 1]].rearrange("p (i j) -> p i j", j=SIZE[g])

            for g in range(5):
                row = 0
                for i0, ni in GROUPS[g]:
                    col = 0
                    for j0, nj in GROUPS[g]:
                        last = V.tensor_copy(square(g)[:, row:row + ni, col:col + nj], whole[:, i0:i0 + ni, j0:j0 + nj])
                        col += nj
                    row += ni
            link(last)
            for g in range(5):
                last = V.tensor_reduce(deg[:, 0, OFF[g]:OFF[g + 1]], square(g), AX_X, ALU.add)
            link(last)
            link(V.tensor_scalar(deg[:, 1, :], deg[:, 0, :], 0.0, None, ALU.is_equal))
            V.tensor_tensor(deg[:, 2, :], deg[:, 0, :], deg[:, 1, :], ALU.add).then_inc(deg_ready, 1)
            link(V.tensor_scalar(deg[:, 4, :], deg[:, 1, :], -1.0, 1.0, ALU.mult, ALU.add))
            dve.wait_ge(root_ready, 2)
            link(V.reciprocal(deg[:, 5, :], deg[:, 3, :]))
            link(V.tensor_tensor(deg[:, 3, :], deg[:, 5, :], deg[:, 4, :], ALU.mult))
            for g in range(5):
                s = SIZE[g]
                inv = deg[:, 3, OFF[g]:OFF[g + 1]].rearrange("p (o n) -> p o n", o=1).to_broadcast([128, s, s])
                last = V.tensor_tensor(square(g, nt_sb), square(g).rearrange("p n m -> p m n"), inv, ALU.mult)
            link(last)
            for g in range(5):
                s = SIZE[g]
                inv = deg[:, 3, OFF[g]:OFF[g + 1]].rearrange("p (m o) -> p m o", o=1).to_broadcast([128, s, s])
                last = V.tensor_tensor(square(g, nt_sb), square(g, nt_sb), inv, ALU.mult)
            last.then_inc(nt_done, 1)

            def norms(c):
                dve.wait_ge(in_chunk[c], 16)
                if c == 3:
                    dve.wait_ge(gl_added, 1)
                if c >= 1:
                    dve.wait_ge(y_ready, GRP * c)
                moments(CHUNKS[c], CH)

            def norms2(c):
                dve.wait_ge(root_ready, 3 + 2 * c)
                link(V.reciprocal(ln[:, 2, :], ln[:, 1, :]))
                link(V.tensor_tensor(small[:, 2, :], ln[:, 0, :], ln[:, 2, :], ALU.mult))
                link(V.tensor_tensor(ln[:, 3, :], small[:, 2, :], ln[:, 2, :], ALU.mult))
                V.tensor_scalar(small[:, 3, :], small[:, 1, :], -0.5, None, ALU.mult).then_inc(var_ready, 1)
                link(V.scalar_tensor_tensor(out=ln[:, 5, :], in0=small[:, 1, :], scalar=-0.5, in1=ln[:, 2, :],
                                            op0=ALU.mult, op1=ALU.mult))

            def norms3(c):
                row = pay[:, CHUNKS[c]:CHUNKS[c] + CH, :]
                dve.wait_ge(root_ready, 4 + 2 * c)
                link(V.reciprocal(small[:, 4, :], ln[:, 4, :]))
                link(V.scalar_tensor_tensor(out=row[:, :, RSTD], in0=small[:, 4, :], scalar=S64, in1=ln[:, 2, :],
                                            op0=ALU.mult, op1=ALU.mult))
                V.tensor_tensor(row[:, :, NBIAS], small[:, 3, :], row[:, :, RSTD], ALU.mult).then_inc(ln_ready, 1)

            def over(v):
                return v.rearrange("p (n o) -> p n o", o=1).to_broadcast([128, CH, E])

            def route(c):
                dve.wait_ge(logits_ready, GRP * (c + 1))
                revb = rev[:, :].rearrange("p (o e) -> p o e", o=1).to_broadcast([128, CH, E])
                brbb = brb[:, :].rearrange("p (o e) -> p o e", o=1).to_broadcast([128, CH, E])
                V.tensor_tensor(logit[:, :, :], bank[7][:, 0:CH * E].rearrange("p (n e) -> p n e", e=E), brbb, ALU.add)\
                    .then_inc(logits_taken, 1)
                dve.wait_ge(logits_taken, c + 1)
                for k in range(2):
                    link(V.tensor_reduce(small[:, k, :], logit[:, :, :], AX_X, ALU.max))
                    link(V.tensor_tensor(pick[:, :, :], logit[:, :, :], over(small[:, k, :]), ALU.is_ge))
                    link(V.tensor_tensor(score[:, :, :], pick[:, :, :], revb, ALU.mult))
                    link(V.tensor_reduce(small[:, 2 + k, :], score[:, :, :], AX_X, ALU.max))
                    if k == 0:
                        link(V.tensor_tensor(pick[:, :, :], revb, over(small[:, 2, :]), ALU.is_equal))
                        link(V.scalar_tensor_tensor(out=logit[:, :, :], in0=pick[:, :, :], scalar=NEG,
                                                    in1=logit[:, :, :], op0=ALU.mult, op1=ALU.add))
                V.tensor_tensor(small[:, 5, :], small[:, 1, :], small[:, 0, :], ALU.subtract).then_inc(gap_ready, 1)
                V.tensor_tensor(small[:, 7, :], small[:, 2, :], small[:, 3, :], ALU.max)
                V.tensor_tensor(small[:, 8, :], small[:, 2, :], small[:, 3, :], ALU.min)
                link(V.tensor_tensor(small[:, 9, :], small[:, 2, :], small[:, 3, :], ALU.is_gt))
                V.tensor_scalar(small[:, 10, :], small[:, 7, :], -0.5, E / 2.0, ALU.mult, ALU.add)
                link(V.tensor_tensor(small[:, 11, :], small[:, 7, :], small[:, 8, :], ALU.subtract))
                link(V.scalar_tensor_tensor(out=small[:, 12, :], in0=small[:, 7, :], scalar=E - 1.0,
                                            in1=small[:, 10, :], op0=ALU.add, op1=ALU.mult))
                link(V.scalar_tensor_tensor(out=small[:, 13, :], in0=small[:, 12, :], scalar=-1.0,
                                            in1=small[:, 11, :], op0=ALU.add, op1=ALU.add))
                link(V.tensor_tensor(
                    onehot[:, :, :], small[:, 13, :].rearrange("p (o n) -> p o n", o=1).to_broadcast([128, PAIRS, CH]),
                    pairs[:, :].rearrange("p (a o) -> p a o", o=1).to_broadcast([128, PAIRS, CH]), ALU.is_equal))
                link(V.tensor_tensor_scan(running[:, :, :].rearrange("p a n -> p (a n)"),
                                          restart[:, :, :].rearrange("p a n -> p (a n)"),
                                          onehot[:, :, :].rearrange("p a n -> p (a n)"), 0.0, ALU.mult, ALU.add))
                V.tensor_tensor(seen[:, c + 1, :], seen[:, c, :], running[:, :, CH - 1], ALU.add).then_inc(seen_ready, 1)
                V.tensor_scalar(small[:, 14, :], small[:, 13, :], float(REGION * 128), None, ALU.mult).then_inc(hot_ready, 1)
                dve.wait_ge(exp_ready, c + 1)
                link(V.tensor_scalar(small[:, 10, :], small[:, 6, :], 1.0, S4096, ALU.add, ALU.mult))
                link(V.reciprocal(small[:, 11, :], small[:, 10, :]))
                link(V.tensor_tensor(small[:, 12, :], small[:, 6, :], small[:, 11, :], ALU.mult))
                link(V.tensor_tensor(small[:, 10, :], small[:, 11, :], small[:, 12, :], ALU.subtract))
                link(V.tensor_tensor(small[:, 15, :], small[:, 10, :], small[:, 9, :], ALU.mult))
                row = pay[:, CHUNKS[c]:CHUNKS[c] + CH, :]
                V.tensor_tensor(row[:, :, WA], small[:, 12, :], small[:, 15, :], ALU.add)
                V.tensor_tensor(row[:, :, WB], small[:, 11, :], small[:, 15, :], ALU.subtract)

            def place(c):
                dve.wait_ge(rank_ready, c + 1)
                half = PAIRS // 2
                for b in range(2):
                    s = slice(b * half, (b + 1) * half)
                    last = V.tensor_tensor(rank[:, s, :], bank[5 + b][:, 0:half * CH].rearrange("p (a n) -> p a n", n=CH),
                                           onehot[:, s, :], ALU.mult)
                last.then_inc(rank_taken, 1)
                dve.wait_ge(rank_taken, c + 1)
                link(V.tensor_reduce(small[:, 12, :], rank[:, :, :].rearrange("p a n -> p n a"), AX_X, ALU.add))
                V.tensor_tensor(slot[:, CHUNKS[c]:CHUNKS[c] + CH], small[:, 12, :], small[:, 14, :], ALU.add)\
                    .then_inc(slots_ready, 1)

            norms(0)
            norms2(0)
            norms3(0)
            route(0)
            place(0)
            dve.wait_ge(in_gw, 16 * 5)
            V.tensor_reduce(fstat[:, 0:1], fus[:, :], AX_X, ALU.max, negate=True).then_inc(fmax_ready, 1)
            dve.wait_ge(fexp_ready, 1)
            link(V.reciprocal(fstat[:, 2:3], fstat[:, 1:2]))
            link(V.tensor_scalar(fus[:, :], fus[:, :], fstat[:, 2:3], None, ALU.mult))
            link(V.tensor_tensor(wb2[:, :, :], wb2[:, :, :],
                                 fus[:, :].rearrange("p (g o) -> p g o", o=1).to_broadcast([128, 5, D]), ALU.mult))

            def blocks(i):
                g, q = QUADS[i]
                p, s, n = ROWS[g], SIZE[g], BATCHES[g]
                dve.wait_ge(in_pack[i % 2], 32 * (i // 2 + 1))
                if i >= 2:
                    dve.wait_ge(o_ready, i - 1)
                for k in range(4):
                    last = V.tensor_tensor(
                        bd[0:p, i % 2, k, 0:p].rearrange("p (b n) -> p b n", n=s),
                        npack[0:p, i % 2, k, 0:s].rearrange("p (o n) -> p o n", o=1).to_broadcast([p, n, s]),
                        mask[min(g, 3)][0:p, :].rearrange("p (b o) -> p b o", o=1).to_broadcast([p, n, s]), ALU.mult)
                last.then_inc(bd_ready, 1)

            def take_z(i):
                p4 = 4 * ROWS[QUADS[i][0]]
                dve.wait_ge(z_ready, i + 1)
                if i >= 2:
                    dve.wait_ge(h_ready, i - 1)
                V.tensor_copy(zs[:, i % 2, 0:p4], bank[0][:, 0:p4]).then_inc(zs_ready, 1)

            def take_s(i):
                p = ROWS[QUADS[i][0]]
                dve.wait_ge(s_ready, i + 1)
                if i >= 2:
                    dve.wait_ge(o_ready, i - 1)
                V.tensor_copy(ss[0:p, i % 2, :, :], bank[3][0:p, :].rearrange("p (k d) -> p k d", d=D)).then_inc(ss_ready, 1)

            def take_o(i):
                g = QUADS[i][0]
                p = ROWS[g]
                dve.wait_ge(o_ready, i + 1)
                if i >= 1:
                    dve.wait_ge(gpost_ready, i)
                V.scalar_tensor_tensor(
                    out=gpre[0:p, :, :], in0=bank[4][0:p, :].rearrange("p (k d) -> p k d", d=D),
                    scalar=fus[0:p, g:g + 1],
                    in1=wb2[0:p, g, :].rearrange("p (o d) -> p o d", o=1).to_broadcast([p, 4, D]),
                    op0=ALU.mult, op1=ALU.add).then_inc(gpre_ready, 1)

            def expert_low():
                for e in range(E):
                    dve.wait_ge(w_high, e + 2)
                    V.scalar_tensor_tensor(out=w1s[:, e, 1, :], in0=w1f[:, e, :], scalar=g64[:, e:e + 1],
                                           in1=w1s[:, e, 0, :], op0=ALU.mult, op1=ALU.subtract)
                    last = V.scalar_tensor_tensor(out=w2s[:, e, 1, :], in0=w2f[:, e, :, :].rearrange("p c d -> p (c d)"),
                                                  scalar=S64, in1=w2s[:, e, 0, :], op0=ALU.mult, op1=ALU.subtract)
                last.then_inc(w_done, 1)

            blocks(0)
            blocks(1)
            take_z(0)
            for i in range(NQ):
                if i >= 1:
                    take_o(i - 1)
                    if i + 1 < NQ:
                        blocks(i + 1)
                if i + 1 < NQ:
                    take_z(i + 1)
                take_s(i)
                for c, first in ((1, 0), (2, 8)):
                    if i == first:
                        norms(c)
                    if i == first + 2:
                        norms2(c)
                    if i == first + 3:
                        norms3(c)
                    if i == first + 5:
                        route(c)
                    if i == first + 7:
                        place(c)
                if i == 16:
                    expert_low()
            take_o(NQ - 1)
            dve.wait_ge(b1_ready, 1)
            V.tensor_tensor(b1s[:, :], bank[0][:, 0:E * HC], b1t[:, :], ALU.add)
            dve.wait_ge(in_b2, 32)
            V.tensor_scalar(b2s[0:1, :], b2f[0:1, :], S64, None, ALU.mult)
            link(V.tensor_scalar(b2hi[32:33, :], b2f[32:33, :], S64, None, ALU.mult))
            V.scalar_tensor_tensor(out=b2s[32:33, :], in0=b2f[32:33, :], scalar=S64, in1=b2hi[32:33, :],
                                   op0=ALU.mult, op1=ALU.subtract).then_inc(b2_done, 1)
            dve.wait_ge(in_gl, 16 * 5)
            for g in range(5):
                col = OFF[g]
                for first, count in GROUPS[g]:
                    v = pay[:, first:first + count, 0:D]
                    last = V.tensor_tensor(v, v, gl[:, col:col + count, :], ALU.add)
                    col += count
                    if g < 4 or first != GROUPS[4][-1][0]:
                        link(last)
            last.then_inc(gl_added, 1)
            norms(3)
            norms2(3)
            norms3(3)
            route(3)
            place(3)

            dve.wait_ge(cnt_ready, 1)
            V.tensor_tensor(padint[:, :], bank[2][0:1, 0:PAIRS], padrow[:, 0, :], ALU.add)
            link(V.tensor_scalar(tint[:, 0:1], bank[1][0:PAIRS, 0:1], 127.0, None, ALU.add))
            link(V.tensor_scalar(tint[:, 1:2], tint[:, 0:1], 7, None, ALU.arith_shift_right))
            V.tensor_copy(tcnt[:, 1:2], tint[:, 1:2]).then_inc(ntile_ready, 1)
            dve.wait_ge(tincl_ready, 1)
            link(V.tensor_copy(tcnt[:, 2:3], bank[3][0:PAIRS, 0:1]))
            link(V.tensor_tensor(tcnt[:, 3:4], tcnt[:, 2:3], tcnt[:, 1:2], ALU.subtract))
            V.tensor_copy(tcnt[:, 4:6], bank[3][0:PAIRS, 1:3])
            V.tensor_tensor(tcnt[:, 6:7], bank[3][0:PAIRS, 3:4], tcnt[:, 3:4], ALU.subtract)
            V.tensor_scalar(ahead[:, :], tline[:, :], tcnt[:, 3:4], None, ALU.is_ge)
            link(V.tensor_scalar(inpair[:, :], tline[:, :], tcnt[:, 2:3], None, ALU.is_ge))
            V.tensor_tensor(inpair[:, :], ahead[:, :], inpair[:, :], ALU.subtract).then_inc(member_ready, 1)
            dve.wait_ge(trow_ready, 1)
            link(V.tensor_tensor(tadd[:, 0:3, :], bank[4][0:1, 0:3 * TABLE].rearrange("p (k t) -> p k t", k=3),
                                 tadd[:, 0:3, :], ALU.add))
            V.tensor_copy(table[:, 0:2, :], tadd[:, 0:2, :])
            V.tensor_scalar(table[:, 2, :], tadd[:, 2, :], float(DUMMY), None, ALU.min).then_inc(table_ready, 1)

            def norm_tile(s):
                V.tensor_scalar(xnt[s % 2], prow[s % RING][:, 0:D], prow[s % RING][:, RSTD:RSTD + 1],
                                prow[s % RING][:, NBIAS:NBIAS + 1], ALU.mult, ALU.add).then_inc(xn_ready, 1)

            def low_x(t, s):
                dve.wait_ge(xh_ready, t + 1)
                V.tensor_tensor(xl[s % 2], bank[s % 2][:, 0:128], xh[s % 2], ALU.subtract).then_inc(xl_ready, 1)

            def split(u, v):
                dve.wait_ge(gelu_ready, u + 1)
                V.tensor_scalar(hh[v], hid[v], S64, None, ALU.mult).then_inc(hh_ready, 1)
                dve.wait_ge(hh_ready, u + 1)
                V.scalar_tensor_tensor(out=hl[v], in0=hid[v], scalar=S64, in1=hh[v], op0=ALU.mult,
                                       op1=ALU.subtract).then_inc(split_ready, 1)

            def combine(t, s):
                r, b = prow[s % RING], bank[6 + s % 2]
                dve.wait_ge(e_ready, 2 * t + 2)
                V.scalar_tensor_tensor(out=orow[s % RING], in0=b[:, 0:D], scalar=r[:, WA:WA + 1], in1=r[:, 0:D],
                                       op0=ALU.mult, op1=ALU.add).then_inc(half_ready, 1)
                dve.wait_ge(half_ready, t + 1)
                V.scalar_tensor_tensor(out=orow[s % RING], in0=b[:, D:2 * D], scalar=r[:, WB:WB + 1], in1=orow[s % RING],
                                       op0=ALU.mult, op1=ALU.add).then_inc(row_ready, 1)

            def tile_step(t, s, i):
                first = isinstance(t, int)
                if not first or t >= 1:
                    split(2 * t - 1, (2 * s - 1) % 4)
                nxt = (s + 2) % RING
                dve.wait_ge(in_tile[nxt], 16 * (i + 1 + (s + 2) // RING))
                dve.wait_ge(xt_ready, t + 1)
                norm_tile(s + 2)
                low_x(t + 1, s + 1)
                if not first or t >= 2:
                    combine(t - 2, s - 2)
                if not first or t >= 3:
                    dve.wait_ge(e_ready, 2 * t - 3)
                split(2 * t, (2 * s) % 4)

            dve.wait_ge(in_tile[0], 16)
            norm_tile(0)
            dve.wait_ge(in_tile[1], 16)
            norm_tile(1)
            low_x(0, 0)
            for t in range(RING):
                tile_step(t, t, 0)
            with dve.Fori(1, TILES // RING) as i:
                for s in range(RING):
                    tile_step(i * RING + s, s, i)
            combine(TILES - 2, TILES - 2)
            split(2 * TILES - 1, (2 * TILES - 1) % 4)
            combine(TILES - 1, TILES - 1)


_INS = ['x', 'adj', 'L0_gnn_W1', 'L0_gnn_b1', 'L0_gnn_W2', 'L0_gnn_b2', 'L0_gnn_fusion_w', 'L0_ffn_Wr', 'L0_ffn_br',
        'L0_ffn_ln_g', 'L0_ffn_ln_b', 'L0_ffn_W1', 'L0_ffn_b1', 'L0_ffn_W2', 'L0_ffn_b2']


def kernel(**inputs):
    import numpy as _np
    import concourse.bacc as _bacc
    from concourse import mybir as _mybir
    from concourse.bass_utils import run_bass_kernel_spmd as _run

    nc = _bacc.Bacc("TRN2", target_bir_lowering=False, num_devices=1)
    arrays, args = {}, []
    for name in _INS:
        a = _np.ascontiguousarray(inputs[name])
        arrays[f"in_{name}"] = a
        args.append(nc.dram_tensor(f"in_{name}", a.shape, _mybir.dt.from_np(a.dtype), kind="ExternalInput").ap())
    args.append(nc.dram_tensor("out_0", (B, N, D), _mybir.dt.float32, kind="ExternalOutput").ap())
    build(nc, *args)
    r = _run(nc, [arrays], core_ids=[0])
    return r.results[0]["out_0"]
```

```python
from contextlib import ExitStack

import concourse.bass as bass
import numpy as np
from concourse import mybir

ALU = mybir.AluOpType
ACT = mybir.ActivationFunctionType
AX_X = mybir.AxisListType.X
F32 = mybir.dt.float32
F16 = mybir.dt.float16
BF16 = mybir.dt.bfloat16
I32 = mybir.dt.int32

B = N = D = 128
GROUPS = [[(0, 25)], [(0, 9)], [(0, 1), (9, 6)], [(6, 3), (12, 3)], [(3, 3), (9, 3)]]
SIZE = [sum(c for _, c in r) for r in GROUPS]
BATCHES = [4, 8, 16, 16, 16]
OFF = [sum(SIZE[:g]) for g in range(6)]
OFF2 = [sum(s * s for s in SIZE[:g]) for g in range(6)]
NG = SIZE[0]
COLS = OFF[5]
HID = 256
ROWS = [BATCHES[g] * SIZE[g] for g in range(5)]
QUADS = [(g, q) for g in range(5) for q in range(B // BATCHES[g] // 4)]
NQ = len(QUADS)

E, H = 8, 512
HC = H // 128
PAIRS = E * (E - 1) // 2
CH = 32
CHUNKS = [32, 64, 96, 0]
GRP = CH // 4
MEAN, NBIAS, RSTD, WA, WB, TOKEN = 0, 128, 129, 130, 131, 132
ROW = 133
REGION = B * N // 128 + 1
DUMMY = PAIRS * REGION
TILES = B * N // 128 + PAIRS
RING = 12
AHEAD = 2
BACK = 2
UNITS = 2 * RING
WRING = 8
BLOCK = 4 * H + D
TABLE = TILES + AHEAD
EPS = 1e-5
S64 = 64.0
S4096 = S64 * S64
NOWHERE = 1 << 20
NEG = -1e30


def build(nc, x, adj, gW1, gb1, gW2, gb2, fusion, Wr, br, ln_g, ln_b, W1, b1, W2, b2, out):
    with ExitStack() as ctx:
        def sb(name, shape, dt=F32):
            return ctx.enter_context(nc.sbuf_tensor(name, shape, dt))

        def sem(name):
            return ctx.enter_context(nc.semaphore(name))

        xg_dram = [nc.dram_tensor(f"xg{g}", [B, SIZE[g] * D], F32).ap() for g in range(5)]
        nt_dram = [nc.dram_tensor(f"nt{g}", [B, SIZE[g] ** 2], F32).ap() for g in range(5)]
        go_dram = [nc.dram_tensor(f"go{g}", [B, SIZE[g] * D], F32).ap() for g in range(5)]
        pay_dram = nc.dram_tensor("pay_rows", [(DUMMY + 1) * 128, ROW], F32).ap()
        out_rows = out.rearrange("b n d -> (b n) d")

        bank = [ctx.enter_context(nc.psum_tensor(f"bank{i}", [128, 512], F32)) for i in range(8)]

        pay = sb("pay", [128, N, ROW])
        slot = sb("slot", [128, N], I32)
        deg = sb("deg", [128, 6, COLS])
        gw1 = sb("gw1", [128, 5, HID])
        gw2 = sb("gw2", [128, 5, 2, D])
        gb1s = sb("gb1s", [128, 5, 2])
        wb2 = sb("wb2", [128, 5, D])
        fus = sb("fus", [128, 5])
        fstat = sb("fstat", [128, 4])
        mask = [sb(f"mask{g}", [128, BATCHES[g]]) for g in range(4)]
        xpack = sb("xpack", [128, 2, 4, D])
        npack = sb("npack", [128, 2, 4, NG])
        bd = sb("bd", [128, 2, 4, 128])
        zs = sb("zs", [128, 2, 512])
        hs = sb("hs", [128, 2, 2, 4 * max(ROWS)])
        ss = sb("ss", [128, 2, 4, D])
        gpre = sb("gpre", [128, 4, D])
        gpost = sb("gpost", [128, 2, 4, D])
        stat = sb("stat", [128, CH, 6])
        ln = sb("ln", [128, 6, CH])
        y = sb("y", [128, 2, 4, D])
        yT = sb("yT", [128, 2, 512])
        wr = sb("wr", [128, E])
        brb = sb("brb", [128, E])
        rev = sb("rev", [128, E])
        logit = sb("logit", [128, CH, E])
        small = sb("small", [128, 16, CH])
        pairs = sb("pairs", [128, PAIRS])
        onehot = sb("onehot", [128, PAIRS, CH], BF16)
        running = sb("running", [128, PAIRS, CH], BF16)
        restart = sb("restart", [128, PAIRS, CH], BF16)
        rank = sb("rank", [128, PAIRS, CH])
        scratch = rank[:, :, :].rearrange("p a n -> p (a n)")
        pick = scratch[:, 0:CH * E].rearrange("p (n e) -> p n e", e=E)
        score = scratch[:, CH * E:2 * CH * E].rearrange("p (n e) -> p n e", e=E)
        inpair = scratch[0:PAIRS, 0:TABLE]
        ahead = scratch[0:PAIRS, TABLE:2 * TABLE]
        seen = sb("seen", [128, 5, PAIRS], BF16)
        ones16 = sb("ones16", [128, 128], BF16)
        below = sb("below", [128, 128], BF16)
        ident = sb("ident", [128, 128])
        vrow = sb("vrow", [1, 3, PAIRS])
        one = sb("one", [1, 1])
        tri = sb("tri", [PAIRS, PAIRS])
        tline = sb("tline", [PAIRS, TABLE])
        tcnt = sb("tcnt", [PAIRS, 8])
        tint = sb("tint", [PAIRS, 2], I32)
        tadd = sb("tadd", [1, 4, TABLE])
        experts = sb("experts", [1, TABLE, 2], I32)
        place_of = sb("place_of", [1, TABLE], I32)
        padrow = sb("padrow", [1, 2, PAIRS])
        padint = sb("padint", [1, PAIRS], I32)
        padding = sb("padding", [128, ROW])
        stage = sb("stage", [128, E * H * 2])
        w1f = stage[:, 0:E * H].rearrange("p (e h) -> p e h", e=E)
        w2f = stage[:, E * H:2 * E * H].rearrange("p (e c d) -> p e c d", e=E, c=HC)
        gl = stage[:, 0:COLS * D].rearrange("p (i d) -> p i d", d=D)
        split_w = sb("split_w", [128, E * BLOCK // 2])
        blocks_w = split_w[:, :].bitcast(F16).rearrange("p (e w) -> p e w", e=E)
        w1s = blocks_w[:, :, 0:2 * H].rearrange("p e (t h) -> p e t h", t=2)
        w2s = blocks_w[:, :, 2 * H:4 * H].rearrange("p e (c t d) -> p e c t d", c=HC, t=2)
        b2s = blocks_w[:, :, 4 * H:BLOCK]
        last_block = split_w[:, (E - 1) * BLOCK // 2:E * BLOCK // 2]
        b1f = last_block[0:E, 0:H]
        mix = last_block[:, H:H + 2 * D].rearrange("p (a m) -> p a m", a=2)
        pick64 = last_block[0:E, H + 2 * D:H + 4 * D].rearrange("p (a m) -> p a m", a=2)
        xn = split_w[:, 0:NG * D].rearrange("p (i d) -> p i d", d=D)
        at0 = NG * D
        adjs = split_w[:, at0:at0 + NG * NG]
        at0 += NG * NG
        acomp = split_w[:, at0:at0 + OFF2[5]]
        at0 += OFF2[5]
        nt_sb = split_w[:, at0:at0 + OFF2[5]]
        lng = sb("lng", [128, E])
        lnb = sb("lnb", [128, E])
        g64 = sb("g64", [128, E])
        b2f = zs[0:33, :, :].rearrange("p a n -> p (a n)")
        b2hi = bd[0:33, 0, :, :].rearrange("p k n -> p (k n)").bitcast(F16)
        ones64 = sb("ones64", [128, 128], F16)
        ident16 = sb("ident16", [128, 128], F16)
        epsc = sb("epsc", [128, 1])

        flat = pay[:, :, :].rearrange("p n r -> p (n r)")
        at = [0]

        def take(words, dt=F32):
            v = flat[:, at[0]:at[0] + words]
            at[0] += words
            return v if dt == F32 else v.bitcast(dt)

        prow = [take(ROW) for _ in range(RING)]
        orow = [take(D) for _ in range(RING)]
        at[0] += at[0] % 2
        xnt = [take(D) for _ in range(2)]
        xsplit = [take(D, F16) for _ in range(2)]
        xT = [take(D, F16) for _ in range(2)]
        hid = [take(H) for _ in range(4)]
        hh = [take(H // 2, F16) for _ in range(4)]
        hl = [take(H // 2, F16) for _ in range(4)]
        wbuf = [take(BLOCK // 2, F16) for _ in range(WRING)]
        assert at[0] <= N * ROW

        in_graph = sem("in_graph")
        in_adj = sem("in_adj")
        in_gw = sem("in_gw")
        in_chunk = [sem(f"in_chunk{c}") for c in range(4)]
        in_router = sem("in_router")
        in_experts = sem("in_experts")
        in_b2 = sem("in_b2")
        xg_out = sem("xg_out")
        nt_out = sem("nt_out")
        in_pack = [sem(f"in_pack{i}") for i in range(2)]
        go_out = [sem(f"go_out{i}") for i in range(2)]
        in_gl = sem("in_gl")
        pads_out = sem("pads_out")
        consts = sem("consts")
        zeros = sem("zeros")
        vec = sem("vec")
        act_own = sem("act_own")
        xn_done = sem("xn_done")
        var_ready = sem("var_ready")
        root_ready = sem("root_ready")
        deg_ready = sem("deg_ready")
        nt_done = sem("nt_done")
        fmax_ready = sem("fmax_ready")
        fexp_ready = sem("fexp_ready")
        bd_ready = sem("bd_ready")
        z_ready = sem("z_ready")
        zs_ready = sem("zs_ready")
        h_ready = sem("h_ready")
        hs_ready = sem("hs_ready")
        s_ready = sem("s_ready")
        ss_ready = sem("ss_ready")
        o_ready = sem("o_ready")
        gpre_ready = sem("gpre_ready")
        gpost_ready = sem("gpost_ready")
        gl_added = sem("gl_added")
        ln_ready = sem("ln_ready")
        y_ready = sem("y_ready")
        yt_ready = sem("yt_ready")
        yT_ready = sem("yT_ready")
        logits_ready = sem("logits_ready")
        logits_taken = sem("logits_taken")
        gap_ready = sem("gap_ready")
        exp_ready = sem("exp_ready")
        hot_ready = sem("hot_ready")
        rank_ready = sem("rank_ready")
        rank_taken = sem("rank_taken")
        slots_ready = sem("slots_ready")
        rows_out = sem("rows_out")
        seen_ready = sem("seen_ready")
        w_high = sem("w_high")
        b2_done = sem("b2_done")
        mix_ready = sem("mix_ready")
        w1_ready = sem("w1_ready")
        w_low = sem("w_low")
        cnt_ready = sem("cnt_ready")
        ntile_ready = sem("ntile_ready")
        tincl_ready = sem("tincl_ready")
        vcol_ready = sem("vcol_ready")
        member_ready = sem("member_ready")
        trow_ready = sem("trow_ready")
        table_ready = sem("table_ready")
        in_tile = [sem(f"in_tile{i}") for i in range(RING)]
        out_tile = [sem(f"out_tile{i}") for i in range(RING)]
        xin_own = sem("xin_own")
        xin_ready = sem("xin_ready")
        xt_ready = sem("xt_ready")
        xT_taken = sem("xT_taken")
        w_copied = sem("w_copied")
        hid_ready = sem("hid_ready")
        gelu_ready = sem("gelu_ready")
        high_ready = sem("high_ready")
        split_ready = sem("split_ready")
        e_ready = sem("e_ready")
        half_ready = sem("half_ready")
        row_ready = sem("row_ready")
        row_seen = sem("row_seen")
        ident_ready = sem("ident_ready")

        def load_values(ap, engine, max_val):
            return nc.values_load_multi_w_load_instructions(
                ap, engines=[engine], min_val=0, max_val=max_val,
                skip_runtime_bounds_check_because="the table's entries are clamped when it is made")[1]

        def load_one(ap, engine, max_val):
            return load_values(ap, engine, max_val)[0]

        block = ctx.enter_context(nc.Block())

        def x_bank(s):
            return bank[s % 2][:, 0:D].bitcast(F16)

        @block.sync
        def _(sp):
            sp.dma_start(pay[:, 0:16, 0:D], x[:, 0:16, :]).then_inc(in_graph, 16)
            sp.dma_start(pay[:, 16:NG, 0:D], x[:, 16:NG, :]).then_inc(in_graph, 16)
            sp.dma_start(adjs[:, :].rearrange("p (i j) -> p i j", j=NG), adj[:, 0:NG, 0:NG]).then_inc(in_adj, 16)
            c0 = CHUNKS[0]
            sp.dma_start(pay[:, c0:c0 + CH, 0:D], x[:, c0:c0 + CH, :]).then_inc(in_chunk[0], 16)
            sp.dma_start(wr[:, :], Wr).then_inc(in_router, 16)
            sp.dma_start(brb[:, :], br.rearrange("(o e) -> o e", o=1).to_broadcast([128, E])).then_inc(in_router, 16)
            sp.dma_start(gw1[:, :, :], gW1.rearrange("g d h -> d g h")).then_inc(in_gw, 16)
            sp.dma_start(gw2[:, :, :, :], gW2.rearrange("g (c p) d -> p g c d", c=2)).then_inc(in_gw, 16)
            with nc.allow_non_contiguous_dma(reason="small bias columns"):
                sp.dma_start(gb1s[:, :, :], gb1.rearrange("g (c p) -> p g c", c=2)).then_inc(in_gw, 16)
            sp.dma_start(wb2[:, :, :].rearrange("p g d -> p (g d)"),
                         gb2.rearrange("(o g) d -> o (g d)", o=1).to_broadcast([128, 5 * D])).then_inc(in_gw, 16)
            sp.dma_start(fus[:, :], fusion.rearrange("(o g) -> o g", o=1).to_broadcast([128, 5])).then_inc(in_gw, 16)
            sp.wait_ge(xn_done, 1)
            for g in range(5):
                to = 0
                for first, count in GROUPS[g]:
                    sp.dma_start(xg_dram[g][:, to * D:(to + count) * D],
                                 xn[:, first:first + count, :].rearrange("p i d -> p (i d)")).then_inc(xg_out, 16)
                    to += count
            sp.wait_ge(nt_done, 1)
            for g in range(5):
                sp.dma_start(nt_dram[g], nt_sb[:, OFF2[g]:OFF2[g + 1]]).then_inc(nt_out, 16)
            for c in (1, 2):
                c0 = CHUNKS[c]
                sp.dma_start(pay[:, c0:c0 + CH, 0:D], x[:, c0:c0 + CH, :]).then_inc(in_chunk[c], 16)
            sp.dma_start(pay[:, NG:CH, 0:D], x[:, NG:CH, :]).then_inc(in_chunk[3], 16)
            sp.dma_start(w1f, W1.rearrange("e d h -> d e h")).then_inc(in_experts, 16)
            for c in range(HC):
                sp.dma_start(w2f[:, :, c, :], W2[:, c * 128:(c + 1) * 128, :].rearrange("e p d -> p e d")).then_inc(in_experts, 16)
            with nc.allow_non_contiguous_dma(reason="small columns of scales and biases"):
                sp.dma_start(lng[:, :], ln_g.rearrange("e d -> d e")).then_inc(in_experts, 16)
                sp.dma_start(lnb[:, :], ln_b.rearrange("e d -> d e")).then_inc(in_experts, 16)
            sp.dma_start(b1f, b1).then_inc(in_experts, 16)
            sp.wait_ge(xg_out, 16 * sum(len(r) for r in GROUPS))
            sp.wait_ge(nt_out, 16 * 5)

            def load_pack(i):
                g, q = QUADS[i]
                p = ROWS[g]
                if i >= 2:
                    sp.wait_ge(z_ready, i - 1)
                    sp.wait_ge(bd_ready, i - 1)
                rows = xg_dram[g].rearrange("b (i d) -> (b i) d", d=D)[q * 4 * p:(q + 1) * 4 * p, :]
                sp.dma_start(xpack[0:p, i % 2, :, :], rows.rearrange("(k p) d -> p k d", k=4)).then_inc(in_pack[i % 2], 16)
                rows = nt_dram[g].rearrange("b (m n) -> (b m) n", n=SIZE[g])[q * 4 * p:(q + 1) * 4 * p, :]
                sp.dma_start(npack[0:p, i % 2, :, 0:SIZE[g]], rows.rearrange("(k p) n -> p k n", k=4))\
                    .then_inc(in_pack[i % 2], 16)

            load_pack(0)
            load_pack(1)
            for i, (g, q) in enumerate(QUADS):
                p = ROWS[g]
                if i + 2 < NQ:
                    load_pack(i + 2)
                sp.wait_ge(gpost_ready, i + 1)
                rows = go_dram[g].rearrange("b (i d) -> (b i) d", d=D)[q * 4 * p:(q + 1) * 4 * p, :]
                sp.dma_start(rows.rearrange("(k p) d -> p k d", k=4), gpost[0:p, i % 2, :, :])\
                    .then_inc(go_out[i % 2], 16)
            sp.wait_ge(o_ready, NQ)
            for r in (0, 32):
                sp.dma_start(b2f[r:r + 1, :], b2.rearrange("(o e) d -> o (e d)", o=1)).then_inc(in_b2, 16)
            for i in range(2):
                sp.wait_ge(go_out[i], 16 * (NQ // 2))
            sp.wait_ge(w_low, 2 * E)
            for g in range(5):
                sp.dma_start(gl[:, OFF[g]:OFF[g + 1], :].rearrange("p i d -> p (i d)"), go_dram[g]).then_inc(in_gl, 16)
            sp.wait_ge(consts, 1)
            sp.dma_start(pay_dram[DUMMY * 128:(DUMMY + 1) * 128, :], padding[:, :]).then_inc(pads_out, 16)
            sp.wait_ge(table_ready, 1)
            for p in range(PAIRS):
                r = sp.value_load(padint[0:1, p:p + 1], min_val=0, max_val=DUMMY * 128 - 128)
                sp.dma_start(pay_dram[bass.ds(r, 128), :], padding[:, :]).then_inc(pads_out, 16)
            sp.wait_ge(pads_out, 16 * (PAIRS + 1))
            sp.wait_ge(rows_out, 16 * N)

            def load_tile(t, s, round_):
                r = load_one(place_of[0:1, bass.ds(t, 1)], mybir.EngineType.SP, DUMMY)
                r = sp.snap(r * 128)
                if round_ is not None:
                    sp.wait_ge(out_tile[s], round_ * 16)
                sp.dma_start(prow[s], pay_dram[bass.ds(r, 128), :]).then_inc(in_tile[s], 16)

            for t in range(RING):
                load_tile(t, t, None)
            with sp.Fori(1, TILES // RING) as i:
                for s in range(RING):
                    load_tile(i * RING + s, s, i)
            for t in range(TILES, TABLE):
                load_tile(t, t - TILES, TILES // RING)
            for s in range(RING):
                sp.wait_ge(out_tile[s], TILES // RING * 16)

        @block.gpsimd
        def _(pool):
            nc.gpsimd.memset(padding[:, :], 0.0).then_inc(zeros, 1)
            nc.gpsimd.memset(ones16[:, :], 1.0).then_inc(zeros, 1)
            nc.gpsimd.memset(ident[:, :], 0.0).then_inc(zeros, 1)
            nc.gpsimd.memset(below[:, :], 0.0).then_inc(zeros, 1)
            nc.gpsimd.memset(tri[:, :], 1.0).then_inc(zeros, 1)
            for g in range(4):
                nc.gpsimd.memset(mask[g][:, :], 1.0).then_inc(zeros, 1)
            nc.gpsimd.memset(epsc[:, :], EPS).then_inc(zeros, 1)
            nc.gpsimd.memset(ones64[:, :], S64).then_inc(zeros, 1)
            nc.gpsimd.memset(pick64, 0.0).then_inc(zeros, 1)
            nc.gpsimd.memset(one[:, :], 1.0).then_inc(zeros, 1)
            nc.gpsimd.memset(seen[:, 0, :], 0.0).then_inc(zeros, 1)
            nc.gpsimd.memset(restart[:, :, :], 1.0).then_inc(zeros, 1)
            pool.wait_ge(zeros, 15)
            nc.gpsimd.memset(restart[:, :, 0:1], 0.0)
            nc.gpsimd.iota(padding[:, TOKEN:TOKEN + 1].bitcast(I32), pattern=[[0, 1]], base=NOWHERE, channel_multiplier=0)
            nc.gpsimd.affine_select(out=ident[:, :], in_=ident[:, :], compare_op=ALU.not_equal, fill=1.0, base=0,
                                    pattern=[[-1, 128]], channel_multiplier=1)
            nc.gpsimd.affine_select(out=below[:, :], in_=below[:, :], compare_op=ALU.is_gt, fill=-1.0, base=0,
                                    pattern=[[1, 128]], channel_multiplier=-1)
            nc.gpsimd.affine_select(out=tri[:, :], in_=tri[:, :], compare_op=ALU.is_ge, fill=0.0, base=0,
                                    pattern=[[1, PAIRS]], channel_multiplier=-1)
            for g in range(4):
                nc.gpsimd.affine_select(out=mask[g][:, :], in_=mask[g][:, :], compare_op=ALU.is_ge, fill=0.0,
                                        base=0, pattern=[[-SIZE[g], BATCHES[g]]], channel_multiplier=1).then_inc(zeros, 1)
            pool.wait_ge(zeros, 19)
            for g in range(4):
                nc.gpsimd.affine_select(out=mask[g][:, :], in_=mask[g][:, :], compare_op=ALU.is_ge, fill=0.0,
                                        base=SIZE[g] - 1, pattern=[[SIZE[g], BATCHES[g]]], channel_multiplier=-1)
            nc.gpsimd.iota(pay[:, :, TOKEN:TOKEN + 1].bitcast(I32), pattern=[[1, N], [0, 1]], base=0, channel_multiplier=N)
            for dst, pattern, base, mult in (
                (rev[:, :], [[-1, E]], E, 0), (pairs[:, :], [[1, PAIRS]], 0, 0),
                (tline[:, :], [[1, TABLE]], 0, 0), (vrow[:, 2, :], [[REGION, PAIRS]], -2 * DUMMY, 0),
                (tadd[:, 2, :], [[1, TABLE]], 2 * DUMMY, 0), (padrow[:, 0, :], [[REGION * 128, PAIRS]], 0, 0),
            ):
                nc.gpsimd.iota(dst, pattern=pattern, base=base, channel_multiplier=mult,
                               allow_small_or_imprecise_dtypes=True)
            first = 0
            for a in range(E - 1):
                k = E - 1 - a
                nc.gpsimd.memset(vrow[:, 0, first:first + k], float(a))
                nc.gpsimd.iota(vrow[:, 1, first:first + k], pattern=[[1, k]], base=a + 1, channel_multiplier=0,
                               allow_small_or_imprecise_dtypes=True)
                first += k
            nc.gpsimd.memset(tadd[:, 0:2, :], 0.0).then_inc(consts, 1)
            for c in range(4):
                pool.wait_ge(slots_ready, c + 1)
                for n in range(CHUNKS[c], CHUNKS[c] + CH):
                    nc.gpsimd.indirect_dma_start(
                        out=pay_dram, out_offset=bass.IndirectOffsetOnAxis(ap=slot[:, n:n + 1], axis=0),
                        in_=pay[:, n, :], in_offset=None).then_inc(rows_out, 16)

            last_token = pool.to_reg(B * N - 1)

            def prepare(t, s, i, n):
                pool.wait_ge(in_tile[s % RING], 16 * (i + 1 + s // RING))
                pool.sem_inc(row_seen, 1)
                if n is not None:
                    pool.wait_ge(xt_ready, n)
                    pool.sem_inc(row_seen, 1)
                nc.gpsimd.tensor_scalar(xnt[s % 2][:, 1:D], prow[s % RING][:, 1:D], prow[s % RING][:, RSTD:RSTD + 1],
                                        prow[s % RING][:, NBIAS:NBIAS + 1], ALU.mult, ALU.add).then_inc(xin_own, 1)
                own = 2 * t + 1
                pool.wait_ge(xin_own, own)
                pool.sem_inc(row_seen, 1)
                nc.gpsimd.tensor_copy(xsplit[s % 2][:, 0:D], xnt[s % 2]).then_inc(xin_own, 1)
                pool.wait_ge(xin_own, own + 1)
                nc.gpsimd.tensor_tensor(xsplit[s % 2][:, D:2 * D], xnt[s % 2], xsplit[s % 2][:, 0:D], ALU.subtract)\
                    .then_inc(xin_ready, 1)

            def scatter(s, n):
                pool.wait_ge(row_ready, n)
                pool.sem_inc(row_seen, 1)
                nc.gpsimd.indirect_dma_start(
                    out=out_rows, out_offset=bass.IndirectOffsetOnAxis(ap=prow[s][:, TOKEN:TOKEN + 1].bitcast(I32), axis=0),
                    in_=orow[s], in_offset=None, bounds_check=last_token, oob_is_err=False).then_inc(out_tile[s], 16)

            pool.sem_inc(row_ready, 2 * 4)
            pool.wait_ge(rows_out, 16 * N)
            for k in range(2):
                nc.gpsimd.memset(xnt[k][:, 0:1], S64).then_inc(zeros, 1)
            pool.wait_ge(zeros, 21)
            for t in range(AHEAD):
                prepare(t, t, 0, None)
            for t in range(RING):
                prepare(t + AHEAD, t + AHEAD, 0, t + 1)
                if t >= 4:
                    scatter(t - 4, 2 * t + 1)
            with pool.Fori(1, TILES // RING) as i:
                for s in range(RING):
                    t = i * RING + s
                    prepare(t + AHEAD, s + AHEAD, i, t + 1)
                    scatter((s - 4) % RING, 2 * t + 1)
            for t in range(TILES, TILES + 4):
                scatter((t - 4) % RING, 2 * t + 1)

        @block.scalar
        def _(act):
            own = [0]

            def link(ins):
                own[0] += 1
                ins.then_inc(act_own, 1)
                act.wait_ge(act_own, own[0])

            act.wait_ge(consts, 1)
            act.wait_ge(var_ready, 1)
            nc.scalar.activation(ln[:, 1, 0:NG], ln[:, 0, 0:NG], ACT.Sqrt, bias=epsc[:, :]).then_inc(root_ready, 1)
            act.wait_ge(deg_ready, 1)
            nc.scalar.activation(deg[:, 3, :], deg[:, 2, :], ACT.Sqrt).then_inc(root_ready, 1)

            def root1(c):
                act.wait_ge(var_ready, 2 + 2 * c)
                nc.scalar.activation(ln[:, 1, :], ln[:, 0, :], ACT.Sqrt, bias=epsc[:, :]).then_inc(root_ready, 1)

            def root2(c):
                act.wait_ge(var_ready, 3 + 2 * c)
                nc.scalar.activation(ln[:, 4, :], ln[:, 3, :], ACT.Sqrt, bias=epsc[:, :]).then_inc(root_ready, 1)

            def normalise(c):
                act.wait_ge(ln_ready, c + 1)
                for j in range(GRP):
                    k = GRP * c + j
                    if k >= 2:
                        act.wait_ge(yt_ready, k - 1)
                    for n in range(4):
                        m = 4 * j + n
                        last = nc.scalar.activation(y[:, k % 2, n, :], pay[:, CHUNKS[c] + m, 0:D], ACT.Identity,
                                                    bias=ln[:, 5, m:m + 1], scale=ln[:, 2, m:m + 1])
                    last.then_inc(y_ready, 1)
                    if j >= 1:
                        take_yT(k - 1)
                take_yT(GRP * c + GRP - 1)

            def take_yT(k):
                act.wait_ge(yt_ready, k + 1)
                if k >= 2:
                    act.wait_ge(logits_ready, k - 1)
                nc.scalar.activation(yT[:, k % 2, :], bank[5 + k % 2][:, :], ACT.Copy).then_inc(yT_ready, 1)

            def gap_exp(c):
                act.wait_ge(gap_ready, c + 1)
                nc.scalar.activation(small[:, 6, :], small[:, 5, :], ACT.Exp).then_inc(exp_ready, 1)

            root1(0)
            root2(0)
            normalise(0)
            gap_exp(0)
            act.wait_ge(fmax_ready, 1)
            nc.scalar.activation(fus[:, :], fus[:, :], ACT.Exp, bias=fstat[:, 0:1], accum_out=fstat[:, 1:2])\
                .then_inc(fexp_ready, 1)

            def quad(i):
                g, q = QUADS[i]
                p4 = 4 * ROWS[g]
                act.wait_ge(h_ready, i + 1)
                if i >= 2:
                    act.wait_ge(s_ready, i - 1)
                for c in range(2):
                    last = nc.scalar.activation(hs[:, i % 2, c, 0:p4], bank[1 + c][:, 0:p4], ACT.Relu,
                                                bias=gb1s[:, g, c:c + 1])
                last.then_inc(hs_ready, 1)
                if i >= 1:
                    post(i - 1)

            def post(i):
                g, q = QUADS[i]
                p = ROWS[g]
                act.wait_ge(gpre_ready, i + 1)
                if i >= 2:
                    act.wait_ge(go_out[i % 2], 16 * (i // 2))
                nc.scalar.activation(gpost[0:p, i % 2, :, :], gpre[0:p, :, :], ACT.Relu).then_inc(gpost_ready, 1)

            def expert_high(e):
                if e == 0:
                    act.wait_ge(in_experts, 16 * (1 + HC + 3))
                act.wait_ge(w1_ready, e + 1)
                nc.scalar.activation(w1s[:, e, 0, :], bank[7][:, :], ACT.Copy)
                nc.scalar.activation(w2s[:, e, :, 0, :], w2f[:, e, :, :], ACT.Copy, scale=S64).then_inc(w_high, 1)

            act.wait_ge(in_gw, 16 * 5)
            for i in range(NQ):
                quad(i)
                for c, first in ((1, 0), (2, 5)):
                    if i == first + 1:
                        root1(c)
                    if i == first + 2:
                        root2(c)
                    if i == first + 3:
                        normalise(c)
                    if i == first + 5:
                        gap_exp(c)
                if 10 <= i < 10 + E:
                    expert_high(i - 10)
            post(NQ - 1)
            root1(3)
            root2(3)
            normalise(3)
            gap_exp(3)

            def take_x(s, n):
                act.wait_ge(xt_ready, n)
                nc.scalar.activation(xT[s % 2], x_bank(s), ACT.Copy).then_inc(xT_taken, 2)

            def gelu(v, n):
                act.wait_ge(hid_ready, n)
                act.wait_ge(split_ready, n)
                nc.scalar.activation(hid[v % 4], bank[2 + v % 4][:, :], ACT.Gelu, scale=1.0 / S4096).then_inc(gelu_ready, 1)

            def high(v, n):
                act.wait_ge(gelu_ready, n)
                act.wait_ge(e_ready, n)
                nc.scalar.activation(hh[v % 4], hid[v % 4], ACT.Copy, scale=S64).then_inc(high_ready, 1)

            act.sem_inc(gelu_ready, 1)
            act.sem_inc(high_ready, 2)
            act.wait_ge(rows_out, 16 * N)
            take_x(0, 1)
            for u in range(UNITS):
                gelu(u, u + 1)
                if u >= 1:
                    high(u - 1, u + 1)
                if u % 2 == 0:
                    take_x(u // 2 + 1, u // 2 + 2)
            with act.Fori(1, TILES // RING) as i:
                for v in range(UNITS):
                    n = act.snap(i * UNITS + (v + 1))
                    gelu(v, n)
                    high(v - 1, n)
                    if v % 2 == 0:
                        take_x(v // 2 + 1, i * RING + (v // 2 + 2))
            high(2 * TILES - 1, 2 * TILES + 1)

        @block.tensor
        def _(pe):
            pe.wait_ge(consts, 1)
            pe.wait_ge(in_router, 32)

            def transposes(k):
                pe.wait_ge(y_ready, k + 1)
                if k >= 2:
                    pe.wait_ge(yT_ready, k - 1)
                if k % GRP < 2 and k >= GRP:
                    pe.wait_ge(rank_taken, k // GRP)
                for n in range(4):
                    last = nc.tensor.transpose(bank[5 + k % 2][:, n * 128:(n + 1) * 128], y[:, k % 2, n, :], ident[:, :])
                last.then_inc(yt_ready, 1)

            def logits(k):
                pe.wait_ge(yT_ready, k + 1)
                if k % GRP == 0 and k >= GRP:
                    pe.wait_ge(logits_taken, k // GRP)
                for n in range(4):
                    col = (4 * (k % GRP) + n) * E
                    last = nc.tensor.matmul(bank[7][:, col:col + E], yT[:, k % 2, n * 128:(n + 1) * 128], wr[:, :],
                                            start=True, stop=True)
                last.then_inc(logits_ready, 1)

            def route(c):
                for j in range(GRP):
                    transposes(GRP * c + j)
                    if j >= 1:
                        logits(GRP * c + j - 1)
                logits(GRP * c + GRP - 1)

            def ranks(c):
                pe.wait_ge(hot_ready, c + 1)
                half = PAIRS // 2
                for b in range(2):
                    s = slice(b * half, (b + 1) * half)
                    o = bank[5 + b][:, 0:half * CH].rearrange("p (a n) -> p a n", n=CH)
                    nc.tensor.matmul(o, below[:, :], onehot[:, s, :], start=True, stop=False)
                    nc.tensor.matmul(o, ones16[:, :], running[:, s, :], start=False, stop=False)
                    last = nc.tensor.matmul(o, ones16[:, :],
                                            seen[:, c, s].rearrange("p (a o) -> p a o", o=1).to_broadcast([128, half, CH]),
                                            start=False, stop=True)
                last.then_inc(rank_ready, 1)

            def z(i):
                g, q = QUADS[i]
                p = ROWS[g]
                pe.wait_ge(bd_ready, i + 1)
                if i >= 1:
                    pe.wait_ge(zs_ready, i)
                for k in range(4):
                    last = nc.tensor.matmul(bank[0][:, k * p:(k + 1) * p], xpack[0:p, i % 2, k, :], bd[0:p, i % 2, k, 0:p],
                                            start=True, stop=True)
                last.then_inc(z_ready, 1)

            def h(i):
                g, q = QUADS[i]
                p4 = 4 * ROWS[g]
                pe.wait_ge(zs_ready, i + 1)
                if i >= 1:
                    pe.wait_ge(hs_ready, i)
                for c in range(2):
                    last = nc.tensor.matmul(bank[1 + c][:, 0:p4], gw1[:, g, c * 128:(c + 1) * 128], zs[:, i % 2, 0:p4],
                                            start=True, stop=True)
                last.then_inc(h_ready, 1)

            def s_(i):
                g, q = QUADS[i]
                p = ROWS[g]
                pe.wait_ge(hs_ready, i + 1)
                if i >= 1:
                    pe.wait_ge(ss_ready, i)
                for k in range(4):
                    for c in range(2):
                        last = nc.tensor.matmul(bank[3][0:p, k * D:(k + 1) * D], hs[:, i % 2, c, k * p:(k + 1) * p],
                                                gw2[:, g, c, :], start=(c == 0), stop=(c == 1))
                last.then_inc(s_ready, 1)

            def o(i):
                g, q = QUADS[i]
                p = ROWS[g]
                pe.wait_ge(ss_ready, i + 1)
                if i >= 1:
                    pe.wait_ge(gpre_ready, i)
                for k in range(4):
                    last = nc.tensor.matmul(bank[4][0:p, k * D:(k + 1) * D], bd[0:p, i % 2, k, 0:p], ss[0:p, i % 2, k, :],
                                            start=True, stop=True)
                last.then_inc(o_ready, 1)

            def mix_first(e):
                if e == 0:
                    pe.wait_ge(in_experts, 16 * (1 + HC + 3))
                    pe.wait_ge(logits_taken, 3)
                else:
                    pe.wait_ge(w_low, 2 * e - 1)
                pe.wait_ge(mix_ready, e + 1)
                nc.tensor.matmul(bank[7][:, :], mix[:, e % 2, :], w1f[:, e, :], start=True, stop=False)
                nc.tensor.matmul(bank[7][:, :], pick64[:, e % 2, :], b1f, start=False, stop=True).then_inc(w1_ready, 1)

            route(0)
            ranks(0)
            pe.wait_ge(in_gw, 16 * 5)
            z(0)
            for i in range(NQ):
                h(i)
                if i >= 1:
                    o(i - 1)
                if i + 1 < NQ:
                    z(i + 1)
                s_(i)
                if 10 <= i < 10 + E:
                    mix_first(i - 10)
                for c, first in ((1, 0), (2, 5)):
                    if i == first + 3:
                        route(c)
                    if i == first + 6:
                        ranks(c)
            o(NQ - 1)
            route(3)
            ranks(3)
            pe.wait_ge(seen_ready, 4)
            nc.tensor.matmul(bank[1][0:PAIRS, 0:1], seen[:, 4, :], ones16[:, 0:1], start=True, stop=True)
            nc.tensor.matmul(bank[2][0:1, 0:PAIRS], ones16[:, 0:1], seen[:, 4, :], start=True, stop=True).then_inc(cnt_ready, 1)
            pe.wait_ge(ntile_ready, 1)
            nc.tensor.matmul(bank[3][0:PAIRS, 0:1], tri[:, :], tcnt[:, 1:2], start=True, stop=True)
            for k in range(3):
                last = nc.tensor.matmul(bank[3][0:PAIRS, 1 + k:2 + k], vrow[:, k, :], one[:, :], start=True, stop=True)
            last.then_inc(tincl_ready, 1)
            pe.wait_ge(member_ready, 1)
            for k in range(3):
                last = nc.tensor.matmul(bank[4][0:1, k * TABLE:(k + 1) * TABLE], tcnt[:, 4 + k:5 + k], inpair[:, :],
                                        start=True, stop=True)
            last.then_inc(trow_ready, 1)

            def turn(s, n):
                pe.wait_ge(xin_ready, n)
                for part in range(2):
                    last = nc.tensor.transpose(x_bank(s)[:, part * D:(part + 1) * D],
                                               xsplit[s % 2][:, part * D:(part + 1) * D], ident16[:, :])
                last.then_inc(xt_ready, 1)

            def first_layer(v, n):
                if v % 2 == 0:
                    pe.wait_ge(xT_taken, n)
                pe.wait_ge(w_copied, n)
                w, x2 = wbuf[v % WRING], xT[v // 2 % 2]
                for c in range(HC):
                    o = bank[2 + v % 4][:, c * 128:(c + 1) * 128]
                    wh, wl = (w[:, part * H + c * 128:part * H + (c + 1) * 128] for part in range(2))
                    nc.tensor.matmul(o, wh, x2[:, 0:D], start=True, stop=False)
                    nc.tensor.matmul(o, wh, x2[:, D:2 * D], start=False, stop=False)
                    last = nc.tensor.matmul(o, wl, x2[:, 0:D], start=False, stop=True)
                last.then_inc(hid_ready, 1)

            def second_layer(v, n):
                if v % 2 == 0:
                    pe.wait_ge(row_ready, n)
                w = wbuf[v % WRING][:, 2 * H:BLOCK]
                o = bank[6 + v // 2 % 2][:, v % 2 * D:(v % 2 + 1) * D]
                nc.tensor.matmul(o, ones64[:, :], w[:, 2 * H:2 * H + D], start=True, stop=False)
                for c in range(HC):
                    wh, wl = (w[:, (2 * c + part) * D:(2 * c + part + 1) * D] for part in range(2))
                    a, b = hh[v % 4][:, c * 128:(c + 1) * 128], hl[v % 4][:, c * 128:(c + 1) * 128]
                    nc.tensor.matmul(o, a, wh, start=False, stop=False)
                    nc.tensor.matmul(o, a, wl, start=False, stop=False)
                    last = nc.tensor.matmul(o, b, wh, start=False, stop=(c == HC - 1))
                last.then_inc(e_ready, 1)

            pe.sem_inc(e_ready, 5)
            pe.wait_ge(rows_out, 16 * N)
            pe.wait_ge(ident_ready, 1)
            pe.wait_ge(b2_done, 1)
            turn(0, 1)
            for u in range(UNITS):
                if u % 2 == 0:
                    turn(u // 2 + 1, u // 2 + 2)
                pe.wait_ge(split_ready, u + 1)
                first_layer(u, u + 1)
                if u >= 2 * BACK:
                    second_layer(u - 2 * BACK, u + 1)
            with pe.Fori(1, TILES // RING) as i:
                for v in range(UNITS):
                    n = pe.snap(i * UNITS + (v + 1))
                    if v % 2 == 0:
                        turn(v // 2 + 1, i * RING + (v // 2 + 2))
                    pe.wait_ge(split_ready, n)
                    first_layer(v, n)
                    second_layer(v - 2 * BACK, n)
            for u in range(2 * TILES, 2 * TILES + 2 * BACK):
                pe.wait_ge(split_ready, u + 1)
                second_layer(u - 2 * BACK, u + 1)

        @block.vector
        def _(dve):
            own = [0]
            V = nc.vector

            def link(ins):
                own[0] += 1
                ins.then_inc(vec, 1)
                dve.wait_ge(vec, own[0])

            dve.wait_ge(consts, 1)
            V.tensor_copy(ident16[:, :], ident[:, :]).then_inc(ident_ready, 1)

            def moments(first, count):
                for j in range(count):
                    last = V.bn_stats(stat[:, j, :], pay[:, first + j, 0:D])
                link(last)
                me, mo, qe, qo = (stat[:, 0:count, k] for k in (1, 4, 2, 5))
                V.tensor_tensor(small[:, 0, 0:count], me, mo, ALU.subtract)
                V.tensor_tensor(small[:, 1, 0:count], me, mo, ALU.add)
                link(V.tensor_tensor(small[:, 2, 0:count], qe, qo, ALU.add))
                link(V.scalar_tensor_tensor(out=small[:, 3, 0:count], in0=small[:, 0, 0:count], scalar=D / 4.0,
                                            in1=small[:, 0, 0:count], op0=ALU.mult, op1=ALU.mult))
                link(V.tensor_tensor(small[:, 4, 0:count], small[:, 2, 0:count], small[:, 3, 0:count], ALU.add))
                V.tensor_scalar(ln[:, 0, 0:count], small[:, 4, 0:count], 1.0 / D, None, ALU.mult).then_inc(var_ready, 1)

            dve.wait_ge(in_graph, 32)
            moments(0, NG)
            dve.wait_ge(root_ready, 1)
            link(V.reciprocal(ln[:, 2, 0:NG], ln[:, 1, 0:NG]))
            link(V.scalar_tensor_tensor(out=ln[:, 5, 0:NG], in0=small[:, 1, 0:NG], scalar=-0.5, in1=ln[:, 2, 0:NG],
                                        op0=ALU.mult, op1=ALU.mult))
            for j in range(NG):
                last = V.tensor_scalar(xn[:, j, :], pay[:, j, 0:D], ln[:, 2, j:j + 1], ln[:, 5, j:j + 1],
                                       ALU.mult, ALU.add)
            last.then_inc(xn_done, 1)
            dve.wait_ge(in_adj, 16)
            link(V.tensor_scalar(adjs[:, 0:NG * NG:NG + 1], adjs[:, 0:NG * NG:NG + 1], 1.0, None, ALU.add))
            whole = adjs[:, :].rearrange("p (i j) -> p i j", j=NG)

            def square(g, t=acomp):
                return t[:, OFF2[g]:OFF2[g + 1]].rearrange("p (i j) -> p i j", j=SIZE[g])

            for g in range(5):
                row = 0
                for i0, ni in GROUPS[g]:
                    col = 0
                    for j0, nj in GROUPS[g]:
                        last = V.tensor_copy(square(g)[:, row:row + ni, col:col + nj], whole[:, i0:i0 + ni, j0:j0 + nj])
                        col += nj
                    row += ni
            link(last)
            for g in range(5):
                last = V.tensor_reduce(deg[:, 0, OFF[g]:OFF[g + 1]], square(g), AX_X, ALU.add)
            link(last)
            link(V.tensor_scalar(deg[:, 1, :], deg[:, 0, :], 0.0, None, ALU.is_equal))
            V.tensor_tensor(deg[:, 2, :], deg[:, 0, :], deg[:, 1, :], ALU.add).then_inc(deg_ready, 1)
            link(V.tensor_scalar(deg[:, 4, :], deg[:, 1, :], -1.0, 1.0, ALU.mult, ALU.add))
            dve.wait_ge(root_ready, 2)
            link(V.reciprocal(deg[:, 5, :], deg[:, 3, :]))
            link(V.tensor_tensor(deg[:, 3, :], deg[:, 5, :], deg[:, 4, :], ALU.mult))
            for g in range(5):
                s = SIZE[g]
                inv = deg[:, 3, OFF[g]:OFF[g + 1]].rearrange("p (o n) -> p o n", o=1).to_broadcast([128, s, s])
                last = V.tensor_tensor(square(g, nt_sb), square(g).rearrange("p n m -> p m n"), inv, ALU.mult)
            link(last)
            for g in range(5):
                s = SIZE[g]
                inv = deg[:, 3, OFF[g]:OFF[g + 1]].rearrange("p (m o) -> p m o", o=1).to_broadcast([128, s, s])
                last = V.tensor_tensor(square(g, nt_sb), square(g, nt_sb), inv, ALU.mult)
            last.then_inc(nt_done, 1)

            def norms(c):
                dve.wait_ge(in_chunk[c], 16)
                if c == 3:
                    dve.wait_ge(gl_added, 1)
                if c >= 1:
                    dve.wait_ge(y_ready, GRP * c)
                moments(CHUNKS[c], CH)

            def norms2(c):
                dve.wait_ge(root_ready, 3 + 2 * c)
                link(V.reciprocal(ln[:, 2, :], ln[:, 1, :]))
                link(V.tensor_tensor(small[:, 2, :], ln[:, 0, :], ln[:, 2, :], ALU.mult))
                link(V.tensor_tensor(ln[:, 3, :], small[:, 2, :], ln[:, 2, :], ALU.mult))
                V.tensor_scalar(small[:, 3, :], small[:, 1, :], -0.5, None, ALU.mult).then_inc(var_ready, 1)
                link(V.scalar_tensor_tensor(out=ln[:, 5, :], in0=small[:, 1, :], scalar=-0.5, in1=ln[:, 2, :],
                                            op0=ALU.mult, op1=ALU.mult))

            def norms3(c):
                row = pay[:, CHUNKS[c]:CHUNKS[c] + CH, :]
                dve.wait_ge(root_ready, 4 + 2 * c)
                link(V.reciprocal(small[:, 4, :], ln[:, 4, :]))
                link(V.scalar_tensor_tensor(out=row[:, :, RSTD], in0=small[:, 4, :], scalar=S64, in1=ln[:, 2, :],
                                            op0=ALU.mult, op1=ALU.mult))
                V.tensor_tensor(row[:, :, NBIAS], small[:, 3, :], row[:, :, RSTD], ALU.mult).then_inc(ln_ready, 1)

            def over(v):
                return v.rearrange("p (n o) -> p n o", o=1).to_broadcast([128, CH, E])

            def route(c):
                dve.wait_ge(logits_ready, GRP * (c + 1))
                revb = rev[:, :].rearrange("p (o e) -> p o e", o=1).to_broadcast([128, CH, E])
                brbb = brb[:, :].rearrange("p (o e) -> p o e", o=1).to_broadcast([128, CH, E])
                V.tensor_tensor(logit[:, :, :], bank[7][:, 0:CH * E].rearrange("p (n e) -> p n e", e=E), brbb, ALU.add)\
                    .then_inc(logits_taken, 1)
                dve.wait_ge(logits_taken, c + 1)
                for k in range(2):
                    link(V.tensor_reduce(small[:, k, :], logit[:, :, :], AX_X, ALU.max))
                    link(V.tensor_tensor(pick[:, :, :], logit[:, :, :], over(small[:, k, :]), ALU.is_ge))
                    link(V.tensor_tensor(score[:, :, :], pick[:, :, :], revb, ALU.mult))
                    link(V.tensor_reduce(small[:, 2 + k, :], score[:, :, :], AX_X, ALU.max))
                    if k == 0:
                        link(V.tensor_tensor(pick[:, :, :], revb, over(small[:, 2, :]), ALU.is_equal))
                        link(V.scalar_tensor_tensor(out=logit[:, :, :], in0=pick[:, :, :], scalar=NEG,
                                                    in1=logit[:, :, :], op0=ALU.mult, op1=ALU.add))
                V.tensor_tensor(small[:, 5, :], small[:, 1, :], small[:, 0, :], ALU.subtract).then_inc(gap_ready, 1)
                V.tensor_tensor(small[:, 7, :], small[:, 2, :], small[:, 3, :], ALU.max)
                V.tensor_tensor(small[:, 8, :], small[:, 2, :], small[:, 3, :], ALU.min)
                link(V.tensor_tensor(small[:, 9, :], small[:, 2, :], small[:, 3, :], ALU.is_gt))
                V.tensor_scalar(small[:, 10, :], small[:, 7, :], -0.5, E / 2.0, ALU.mult, ALU.add)
                link(V.tensor_tensor(small[:, 11, :], small[:, 7, :], small[:, 8, :], ALU.subtract))
                link(V.scalar_tensor_tensor(out=small[:, 12, :], in0=small[:, 7, :], scalar=E - 1.0,
                                            in1=small[:, 10, :], op0=ALU.add, op1=ALU.mult))
                link(V.scalar_tensor_tensor(out=small[:, 13, :], in0=small[:, 12, :], scalar=-1.0,
                                            in1=small[:, 11, :], op0=ALU.add, op1=ALU.add))
                link(V.tensor_tensor(
                    onehot[:, :, :], small[:, 13, :].rearrange("p (o n) -> p o n", o=1).to_broadcast([128, PAIRS, CH]),
                    pairs[:, :].rearrange("p (a o) -> p a o", o=1).to_broadcast([128, PAIRS, CH]), ALU.is_equal))
                link(V.tensor_tensor_scan(running[:, :, :].rearrange("p a n -> p (a n)"),
                                          restart[:, :, :].rearrange("p a n -> p (a n)"),
                                          onehot[:, :, :].rearrange("p a n -> p (a n)"), 0.0, ALU.mult, ALU.add))
                V.tensor_tensor(seen[:, c + 1, :], seen[:, c, :], running[:, :, CH - 1], ALU.add).then_inc(seen_ready, 1)
                V.tensor_scalar(small[:, 14, :], small[:, 13, :], float(REGION * 128), None, ALU.mult).then_inc(hot_ready, 1)
                dve.wait_ge(exp_ready, c + 1)
                link(V.tensor_scalar(small[:, 10, :], small[:, 6, :], 1.0, S4096, ALU.add, ALU.mult))
                link(V.reciprocal(small[:, 11, :], small[:, 10, :]))
                link(V.tensor_tensor(small[:, 12, :], small[:, 6, :], small[:, 11, :], ALU.mult))
                link(V.tensor_tensor(small[:, 10, :], small[:, 11, :], small[:, 12, :], ALU.subtract))
                link(V.tensor_tensor(small[:, 15, :], small[:, 10, :], small[:, 9, :], ALU.mult))
                row = pay[:, CHUNKS[c]:CHUNKS[c] + CH, :]
                V.tensor_tensor(row[:, :, WA], small[:, 12, :], small[:, 15, :], ALU.add)
                V.tensor_tensor(row[:, :, WB], small[:, 11, :], small[:, 15, :], ALU.subtract)

            def place(c):
                dve.wait_ge(rank_ready, c + 1)
                half = PAIRS // 2
                for b in range(2):
                    s = slice(b * half, (b + 1) * half)
                    last = V.tensor_tensor(rank[:, s, :], bank[5 + b][:, 0:half * CH].rearrange("p (a n) -> p a n", n=CH),
                                           onehot[:, s, :], ALU.mult)
                last.then_inc(rank_taken, 1)
                dve.wait_ge(rank_taken, c + 1)
                link(V.tensor_reduce(small[:, 12, :], rank[:, :, :].rearrange("p a n -> p n a"), AX_X, ALU.add))
                V.tensor_tensor(slot[:, CHUNKS[c]:CHUNKS[c] + CH], small[:, 12, :], small[:, 14, :], ALU.add)\
                    .then_inc(slots_ready, 1)

            norms(0)
            norms2(0)
            norms3(0)
            route(0)
            place(0)
            dve.wait_ge(in_gw, 16 * 5)
            V.tensor_reduce(fstat[:, 0:1], fus[:, :], AX_X, ALU.max, negate=True).then_inc(fmax_ready, 1)
            dve.wait_ge(fexp_ready, 1)
            link(V.reciprocal(fstat[:, 2:3], fstat[:, 1:2]))
            link(V.tensor_scalar(fus[:, :], fus[:, :], fstat[:, 2:3], None, ALU.mult))
            link(V.tensor_tensor(wb2[:, :, :], wb2[:, :, :],
                                 fus[:, :].rearrange("p (g o) -> p g o", o=1).to_broadcast([128, 5, D]), ALU.mult))

            def blocks(i):
                g, q = QUADS[i]
                p, s, n = ROWS[g], SIZE[g], BATCHES[g]
                dve.wait_ge(in_pack[i % 2], 32 * (i // 2 + 1))
                if i >= 2:
                    dve.wait_ge(o_ready, i - 1)
                for k in range(4):
                    last = V.tensor_tensor(
                        bd[0:p, i % 2, k, 0:p].rearrange("p (b n) -> p b n", n=s),
                        npack[0:p, i % 2, k, 0:s].rearrange("p (o n) -> p o n", o=1).to_broadcast([p, n, s]),
                        mask[min(g, 3)][0:p, :].rearrange("p (b o) -> p b o", o=1).to_broadcast([p, n, s]), ALU.mult)
                last.then_inc(bd_ready, 1)

            def take_z(i):
                p4 = 4 * ROWS[QUADS[i][0]]
                dve.wait_ge(z_ready, i + 1)
                if i >= 2:
                    dve.wait_ge(h_ready, i - 1)
                V.tensor_copy(zs[:, i % 2, 0:p4], bank[0][:, 0:p4]).then_inc(zs_ready, 1)

            def take_s(i):
                p = ROWS[QUADS[i][0]]
                dve.wait_ge(s_ready, i + 1)
                if i >= 2:
                    dve.wait_ge(o_ready, i - 1)
                V.tensor_copy(ss[0:p, i % 2, :, :], bank[3][0:p, :].rearrange("p (k d) -> p k d", d=D)).then_inc(ss_ready, 1)

            def take_o(i):
                g = QUADS[i][0]
                p = ROWS[g]
                dve.wait_ge(o_ready, i + 1)
                if i >= 1:
                    dve.wait_ge(gpost_ready, i)
                V.scalar_tensor_tensor(
                    out=gpre[0:p, :, :], in0=bank[4][0:p, :].rearrange("p (k d) -> p k d", d=D),
                    scalar=fus[0:p, g:g + 1],
                    in1=wb2[0:p, g, :].rearrange("p (o d) -> p o d", o=1).to_broadcast([p, 4, D]),
                    op0=ALU.mult, op1=ALU.add).then_inc(gpre_ready, 1)

            def mix_for(e):
                if e == 0:
                    dve.wait_ge(in_experts, 16 * (1 + HC + 3))
                    link(V.tensor_scalar(g64[:, :], lng[:, :], S64, None, ALU.mult))
                elif e >= 2:
                    dve.wait_ge(w1_ready, e - 1)
                V.tensor_scalar(pick64[:, e % 2, 0:1], ident[0:E, e:e + 1], S64, None, ALU.mult)
                link(V.tensor_scalar(mix[:, e % 2, :], ident[:, :], g64[:, e:e + 1], None, ALU.mult))
                link(V.tensor_scalar(mix[0:1, e % 2, :], ones64[0:1, :], lng[0:1, e:e + 1], -1.0, ALU.mult, ALU.mult))
                V.tensor_scalar(mix[:, e % 2, 0:1], lnb[:, e:e + 1], S64, None, ALU.mult).then_inc(mix_ready, 1)

            def expert_low(e):
                dve.wait_ge(w_high, e + 1)
                V.tensor_tensor(w1s[:, e, 1, :], bank[7][:, :], w1s[:, e, 0, :], ALU.subtract).then_inc(w_low, 1)
                V.memset(b2s[:, e, :], 0.0)
                V.scalar_tensor_tensor(out=w2s[:, e, :, 1, :], in0=w2f[:, e, :, :], scalar=S64,
                                       in1=w2s[:, e, :, 0, :], op0=ALU.mult, op1=ALU.subtract).then_inc(w_low, 1)

            blocks(0)
            blocks(1)
            take_z(0)
            for i in range(NQ):
                if i >= 1:
                    take_o(i - 1)
                    if i + 1 < NQ:
                        blocks(i + 1)
                if i + 1 < NQ:
                    take_z(i + 1)
                take_s(i)
                for c, first in ((1, 0), (2, 5)):
                    if i == first:
                        norms(c)
                    if i == first + 2:
                        norms2(c)
                    if i == first + 3:
                        norms3(c)
                    if i == first + 5:
                        route(c)
                    if i == first + 7:
                        place(c)
                if 9 <= i < 9 + E:
                    mix_for(i - 9)
                if 10 <= i < 10 + E:
                    expert_low(i - 10)
            take_o(NQ - 1)
            dve.wait_ge(in_b2, 32)
            by_e = (lambda v: v.rearrange("p (e d) -> p e d", e=E))
            V.tensor_scalar(b2s[0:1, :, :], by_e(b2f[0:1, :]), S64, None, ALU.mult)
            link(V.tensor_scalar(b2hi[32:33, 0:E * D], b2f[32:33, :], S64, None, ALU.mult))
            V.scalar_tensor_tensor(out=b2s[32:33, :, :], in0=by_e(b2f[32:33, :]), scalar=S64, in1=by_e(b2hi[32:33, 0:E * D]),
                                   op0=ALU.mult, op1=ALU.subtract).then_inc(b2_done, 1)
            dve.wait_ge(in_gl, 16 * 5)
            for g in range(5):
                col = OFF[g]
                for first, count in GROUPS[g]:
                    v = pay[:, first:first + count, 0:D]
                    last = V.tensor_tensor(v, v, gl[:, col:col + count, :], ALU.add)
                    col += count
                    if g < 4 or first != GROUPS[4][-1][0]:
                        link(last)
            last.then_inc(gl_added, 1)
            norms(3)
            norms2(3)
            norms3(3)
            route(3)
            place(3)

            dve.wait_ge(cnt_ready, 1)
            V.tensor_tensor(padint[:, :], bank[2][0:1, 0:PAIRS], padrow[:, 0, :], ALU.add)
            link(V.tensor_scalar(tint[:, 0:1], bank[1][0:PAIRS, 0:1], 127.0, None, ALU.add))
            link(V.tensor_scalar(tint[:, 1:2], tint[:, 0:1], 7, None, ALU.arith_shift_right))
            V.tensor_copy(tcnt[:, 1:2], tint[:, 1:2]).then_inc(ntile_ready, 1)
            dve.wait_ge(tincl_ready, 1)
            link(V.tensor_copy(tcnt[:, 2:3], bank[3][0:PAIRS, 0:1]))
            link(V.tensor_tensor(tcnt[:, 3:4], tcnt[:, 2:3], tcnt[:, 1:2], ALU.subtract))
            V.tensor_copy(tcnt[:, 4:6], bank[3][0:PAIRS, 1:3])
            V.tensor_tensor(tcnt[:, 6:7], bank[3][0:PAIRS, 3:4], tcnt[:, 3:4], ALU.subtract)
            V.tensor_scalar(ahead[:, :], tline[:, :], tcnt[:, 3:4], None, ALU.is_ge)
            link(V.tensor_scalar(inpair[:, :], tline[:, :], tcnt[:, 2:3], None, ALU.is_ge))
            V.tensor_tensor(inpair[:, :], ahead[:, :], inpair[:, :], ALU.subtract).then_inc(member_ready, 1)
            dve.wait_ge(trow_ready, 1)
            link(V.tensor_tensor(tadd[:, 0:3, :], bank[4][0:1, 0:3 * TABLE].rearrange("p (k t) -> p k t", k=3),
                                 tadd[:, 0:3, :], ALU.add))
            V.tensor_copy(experts[:, :, :].rearrange("p t k -> p k t"), tadd[:, 0:2, :])
            V.tensor_scalar(place_of[:, :], tadd[:, 2, :], float(DUMMY), None, ALU.min).then_inc(table_ready, 1)

            def copy_weights(t, s):
                pair = load_values(experts[0:1, bass.ds(t, 1), :].rearrange("p t k -> p (t k)"), mybir.EngineType.DVE, E - 1)
                for k in range(2):
                    V.tensor_copy(wbuf[(2 * s + k) % WRING], blocks_w[:, bass.ds(pair[k], 1), :].rearrange("p e w -> p (e w)"))\
                        .then_inc(w_copied, 1)

            def low(v, n):
                dve.wait_ge(high_ready, n)
                V.scalar_tensor_tensor(out=hl[v % 4], in0=hid[v % 4], scalar=S64, in1=hh[v % 4], op0=ALU.mult,
                                       op1=ALU.subtract).then_inc(split_ready, 1)

            def combine(t, s):
                r, b = prow[s % RING], bank[6 + s % 2]
                V.scalar_tensor_tensor(out=orow[s % RING], in0=b[:, 0:D], scalar=r[:, WA:WA + 1], in1=r[:, 0:D],
                                       op0=ALU.mult, op1=ALU.add).then_inc(half_ready, 1)
                dve.wait_ge(half_ready, t + 1)
                V.scalar_tensor_tensor(out=orow[s % RING], in0=b[:, D:2 * D], scalar=r[:, WB:WB + 1], in1=orow[s % RING],
                                       op0=ALU.mult, op1=ALU.add).then_inc(row_ready, 2)

            dve.sem_inc(split_ready, 4)
            dve.wait_ge(rows_out, 16 * N)
            dve.wait_ge(table_ready, 1)
            copy_weights(0, 0)
            for u in range(UNITS):
                t = u // 2
                dve.wait_ge(e_ready, u + 1)
                if u % 2 == 0:
                    copy_weights(t + 1, t + 1)
                    if t >= 3:
                        combine(t - 3, t - 3)
                if u >= 2:
                    low(u - 2, u + 1)
            with dve.Fori(1, TILES // RING) as i:
                for v in range(UNITS):
                    t = i * RING + v // 2
                    n = dve.snap(i * UNITS + (v + 1))
                    dve.wait_ge(e_ready, n)
                    if v % 2 == 0:
                        copy_weights(t + 1, v // 2 + 1)
                        combine(t - 3, v // 2 - 3)
                    low(v - 2, n)
            for u in range(2 * TILES, 2 * TILES + 5):
                t = u // 2
                dve.wait_ge(e_ready, u + 1)
                if u % 2 == 0:
                    combine(t - 3, t - 3)
                if u < 2 * TILES + 2:
                    low(u - 2, u + 1)


_INS = ['x', 'adj', 'L0_gnn_W1', 'L0_gnn_b1', 'L0_gnn_W2', 'L0_gnn_b2', 'L0_gnn_fusion_w', 'L0_ffn_Wr', 'L0_ffn_br',
        'L0_ffn_ln_g', 'L0_ffn_ln_b', 'L0_ffn_W1', 'L0_ffn_b1', 'L0_ffn_W2', 'L0_ffn_b2']


def kernel(**inputs):
    import numpy as _np
    import concourse.bacc as _bacc
    from concourse import mybir as _mybir
    from concourse.bass_utils import run_bass_kernel_spmd as _run

    nc = _bacc.Bacc("TRN2", target_bir_lowering=False, num_devices=1)
    arrays, args = {}, []
    for name in _INS:
        a = _np.ascontiguousarray(inputs[name])
        arrays[f"in_{name}"] = a
        args.append(nc.dram_tensor(f"in_{name}", a.shape, _mybir.dt.from_np(a.dtype), kind="ExternalInput").ap())
    args.append(nc.dram_tensor("out_0", (B, N, D), _mybir.dt.float32, kind="ExternalOutput").ap())
    build(nc, *args)
    r = _run(nc, [arrays], core_ids=[0])
    return r.results[0]["out_0"]
```

```python
from contextlib import ExitStack

import concourse.bass as bass
import numpy as np
from concourse import mybir

ALU = mybir.AluOpType
ACT = mybir.ActivationFunctionType
AX_X = mybir.AxisListType.X
F32 = mybir.dt.float32
F16 = mybir.dt.float16
BF16 = mybir.dt.bfloat16
I32 = mybir.dt.int32

B = N = D = 128
GROUPS = [[(0, 25)], [(0, 9)], [(0, 1), (9, 6)], [(6, 3), (12, 3)], [(3, 3), (9, 3)]]
SIZE = [sum(c for _, c in r) for r in GROUPS]
BATCHES = [4, 8, 16, 16, 16]
OFF = [sum(SIZE[:g]) for g in range(6)]
OFF2 = [sum(s * s for s in SIZE[:g]) for g in range(6)]
NG = SIZE[0]
COLS = OFF[5]
HID = 256
ROWS = [BATCHES[g] * SIZE[g] for g in range(5)]
QUADS = [(g, q) for g in range(5) for q in range(B // BATCHES[g] // 4)]
NQ = len(QUADS)

E, H = 8, 512
HC = H // 128
PAIRS = E * (E - 1) // 2
CH = 32
CHUNKS = [(32, 32), (64, 32), (96, 32), (16, 16), (0, 16)]
NC = len(CHUNKS)
FOURS = [(c, j) for c in range(NC) for j in range(CHUNKS[c][1] // 4)]
FIRST4 = [FOURS.index((c, 0)) for c in range(NC)] + [len(FOURS)]
STATS_AT = {0: (1, 0), 1: (1, 1), 4: (2, 0), 5: (2, 1), 9: (3, 0)}
FACTORS_AT = {1: 1, 5: 2, 9: 3}
FOURS_AT = {0: (0, 2), 1: (4, 6), 2: (8,), 3: (10,), 4: (12,), 5: (14,), 6: (16,),
            7: (18,), 8: (20,), 9: (22,), 10: (24,), 11: (26,)}
TOP2_AT = {2: 0, 6: 1, 10: 2, 13: 3}
PAIR_AT = {3: 0, 7: 1, 11: 2, 14: 3}
PLACE_AT = {i + 1: c for i, c in PAIR_AT.items()}
SECOND_AT = 10
FIRST_AT = 16
EARLY = NQ - FIRST_AT
LOGW = 96
NBIAS, RSTD, WA, WB, TOKEN = 128, 129, 130, 131, 132
ROW = 133
REGION = B * N // 128 + 1
DUMMY = PAIRS * REGION
TILES = B * N // 128 + PAIRS
RING = 12
AHEAD = 2
BACK = 2
UNITS = 2 * RING
WRING = 8
BLOCK = 4 * H + D
TABLE = TILES + AHEAD
EPS = 1e-5
S64 = 64.0
S4096 = S64 * S64
NOWHERE = 1 << 20
NEG = -1e30


def build(nc, x, adj, gW1, gb1, gW2, gb2, fusion, Wr, br, ln_g, ln_b, W1, b1, W2, b2, out):
    with ExitStack() as ctx:
        def sb(name, shape, dt=F32):
            return ctx.enter_context(nc.sbuf_tensor(name, shape, dt))

        def sem(name):
            return ctx.enter_context(nc.semaphore(name))

        xg_dram = [nc.dram_tensor(f"xg{g}", [B, SIZE[g] * D], F32).ap() for g in range(5)]
        nt_dram = [nc.dram_tensor(f"nt{g}", [B, SIZE[g] ** 2], F32).ap() for g in range(5)]
        go_dram = [nc.dram_tensor(f"go{g}", [B, SIZE[g] * D], F32).ap() for g in range(5)]
        pay_dram = nc.dram_tensor("pay_rows", [(DUMMY + 1) * 128, ROW], F32).ap()
        out_rows = out.rearrange("b n d -> (b n) d")

        bank = [ctx.enter_context(nc.psum_tensor(f"bank{i}", [128, 512], F32)) for i in range(8)]

        pay = sb("pay", [128, N, ROW])
        slot = sb("slot", [128, N], I32)
        deg = sb("deg", [128, 6, COLS])
        gw1 = sb("gw1", [128, 5, HID])
        gw2 = sb("gw2", [128, 5, 2, D])
        gb1s = sb("gb1s", [128, 5, 2])
        wb2 = sb("wb2", [128, 5, D])
        fus = sb("fus", [128, 5])
        fstat = sb("fstat", [128, 4])
        mask = [sb(f"mask{g}", [128, BATCHES[g]]) for g in range(4)]
        xpack = sb("xpack", [128, 2, 4, D])
        npack = sb("npack", [128, 2, 4, NG])
        bd = sb("bd", [128, 3, 4, 128])
        zs = sb("zs", [128, 2, 512])
        hs = sb("hs", [128, 2, 2, 4 * max(ROWS)])
        ss = sb("ss", [128, 2, 4, D])
        gpost = sb("gpost", [128, 2, 4, D])
        stat = sb("stat", [128, CH, 6])
        ln = sb("ln", [128, 2, 6, CH])
        mom = sb("mom", [128, 5, CH])
        y = sb("y", [128, 2, 4, D])
        yT = sb("yT", [128, 2, 512])
        wr = sb("wr", [128, LOGW])
        brb = sb("brb", [128, E])
        rev = sb("rev", [128, E])
        logit = sb("logit", [128, CH, E])
        small = sb("small", [128, 16, CH])
        pairs = sb("pairs", [128, PAIRS])
        onehot = sb("onehot", [128, PAIRS * CH], BF16)
        running = sb("running", [128, PAIRS * CH], BF16)
        restart = {n: sb(f"restart{n}", [128, PAIRS * n], BF16) for n in sorted({n for _, n in CHUNKS})}
        rank = sb("rank", [128, PAIRS * CH])
        scratch = rank[:, :]
        pick = scratch[:, 0:CH * E].rearrange("p (n e) -> p n e", e=E)
        score = scratch[:, CH * E:2 * CH * E].rearrange("p (n e) -> p n e", e=E)
        inpair = scratch[0:PAIRS, 0:TABLE]
        ahead = scratch[0:PAIRS, TABLE:2 * TABLE]
        seen = sb("seen", [128, NC + 1, PAIRS], BF16)
        ones16 = sb("ones16", [128, 128], BF16)
        below = sb("below", [128, 128], BF16)
        ident = sb("ident", [128, 128])
        vrow = sb("vrow", [1, 3, PAIRS])
        one = sb("one", [1, 1])
        tri = sb("tri", [PAIRS, PAIRS])
        tline = sb("tline", [PAIRS, TABLE])
        tcnt = sb("tcnt", [PAIRS, 8])
        tint = sb("tint", [PAIRS, 2], I32)
        experts = sb("experts", [1, TABLE, 2], I32)
        place_of = sb("place_of", [1, TABLE], I32)
        padrow = sb("padrow", [1, 2, PAIRS])
        padint = sb("padint", [1, PAIRS], I32)
        padding = sb("padding", [128, ROW])
        stage = sb("stage", [128, E * H * 2])
        w1f = stage[:, 0:E * H].rearrange("p (e h) -> p e h", e=E)
        w2f = stage[:, E * H:2 * E * H].rearrange("p (e c d) -> p e c d", e=E, c=HC)
        split_w = sb("split_w", [128, E * BLOCK // 2])
        blocks_w = split_w[:, :].bitcast(F16).rearrange("p (e w) -> p e w", e=E)
        w1s = blocks_w[:, :, 0:2 * H].rearrange("p e (t h) -> p e t h", t=2)
        w2s = blocks_w[:, :, 2 * H:4 * H].rearrange("p e (c t d) -> p e c t d", c=HC, t=2)
        b2s = blocks_w[:, :, 4 * H:BLOCK]
        last_block = split_w[:, (E - 1) * BLOCK // 2:E * BLOCK // 2]
        b1f = last_block[0:E, 0:H]
        mix = last_block[:, H:H + 2 * D].rearrange("p (a m) -> p a m", a=2)
        pick64 = last_block[0:E, H + 2 * D:H + 4 * D].rearrange("p (a m) -> p a m", a=2)
        xn = split_w[:, 0:NG * D].rearrange("p (i d) -> p i d", d=D)
        at0 = NG * D
        adjs = split_w[:, at0:at0 + NG * NG]
        at0 += NG * NG
        acomp = split_w[:, at0:at0 + OFF2[5]]
        at0 += OFF2[5]
        nt_sb = split_w[:, at0:at0 + OFF2[5]]
        lng = sb("lng", [128, E])
        lnb = sb("lnb", [128, E])
        g64 = sb("g64", [128, E])
        b2f = zs[0:33, :, :].rearrange("p a n -> p (a n)")
        b2hi = bd[0:33, 0, :, :].rearrange("p k n -> p (k n)").bitcast(F16)
        ones64 = sb("ones64", [128, 128], F16)
        ident16 = sb("ident16", [128, 128], F16)
        epsc = sb("epsc", [128, 1])

        flat = pay[:, :, :].rearrange("p n r -> p (n r)")
        at = [0]

        def take(words, dt=F32):
            v = flat[:, at[0]:at[0] + words]
            at[0] += words
            return v if dt == F32 else v.bitcast(dt)

        prow = [take(ROW) for _ in range(RING)]
        orow = [take(D) for _ in range(RING)]
        at[0] += at[0] % 2
        xnt = [take(D) for _ in range(2)]
        xsplit = [take(D, F16) for _ in range(2)]
        xT = [take(D, F16) for _ in range(2)]
        hid = [take(H) for _ in range(4)]
        hh = [take(H // 2, F16) for _ in range(4)]
        hl = [take(H // 2, F16) for _ in range(4)]
        wbuf = [take(BLOCK // 2, F16) for _ in range(WRING)]
        assert at[0] <= N * ROW

        in_graph = [sem(f"in_graph{k}") for k in range(3)]
        in_adj = sem("in_adj")
        in_gw = sem("in_gw")
        in_chunk = [sem(f"in_chunk{c}") for c in range(NC - 1)]
        in_router = sem("in_router")
        in_experts = sem("in_experts")
        in_b2 = sem("in_b2")
        xg_out = sem("xg_out")
        nt_out = sem("nt_out")
        in_pack = [sem(f"in_pack{i}") for i in range(2)]
        go_out = [sem(f"go_out{i}") for i in range(2)]
        summed = sem("summed")
        adj_diag = sem("adj_diag")
        adj_copied = sem("adj_copied")
        wr_zero = sem("wr_zero")
        pads_out = sem("pads_out")
        consts = sem("consts")
        zeros = sem("zeros")
        vec = sem("vec")
        norm_ready = sem("norm_ready")
        xn_done = sem("xn_done")
        var_ready = sem("var_ready")
        root_ready = sem("root_ready")
        deg_ready = sem("deg_ready")
        nt_done = sem("nt_done")
        fmax_ready = sem("fmax_ready")
        fexp_ready = sem("fexp_ready")
        bd_ready = sem("bd_ready")
        z_ready = sem("z_ready")
        zs_ready = sem("zs_ready")
        h_ready = sem("h_ready")
        hs_ready = sem("hs_ready")
        s_ready = sem("s_ready")
        ss_ready = sem("ss_ready")
        o_ready = sem("o_ready")
        o_taken = sem("o_taken")
        gpost_ready = sem("gpost_ready")
        ln_ready = sem("ln_ready")
        y_ready = sem("y_ready")
        y_last = sem("y_last")
        yt_ready = sem("yt_ready")
        yT_ready = sem("yT_ready")
        logits_ready = sem("logits_ready")
        logits_taken = sem("logits_taken")
        gap_ready = sem("gap_ready")
        exp_ready = sem("exp_ready")
        hot_ready = sem("hot_ready")
        rank_ready = sem("rank_ready")
        rank_taken = sem("rank_taken")
        slots_ready = sem("slots_ready")
        rows_out = sem("rows_out")
        seen_ready = sem("seen_ready")
        w1_high = sem("w1_high")
        w2_high = sem("w2_high")
        b2_done = sem("b2_done")
        b2_cleared = sem("b2_cleared")
        mix_ready = sem("mix_ready")
        w1_ready = sem("w1_ready")
        w1_low = sem("w1_low")
        w2_low = sem("w2_low")
        cnt_ready = sem("cnt_ready")
        ntile_ready = sem("ntile_ready")
        tincl_ready = sem("tincl_ready")
        member_ready = sem("member_ready")
        trow_ready = sem("trow_ready")
        table_ready = sem("table_ready")
        in_tile = [sem(f"in_tile{i}") for i in range(RING)]
        out_tile = [sem(f"out_tile{i}") for i in range(RING)]
        xin_own = sem("xin_own")
        xin_ready = sem("xin_ready")
        xt_ready = sem("xt_ready")
        xT_taken = sem("xT_taken")
        w_copied = sem("w_copied")
        hid_ready = sem("hid_ready")
        gelu_ready = sem("gelu_ready")
        high_ready = sem("high_ready")
        split_ready = sem("split_ready")
        e_ready = sem("e_ready")
        half_ready = sem("half_ready")
        row_ready = sem("row_ready")
        row_seen = sem("row_seen")
        ident_ready = sem("ident_ready")

        def load_values(ap, engine, max_val):
            return nc.values_load_multi_w_load_instructions(
                ap, engines=[engine], min_val=0, max_val=max_val,
                skip_runtime_bounds_check_because="the counts that the entries are computed from bound them")[1]

        def load_one(ap, engine, max_val):
            return load_values(ap, engine, max_val)[0]

        def write_padding(engine, kind, first):
            engine.wait_ge(table_ready, 1)
            for r in load_values(padint[0:1, first:first + PAIRS // 2], kind, DUMMY * 128 - 128):
                engine.dma_start(pay_dram[bass.ds(r, 128), :], padding[:, :]).then_inc(pads_out, 16)

        block = ctx.enter_context(nc.Block())

        def w_bank(e):
            return bank[7] if e < EARLY else bank[e % 2]

        def by_pair(t, count):
            return t[:, 0:PAIRS * count].rearrange("p (a n) -> p a n", n=count)

        def square(g, t=acomp):
            return t[:, OFF2[g]:OFF2[g + 1]].rearrange("p (i j) -> p i j", j=SIZE[g])

        def x_bank(s):
            return bank[s % 2][:, 0:D].bitcast(F16)

        @block.sync
        def _(sp):
            for k, (a, b) in enumerate(((0, 9), (9, 17), (17, NG))):
                sp.dma_start(pay[:, a:b, 0:D], x[:, a:b, :]).then_inc(in_graph[k], 16)
                if a == 0:
                    sp.dma_start(adjs[:, :].rearrange("p (i j) -> p i j", j=NG), adj[:, 0:NG, 0:NG]).then_inc(in_adj, 16)
            c0, n0 = CHUNKS[0]
            sp.dma_start(pay[:, c0:c0 + n0, 0:D], x[:, c0:c0 + n0, :]).then_inc(in_chunk[0], 16)
            sp.wait_ge(wr_zero, 1)
            sp.dma_start(wr[:, 0:E], Wr).then_inc(in_router, 16)
            sp.dma_start(brb[:, :], br.rearrange("(o e) -> o e", o=1).to_broadcast([128, E])).then_inc(in_router, 16)
            sp.dma_start(gw1[:, :, :], gW1.rearrange("g d h -> d g h")).then_inc(in_gw, 16)
            sp.dma_start(gw2[:, :, :, :], gW2.rearrange("g (c p) d -> p g c d", c=2)).then_inc(in_gw, 16)
            with nc.allow_non_contiguous_dma(reason="small bias columns"):
                sp.dma_start(gb1s[:, :, :], gb1.rearrange("g (c p) -> p g c", c=2)).then_inc(in_gw, 16)
            sp.dma_start(wb2[:, :, :].rearrange("p g d -> p (g d)"),
                         gb2.rearrange("(o g) d -> o (g d)", o=1).to_broadcast([128, 5 * D])).then_inc(in_gw, 16)
            sp.dma_start(fus[:, :], fusion.rearrange("(o g) -> o g", o=1).to_broadcast([128, 5])).then_inc(in_gw, 16)

            def write_group(g):
                to = 0
                for first, count in GROUPS[g]:
                    sp.dma_start(xg_dram[g][:, to * D:(to + count) * D],
                                 xn[:, first:first + count, :].rearrange("p i d -> p (i d)")).then_inc(xg_out, 16)
                    to += count
                if g == 0:
                    sp.wait_ge(nt_done, 1)
                sp.dma_start(nt_dram[g], nt_sb[:, OFF2[g]:OFF2[g + 1]]).then_inc(nt_out, 16)

            def load_pack(i):
                g, q = QUADS[i]
                p = ROWS[g]
                if i >= 2:
                    sp.wait_ge(z_ready, i - 1)
                    sp.wait_ge(bd_ready, i - 1)
                rows = xg_dram[g].rearrange("b (i d) -> (b i) d", d=D)[q * 4 * p:(q + 1) * 4 * p, :]
                sp.dma_start(xpack[0:p, i % 2, :, :], rows.rearrange("(k p) d -> p k d", k=4)).then_inc(in_pack[i % 2], 16)
                rows = nt_dram[g].rearrange("b (m n) -> (b m) n", n=SIZE[g])[q * 4 * p:(q + 1) * 4 * p, :]
                sp.dma_start(npack[0:p, i % 2, :, 0:SIZE[g]], rows.rearrange("(k p) n -> p k n", k=4))\
                    .then_inc(in_pack[i % 2], 16)

            sp.wait_ge(xn_done, 2)
            write_group(0)
            sp.wait_ge(xg_out, 16)
            sp.wait_ge(nt_out, 16)
            load_pack(0)
            load_pack(1)
            for g in range(1, 5):
                write_group(g)
            for c in (1, 2):
                c0, n = CHUNKS[c]
                sp.dma_start(pay[:, c0:c0 + n, 0:D], x[:, c0:c0 + n, :]).then_inc(in_chunk[c], 16)
            sp.dma_start(pay[:, NG:CH, 0:D], x[:, NG:CH, :]).then_inc(in_chunk[3], 16)
            sp.wait_ge(xg_out, 16 * sum(len(r) for r in GROUPS))
            sp.wait_ge(nt_out, 16 * 5)
            done = 0
            for i, (g, q) in enumerate(QUADS):
                p = ROWS[g]
                if i + 2 < NQ:
                    load_pack(i + 2)
                if i == 2:
                    sp.dma_start(w1f, W1.rearrange("e d h -> d e h")).then_inc(in_experts, 16)
                if 3 <= i < 3 + HC:
                    c = i - 3
                    sp.dma_start(w2f[:, :, c, :], W2[:, c * 128:(c + 1) * 128, :].rearrange("e p d -> p e d"))\
                        .then_inc(in_experts, 16)
                if i == 3 + HC:
                    with nc.allow_non_contiguous_dma(reason="small columns of scales and biases"):
                        sp.dma_start(lng[:, :], ln_g.rearrange("e d -> d e")).then_inc(in_experts, 16)
                        sp.dma_start(lnb[:, :], ln_b.rearrange("e d -> d e")).then_inc(in_experts, 16)
                    sp.dma_start(b1f, b1).then_inc(in_experts, 16)
                sp.wait_ge(gpost_ready, i + 1)
                rows = go_dram[g].rearrange("b (i d) -> (b i) d", d=D)[q * 4 * p:(q + 1) * 4 * p, :]
                sp.dma_start(rows.rearrange("(k p) d -> p k d", k=4), gpost[0:p, i % 2, :, :])\
                    .then_inc(go_out[i % 2], 16)
            sp.wait_ge(o_ready, NQ)
            for r in (0, 32):
                sp.dma_start(b2f[r:r + 1, :], b2.rearrange("(o e) d -> o (e d)", o=1)).then_inc(in_b2, 16)
            sp.wait_ge(consts, 1)
            sp.dma_start(pay_dram[DUMMY * 128:(DUMMY + 1) * 128, :], padding[:, :]).then_inc(pads_out, 16)
            write_padding(sp, mybir.EngineType.SP, 0)
            sp.wait_ge(pads_out, 16 * (PAIRS + 1))
            sp.wait_ge(rows_out, 16 * N)

            def load_tile(t, s, round_):
                r = load_one(place_of[0:1, bass.ds(t, 1)], mybir.EngineType.SP, DUMMY)
                r = sp.snap(r * 128)
                if round_ is not None:
                    sp.wait_ge(out_tile[s], round_ * 16)
                sp.dma_start(prow[s], pay_dram[bass.ds(r, 128), :]).then_inc(in_tile[s], 16)

            for t in range(RING):
                load_tile(t, t, None)
            with sp.Fori(1, TILES // RING) as i:
                for s in range(RING):
                    load_tile(i * RING + s, s, i)
            for t in range(TILES, TABLE):
                load_tile(t, t - TILES, TILES // RING)
            for s in range(RING):
                sp.wait_ge(out_tile[s], TILES // RING * 16)

        @block.gpsimd
        def _(pool):
            nc.gpsimd.memset(wr[:, :], 0.0).then_inc(wr_zero, 1)
            nc.gpsimd.memset(padding[:, :], 0.0).then_inc(zeros, 1)
            nc.gpsimd.memset(ones16[:, :], 1.0).then_inc(zeros, 1)
            nc.gpsimd.memset(ident[:, :], 0.0).then_inc(zeros, 1)
            nc.gpsimd.memset(below[:, :], 0.0).then_inc(zeros, 1)
            nc.gpsimd.memset(tri[:, :], 1.0).then_inc(zeros, 1)
            for g in range(4):
                nc.gpsimd.memset(mask[g][:, :], 1.0).then_inc(zeros, 1)
            nc.gpsimd.memset(epsc[:, :], EPS).then_inc(zeros, 1)
            nc.gpsimd.memset(ones64[:, :], S64).then_inc(zeros, 1)
            nc.gpsimd.memset(pick64, 0.0).then_inc(zeros, 1)
            nc.gpsimd.memset(seen[:, 0, :], 0.0).then_inc(zeros, 1)
            for n in restart:
                nc.gpsimd.memset(restart[n][:, :], 1.0).then_inc(zeros, 1)
            pool.wait_ge(zeros, 15)
            for n in restart:
                nc.gpsimd.memset(restart[n][:, ::n], 0.0)
            nc.gpsimd.iota(padding[:, TOKEN:TOKEN + 1].bitcast(I32), pattern=[[0, 1]], base=NOWHERE, channel_multiplier=0)
            nc.gpsimd.affine_select(out=ident[:, :], in_=ident[:, :], compare_op=ALU.not_equal, fill=1.0, base=0,
                                    pattern=[[-1, 128]], channel_multiplier=1)
            nc.gpsimd.affine_select(out=below[:, :], in_=below[:, :], compare_op=ALU.is_gt, fill=-1.0, base=0,
                                    pattern=[[1, 128]], channel_multiplier=-1)
            nc.gpsimd.affine_select(out=tri[:, :], in_=tri[:, :], compare_op=ALU.is_ge, fill=0.0, base=0,
                                    pattern=[[1, PAIRS]], channel_multiplier=-1)
            for g in range(4):
                nc.gpsimd.affine_select(out=mask[g][:, :], in_=mask[g][:, :], compare_op=ALU.is_ge, fill=0.0,
                                        base=0, pattern=[[-SIZE[g], BATCHES[g]]], channel_multiplier=1).then_inc(zeros, 1)
            pool.wait_ge(zeros, 19)
            for g in range(4):
                nc.gpsimd.affine_select(out=mask[g][:, :], in_=mask[g][:, :], compare_op=ALU.is_ge, fill=0.0,
                                        base=SIZE[g] - 1, pattern=[[SIZE[g], BATCHES[g]]], channel_multiplier=-1)
            nc.gpsimd.iota(pay[:, :, TOKEN:TOKEN + 1].bitcast(I32), pattern=[[1, N], [0, 1]], base=0, channel_multiplier=N)
            for dst, pattern, base, mult in (
                (rev[:, :], [[-1, E]], E, 0), (pairs[:, :], [[1, PAIRS]], 0, 0),
                (tline[:, :], [[1, TABLE]], 0, 0), (vrow[:, 2, :], [[REGION, PAIRS]], -2 * DUMMY, 0),
                (padrow[:, 0, :], [[REGION * 128, PAIRS]], 0, 0),
            ):
                nc.gpsimd.iota(dst, pattern=pattern, base=base, channel_multiplier=mult,
                               allow_small_or_imprecise_dtypes=True)
            first = 0
            for a in range(E - 1):
                k = E - 1 - a
                nc.gpsimd.memset(vrow[:, 0, first:first + k], float(a))
                nc.gpsimd.iota(vrow[:, 1, first:first + k], pattern=[[1, k]], base=a + 1, channel_multiplier=0,
                               allow_small_or_imprecise_dtypes=True)
                first += k
            nc.gpsimd.memset(one[:, :], 1.0).then_inc(consts, 1)
            pool.wait_ge(in_adj, 16)
            nc.gpsimd.tensor_scalar(adjs[:, 0:NG * NG:NG + 1], adjs[:, 0:NG * NG:NG + 1], 1.0, None, ALU.add)\
                .then_inc(adj_diag, 1)
            pool.wait_ge(adj_diag, 1)
            whole = adjs[:, :].rearrange("p (i j) -> p i j", j=NG)
            for g in range(5):
                row = 0
                for i0, ni in GROUPS[g]:
                    col = 0
                    for j0, nj in GROUPS[g]:
                        last = nc.gpsimd.tensor_copy(square(g)[:, row:row + ni, col:col + nj],
                                                     whole[:, i0:i0 + ni, j0:j0 + nj])
                        col += nj
                    row += ni
            last.then_inc(adj_copied, 1)
            def scatter_nodes(first, count):
                for n in range(first, first + count):
                    nc.gpsimd.indirect_dma_start(
                        out=pay_dram, out_offset=bass.IndirectOffsetOnAxis(ap=slot[:, n:n + 1], axis=0),
                        in_=pay[:, n, :], in_offset=None).then_inc(rows_out, 16)

            def sum_group(g):
                last = max(i for i in range(NQ) if QUADS[i][0] == g)
                for k in range(2):
                    pool.wait_ge(go_out[k], 16 * ((last + 2 - k) // 2))
                if g >= 1:
                    pool.wait_ge(summed, 16 * sum(len(r) for r in GROUPS[:g]))
                to = 0
                for first, count in GROUPS[g]:
                    pool.dma_start(pay[:, first:first + count, 0:D],
                                   go_dram[g].rearrange("b (i d) -> b i d", d=D)[:, to:to + count, :],
                                   accum_op=ALU.add).then_inc(summed, 16)
                    to += count

            for c in range(NC):
                if c == 3:
                    sum_group(3)
                    sum_group(4)
                pool.wait_ge(slots_ready, c + 1)
                scatter_nodes(*CHUNKS[c])
                if c < 3:
                    sum_group(c)

            last_token = pool.to_reg(B * N - 1)

            def prepare(t, s, i, n):
                pool.wait_ge(in_tile[s % RING], 16 * (i + 1 + s // RING))
                pool.sem_inc(row_seen, 1)
                if n is not None:
                    pool.wait_ge(xt_ready, n)
                    pool.sem_inc(row_seen, 1)
                nc.gpsimd.tensor_scalar(xnt[s % 2][:, 1:D], prow[s % RING][:, 1:D], prow[s % RING][:, RSTD:RSTD + 1],
                                        prow[s % RING][:, NBIAS:NBIAS + 1], ALU.mult, ALU.add).then_inc(xin_own, 1)
                own = 2 * t + 1
                pool.wait_ge(xin_own, own)
                pool.sem_inc(row_seen, 1)
                nc.gpsimd.tensor_copy(xsplit[s % 2][:, 0:D], xnt[s % 2]).then_inc(xin_own, 1)
                pool.wait_ge(xin_own, own + 1)
                nc.gpsimd.tensor_tensor(xsplit[s % 2][:, D:2 * D], xnt[s % 2], xsplit[s % 2][:, 0:D], ALU.subtract)\
                    .then_inc(xin_ready, 1)

            def scatter(s, n):
                pool.wait_ge(row_ready, n)
                pool.sem_inc(row_seen, 1)
                nc.gpsimd.indirect_dma_start(
                    out=out_rows, out_offset=bass.IndirectOffsetOnAxis(ap=prow[s][:, TOKEN:TOKEN + 1].bitcast(I32), axis=0),
                    in_=orow[s], in_offset=None, bounds_check=last_token, oob_is_err=False).then_inc(out_tile[s], 16)

            pool.sem_inc(row_ready, 2 * 4)
            pool.wait_ge(rows_out, 16 * N)
            for k in range(2):
                nc.gpsimd.memset(xnt[k][:, 0:1], S64).then_inc(zeros, 1)
            pool.wait_ge(zeros, 21)
            for t in range(AHEAD):
                prepare(t, t, 0, None)
            for t in range(RING):
                prepare(t + AHEAD, t + AHEAD, 0, t + 1)
                if t >= 4:
                    scatter(t - 4, 2 * t + 1)
            with pool.Fori(1, TILES // RING) as i:
                for s in range(RING):
                    t = i * RING + s
                    prepare(t + AHEAD, s + AHEAD, i, t + 1)
                    scatter((s - 4) % RING, 2 * t + 1)
            for t in range(TILES, TILES + 4):
                scatter((t - 4) % RING, 2 * t + 1)

        @block.scalar
        def _(act):
            act.wait_ge(consts, 1)
            act.wait_ge(var_ready, 1)
            nc.scalar.activation(ln[:, 0, 1, 0:NG], ln[:, 0, 0, 0:NG], ACT.Sqrt, bias=epsc[:, :]).then_inc(root_ready, 1)
            act.wait_ge(norm_ready, 1)
            for j in range(NG // 2, NG):
                last = nc.scalar.activation(xn[:, j, :], pay[:, j, 0:D], ACT.Identity, bias=ln[:, 0, 5, j:j + 1],
                                            scale=ln[:, 0, 2, j:j + 1])
            last.then_inc(xn_done, 1)
            act.wait_ge(deg_ready, 1)
            nc.scalar.activation(deg[:, 3, :], deg[:, 2, :], ACT.Sqrt).then_inc(root_ready, 1)

            def root1(c):
                act.wait_ge(var_ready, 2 + 2 * c)
                r = (c + 1) % 2
                nc.scalar.activation(ln[:, r, 1, :], ln[:, r, 0, :], ACT.Sqrt, bias=epsc[:, :]).then_inc(root_ready, 1)

            def root2(c):
                act.wait_ge(var_ready, 3 + 2 * c)
                r = (c + 1) % 2
                nc.scalar.activation(ln[:, r, 4, :], ln[:, r, 3, :], ACT.Sqrt, bias=epsc[:, :]).then_inc(root_ready, 1)

            def normalise(k):
                c, j = FOURS[k]
                act.wait_ge(ln_ready, c + 1)
                if k >= 2:
                    act.wait_ge(yt_ready, k - 1)
                for n in range(4):
                    m = 4 * j + n
                    last = nc.scalar.activation(y[:, k % 2, n, :], pay[:, CHUNKS[c][0] + m, 0:D], ACT.Identity,
                                                bias=ln[:, (c + 1) % 2, 5, m:m + 1], scale=ln[:, (c + 1) % 2, 2, m:m + 1])
                last.then_inc(y_ready, 1)

            def take_yT(k):
                act.wait_ge(yt_ready, k + 1)
                if k >= 2:
                    act.wait_ge(logits_ready, k - 1)
                nc.scalar.activation(yT[:, k % 2, :], bank[5 + k % 2][:, :], ACT.Copy).then_inc(yT_ready, 1)

            def two_fours(k, following):
                take_yT(k)
                take_yT(k + 1)
                if following is not None:
                    normalise(following)
                    normalise(following + 1)

            def gap_exp(c):
                act.wait_ge(gap_ready, c + 1)
                nc.scalar.activation(small[:, 6, :], small[:, 5, :], ACT.Exp).then_inc(exp_ready, 1)

            act.wait_ge(fmax_ready, 1)
            nc.scalar.activation(fus[:, :], fus[:, :], ACT.Exp, bias=fstat[:, 0:1], accum_out=fstat[:, 1:2])\
                .then_inc(fexp_ready, 1)
            root1(0)
            root2(0)
            normalise(0)
            normalise(1)

            def relu_h(i):
                g, q = QUADS[i]
                p4 = 4 * ROWS[g]
                act.wait_ge(h_ready, i + 1)
                if i >= 2:
                    act.wait_ge(s_ready, i - 1)
                for c in range(2):
                    last = nc.scalar.activation(hs[:, i % 2, c, 0:p4], bank[1 + c][:, 0:p4], ACT.Relu,
                                                bias=gb1s[:, g, c:c + 1])
                last.then_inc(hs_ready, 1)

            def post(i):
                g, q = QUADS[i]
                p = ROWS[g]
                act.wait_ge(o_taken, i + 1)
                nc.scalar.activation(gpost[0:p, i % 2, :, :], gpost[0:p, i % 2, :, :], ACT.Relu).then_inc(gpost_ready, 1)

            def high1(e):
                act.wait_ge(w1_ready, e + 1)
                nc.scalar.activation(w1s[:, e, 0, :], w_bank(e)[:, :], ACT.Copy).then_inc(w1_high, 1)

            def high2(e):
                nc.scalar.activation(w2s[:, e, :, 0, :], w2f[:, e, :, :], ACT.Copy, scale=S64).then_inc(w2_high, 1)

            act.wait_ge(in_gw, 16 * 5)
            relu_h(0)
            for i in range(NQ):
                begins = i > 0 and FOURS_AT.get(i, (None,))[0] in FIRST4
                if begins and i + 1 < NQ:
                    relu_h(i + 1)
                for k in FOURS_AT.get(i, ()):
                    two_fours(k, k + 2 if k + 2 not in FIRST4 else None)
                if not begins and i + 1 < NQ:
                    relu_h(i + 1)
                if i in STATS_AT and STATS_AT[i] in ((1, 1), (2, 1), (3, 0)):
                    root1(STATS_AT[i][0])
                post(i)
                if i in FACTORS_AT:
                    root2(FACTORS_AT[i])
                if i in PAIR_AT:
                    gap_exp(PAIR_AT[i])
                for k in FOURS_AT.get(i + 1, ()):
                    if k in FIRST4:
                        normalise(k)
                        normalise(k + 1)
                if i >= SECOND_AT and i < SECOND_AT + E - 1:
                    if i == SECOND_AT:
                        act.wait_ge(in_experts, 16 * (1 + HC + 3))
                    high2(i - SECOND_AT)
                if i >= FIRST_AT:
                    high1(i - FIRST_AT)
            for e in range(EARLY, EARLY + 2):
                high1(e)
            root1(NC - 1)
            root2(NC - 1)
            two_fours(FIRST4[NC - 1], None)
            two_fours(FIRST4[NC - 1] + 2, None)
            for e in range(EARLY + 2, EARLY + 4):
                high1(e)
            gap_exp(NC - 1)
            write_padding(act, mybir.EngineType.Activation, PAIRS // 2)
            for e in range(EARLY + 4, E):
                high1(e)
            high2(E - 1)

            def take_x(s, n):
                act.wait_ge(xt_ready, n)
                nc.scalar.activation(xT[s % 2], x_bank(s), ACT.Copy).then_inc(xT_taken, 2)

            def gelu(v, n):
                act.wait_ge(hid_ready, n)
                act.wait_ge(split_ready, n)
                nc.scalar.activation(hid[v % 4], bank[2 + v % 4][:, :], ACT.Gelu, scale=1.0 / S4096).then_inc(gelu_ready, 1)

            def high(v, n):
                act.wait_ge(gelu_ready, n)
                act.wait_ge(e_ready, n)
                nc.scalar.activation(hh[v % 4], hid[v % 4], ACT.Copy, scale=S64).then_inc(high_ready, 1)

            act.sem_inc(gelu_ready, 1)
            act.sem_inc(high_ready, 2)
            act.wait_ge(rows_out, 16 * N)
            take_x(0, 1)
            for u in range(UNITS):
                gelu(u, u + 1)
                if u >= 1:
                    high(u - 1, u + 1)
                if u % 2 == 0:
                    take_x(u // 2 + 1, u // 2 + 2)
            with act.Fori(1, TILES // RING) as i:
                for v in range(UNITS):
                    n = act.snap(i * UNITS + (v + 1))
                    gelu(v, n)
                    high(v - 1, n)
                    if v % 2 == 0:
                        take_x(v // 2 + 1, i * RING + (v // 2 + 2))
            high(2 * TILES - 1, 2 * TILES + 1)

        @block.tensor
        def _(pe):
            pe.wait_ge(consts, 1)
            pe.wait_ge(in_router, 32)

            def transposes(k):
                c, j = FOURS[k]
                if c < NC - 1:
                    pe.wait_ge(y_ready, k + 1)
                else:
                    pe.wait_ge(y_last, j + 1)
                if k >= 2:
                    pe.wait_ge(yT_ready, k - 1)
                for n in range(4):
                    last = nc.tensor.transpose(bank[5 + k % 2][:, n * 128:(n + 1) * 128], y[:, k % 2, n, :], ident[:, :])
                last.then_inc(yt_ready, 1)

            def logits(k):
                c, j = FOURS[k]
                pe.wait_ge(yT_ready, k + 1)
                if j == 0 and c >= 1:
                    pe.wait_ge(logits_taken, c)
                for n in range(4):
                    col = (4 * j + n) * E
                    last = nc.tensor.matmul(bank[7][:, col:col + LOGW], yT[:, k % 2, n * 128:(n + 1) * 128], wr[:, :],
                                            start=True, stop=True)
                last.then_inc(logits_ready, 1)

            def two_fours(k):
                transposes(k)
                transposes(k + 1)
                logits(k)
                logits(k + 1)

            def ranks(c):
                pe.wait_ge(hot_ready, c + 1)
                half, n = PAIRS // 2, CHUNKS[c][1]
                for b in range(2):
                    s = slice(b * half, (b + 1) * half)
                    o = bank[5 + b][:, 0:half * n].rearrange("p (a n) -> p a n", n=n)
                    nc.tensor.matmul(o, below[:, :], by_pair(onehot, n)[:, s, :], start=True, stop=False)
                    nc.tensor.matmul(o, ones16[:, :], by_pair(running, n)[:, s, :], start=False, stop=False)
                    last = nc.tensor.matmul(o, ones16[:, :],
                                            seen[:, c, s].rearrange("p (a o) -> p a o", o=1).to_broadcast([128, half, n]),
                                            start=False, stop=True)
                last.then_inc(rank_ready, 1)

            def z(i):
                g, q = QUADS[i]
                p = ROWS[g]
                pe.wait_ge(bd_ready, i + 1)
                if i >= 1:
                    pe.wait_ge(zs_ready, i)
                for k in range(4):
                    last = nc.tensor.matmul(bank[0][:, k * p:(k + 1) * p], xpack[0:p, i % 2, k, :], bd[0:p, i % 3, k, 0:p],
                                            start=True, stop=True)
                last.then_inc(z_ready, 1)

            def h(i):
                g, q = QUADS[i]
                p4 = 4 * ROWS[g]
                pe.wait_ge(zs_ready, i + 1)
                if i >= 1:
                    pe.wait_ge(hs_ready, i)
                for c in range(2):
                    last = nc.tensor.matmul(bank[1 + c][:, 0:p4], gw1[:, g, c * 128:(c + 1) * 128], zs[:, i % 2, 0:p4],
                                            start=True, stop=True)
                last.then_inc(h_ready, 1)

            def s_(i):
                g, q = QUADS[i]
                p = ROWS[g]
                pe.wait_ge(hs_ready, i + 1)
                if i >= 1:
                    pe.wait_ge(ss_ready, i)
                for k in range(4):
                    for c in range(2):
                        last = nc.tensor.matmul(bank[3][0:p, k * D:(k + 1) * D], hs[:, i % 2, c, k * p:(k + 1) * p],
                                                gw2[:, g, c, :], start=(c == 0), stop=(c == 1))
                last.then_inc(s_ready, 1)

            def o(i):
                g, q = QUADS[i]
                p = ROWS[g]
                pe.wait_ge(ss_ready, i + 1)
                if i >= 1:
                    pe.wait_ge(o_taken, i)
                for k in range(4):
                    last = nc.tensor.matmul(bank[4][0:p, k * D:(k + 1) * D], bd[0:p, i % 3, k, 0:p], ss[0:p, i % 2, k, :],
                                            start=True, stop=True)
                last.then_inc(o_ready, 1)

            def mix_first(e):
                if e == 0:
                    pe.wait_ge(in_experts, 16 * (1 + HC + 3))
                    pe.wait_ge(logits_taken, NC - 1)
                elif e < EARLY:
                    pe.wait_ge(w1_low, e)
                elif e >= EARLY + 2:
                    pe.wait_ge(w1_low, e - 1)
                pe.wait_ge(mix_ready, e + 1)
                nc.tensor.matmul(w_bank(e)[:, :], mix[:, e % 2, :], w1f[:, e, :], start=True, stop=False)
                nc.tensor.matmul(w_bank(e)[:, :], pick64[:, e % 2, :], b1f, start=False, stop=True).then_inc(w1_ready, 1)

            pe.wait_ge(in_gw, 16 * 5)
            z(0)
            h(0)
            z(1)
            for i in range(NQ):
                s_(i)
                if i - 2 in PLACE_AT or i - 1 in PLACE_AT:
                    pe.wait_ge(rank_taken, PLACE_AT.get(i - 1, PLACE_AT.get(i - 2)) + 1)
                begins = i > 0 and FOURS_AT.get(i, (None,))[0] in FIRST4
                if not begins:
                    for k in FOURS_AT.get(i, ()):
                        two_fours(k)
                if i in PLACE_AT:
                    ranks(PLACE_AT[i])
                if i >= FIRST_AT:
                    mix_first(i - FIRST_AT)
                if i + 1 < NQ:
                    h(i + 1)
                o(i)
                if begins:
                    two_fours(FOURS_AT[i][0])
                if i + 2 < NQ:
                    z(i + 2)
            for e in range(EARLY, EARLY + 2):
                mix_first(e)
            pe.wait_ge(w1_low, EARLY)
            pe.wait_ge(rank_taken, NC - 1)
            for k in range(FIRST4[NC - 1], FIRST4[NC], 2):
                two_fours(k)
            for e in range(EARLY + 2, EARLY + 4):
                mix_first(e)
            ranks(NC - 1)
            pe.wait_ge(seen_ready, NC)
            nc.tensor.matmul(bank[7][0:PAIRS, 0:1], seen[:, NC, :], ones16[:, 0:1], start=True, stop=True)
            nc.tensor.matmul(bank[2][0:1, 0:PAIRS], ones16[:, 0:1], seen[:, NC, :], start=True, stop=True).then_inc(cnt_ready, 1)
            pe.wait_ge(ntile_ready, 1)
            nc.tensor.matmul(bank[3][0:PAIRS, 0:1], tri[:, :], tcnt[:, 1:2], start=True, stop=True)
            for k in range(3):
                last = nc.tensor.matmul(bank[3][0:PAIRS, 1 + k:2 + k], vrow[:, k, :], one[:, :], start=True, stop=True)
            last.then_inc(tincl_ready, 1)
            pe.wait_ge(member_ready, 1)
            for k in range(3):
                last = nc.tensor.matmul(bank[4][0:1, k * TABLE:(k + 1) * TABLE], tcnt[:, 4 + k:5 + k], inpair[:, :],
                                        start=True, stop=True)
            last.then_inc(trow_ready, 1)
            for e in range(EARLY + 4, E):
                mix_first(e)

            def turn(s, n):
                pe.wait_ge(xin_ready, n)
                for part in range(2):
                    last = nc.tensor.transpose(x_bank(s)[:, part * D:(part + 1) * D],
                                               xsplit[s % 2][:, part * D:(part + 1) * D], ident16[:, :])
                last.then_inc(xt_ready, 1)

            def first_layer(v, n):
                if v % 2 == 0:
                    pe.wait_ge(xT_taken, n)
                pe.wait_ge(w_copied, n)
                w, x2 = wbuf[v % WRING], xT[v // 2 % 2]
                for c in range(HC):
                    o = bank[2 + v % 4][:, c * 128:(c + 1) * 128]
                    wh, wl = (w[:, part * H + c * 128:part * H + (c + 1) * 128] for part in range(2))
                    nc.tensor.matmul(o, wh, x2[:, 0:D], start=True, stop=False)
                    nc.tensor.matmul(o, wh, x2[:, D:2 * D], start=False, stop=False)
                    last = nc.tensor.matmul(o, wl, x2[:, 0:D], start=False, stop=True)
                last.then_inc(hid_ready, 1)

            def second_layer(v, n):
                if v % 2 == 0:
                    pe.wait_ge(row_ready, n)
                w = wbuf[v % WRING][:, 2 * H:BLOCK]
                o = bank[6 + v // 2 % 2][:, v % 2 * D:(v % 2 + 1) * D]
                nc.tensor.matmul(o, ones64[:, :], w[:, 2 * H:2 * H + D], start=True, stop=False)
                for c in range(HC):
                    wh, wl = (w[:, (2 * c + part) * D:(2 * c + part + 1) * D] for part in range(2))
                    a, b = hh[v % 4][:, c * 128:(c + 1) * 128], hl[v % 4][:, c * 128:(c + 1) * 128]
                    nc.tensor.matmul(o, a, wh, start=False, stop=False)
                    nc.tensor.matmul(o, a, wl, start=False, stop=False)
                    last = nc.tensor.matmul(o, b, wh, start=False, stop=(c == HC - 1))
                last.then_inc(e_ready, 1)

            pe.sem_inc(e_ready, 5)
            pe.wait_ge(rows_out, 16 * N)
            pe.wait_ge(ident_ready, 1)
            pe.wait_ge(b2_done, 1)
            turn(0, 1)
            for u in range(UNITS):
                if u % 2 == 0:
                    turn(u // 2 + 1, u // 2 + 2)
                pe.wait_ge(split_ready, u + 1)
                first_layer(u, u + 1)
                if u >= 2 * BACK:
                    second_layer(u - 2 * BACK, u + 1)
            with pe.Fori(1, TILES // RING) as i:
                for v in range(UNITS):
                    n = pe.snap(i * UNITS + (v + 1))
                    if v % 2 == 0:
                        turn(v // 2 + 1, i * RING + (v // 2 + 2))
                    pe.wait_ge(split_ready, n)
                    first_layer(v, n)
                    second_layer(v - 2 * BACK, n)
            for u in range(2 * TILES, 2 * TILES + 2 * BACK):
                pe.wait_ge(split_ready, u + 1)
                second_layer(u - 2 * BACK, u + 1)

        @block.vector
        def _(dve):
            own = [0]
            V = nc.vector

            def link(ins):
                own[0] += 1
                ins.then_inc(vec, 1)
                dve.wait_ge(vec, own[0])

            def moments(count, r):
                me, mo, qe, qo = (stat[:, 0:count, k] for k in (1, 4, 2, 5))
                V.tensor_tensor(mom[:, 0, 0:count], me, mo, ALU.subtract)
                V.tensor_tensor(mom[:, 1, 0:count], me, mo, ALU.add)
                link(V.tensor_tensor(mom[:, 2, 0:count], qe, qo, ALU.add))
                link(V.scalar_tensor_tensor(out=mom[:, 3, 0:count], in0=mom[:, 0, 0:count], scalar=D / 4.0,
                                            in1=mom[:, 0, 0:count], op0=ALU.mult, op1=ALU.mult))
                link(V.tensor_tensor(mom[:, 4, 0:count], mom[:, 2, 0:count], mom[:, 3, 0:count], ALU.add))
                V.tensor_scalar(ln[:, r, 0, 0:count], mom[:, 4, 0:count], 1.0 / D, None, ALU.mult).then_inc(var_ready, 1)

            for j in range(NG):
                if j in (0, 9, 17):
                    dve.wait_ge(in_graph[j // 8], 16)
                last = V.bn_stats(stat[:, j, :], pay[:, j, 0:D])
            link(last)
            moments(NG, 0)
            dve.wait_ge(root_ready, 1)
            link(V.reciprocal(ln[:, 0, 2, 0:NG], ln[:, 0, 1, 0:NG]))
            V.scalar_tensor_tensor(out=ln[:, 0, 5, 0:NG], in0=mom[:, 1, 0:NG], scalar=-0.5, in1=ln[:, 0, 2, 0:NG],
                                   op0=ALU.mult, op1=ALU.mult).then_inc(norm_ready, 1)
            dve.wait_ge(norm_ready, 1)
            for j in range(NG // 2):
                last = V.tensor_scalar(xn[:, j, :], pay[:, j, 0:D], ln[:, 0, 2, j:j + 1], ln[:, 0, 5, j:j + 1],
                                       ALU.mult, ALU.add)
            last.then_inc(xn_done, 1)
            dve.wait_ge(consts, 1)
            V.tensor_copy(ident16[:, :], ident[:, :]).then_inc(ident_ready, 1)
            dve.wait_ge(adj_copied, 1)
            for g in range(5):
                last = V.tensor_reduce(deg[:, 0, OFF[g]:OFF[g + 1]], square(g), AX_X, ALU.add)
            link(last)
            link(V.tensor_scalar(deg[:, 1, :], deg[:, 0, :], 0.0, None, ALU.is_equal))
            V.tensor_tensor(deg[:, 2, :], deg[:, 0, :], deg[:, 1, :], ALU.add).then_inc(deg_ready, 1)
            link(V.tensor_scalar(deg[:, 4, :], deg[:, 1, :], -1.0, 1.0, ALU.mult, ALU.add))
            dve.wait_ge(root_ready, 2)
            link(V.reciprocal(deg[:, 5, :], deg[:, 3, :]))
            link(V.tensor_tensor(deg[:, 3, :], deg[:, 5, :], deg[:, 4, :], ALU.mult))
            for g in range(5):
                s = SIZE[g]
                inv = deg[:, 3, OFF[g]:OFF[g + 1]].rearrange("p (o n) -> p o n", o=1).to_broadcast([128, s, s])
                last = V.tensor_tensor(square(g, nt_sb), square(g).rearrange("p n m -> p m n"), inv, ALU.mult)
            link(last)
            for g in range(5):
                s = SIZE[g]
                inv = deg[:, 3, OFF[g]:OFF[g + 1]].rearrange("p (m o) -> p m o", o=1).to_broadcast([128, s, s])
                last = V.tensor_tensor(square(g, nt_sb), square(g, nt_sb), inv, ALU.mult)
            last.then_inc(nt_done, 1)

            def stats(c, part):
                first, count = CHUNKS[c]
                if part == 0 and c < NC - 1:
                    dve.wait_ge(in_chunk[c], 16)
                if c >= 3:
                    dve.wait_ge(summed, 16 * sum(len(r) for r in (GROUPS if c == NC - 1 else GROUPS[:1])))
                for j in range(16 * part, 16 * part + 16):
                    last = V.bn_stats(stat[:, j, :], pay[:, first + j, 0:D])
                if 16 * part + 16 == count:
                    link(last)
                    if c >= 2:
                        dve.wait_ge(y_ready, FIRST4[c - 1])
                    moments(count, (c + 1) % 2)

            def factors(c):
                r, m = (c + 1) % 2, slice(0, CHUNKS[c][1])
                dve.wait_ge(root_ready, 3 + 2 * c)
                link(V.reciprocal(ln[:, r, 2, m], ln[:, r, 1, m]))
                link(V.tensor_tensor(mom[:, 2, m], ln[:, r, 0, m], ln[:, r, 2, m], ALU.mult))
                V.tensor_tensor(ln[:, r, 3, m], mom[:, 2, m], ln[:, r, 2, m], ALU.mult).then_inc(var_ready, 1)
                V.tensor_scalar(mom[:, 3, m], mom[:, 1, m], -0.5, None, ALU.mult)
                V.scalar_tensor_tensor(out=ln[:, r, 5, m], in0=mom[:, 1, m], scalar=-0.5, in1=ln[:, r, 2, m],
                                       op0=ALU.mult, op1=ALU.mult).then_inc(ln_ready, 1)

            def normalise_last(j):
                r, (first, _), k = NC % 2, CHUNKS[NC - 1], FIRST4[NC - 1] + j
                dve.wait_ge(ln_ready, NC)
                dve.wait_ge(yt_ready, k - 1)
                for n in range(4):
                    m = 4 * j + n
                    last = V.tensor_scalar(y[:, k % 2, n, :], pay[:, first + m, 0:D], ln[:, r, 2, m:m + 1],
                                           ln[:, r, 5, m:m + 1], ALU.mult, ALU.add)
                last.then_inc(y_last, 1)

            def row_factors(c):
                r, (first, count) = (c + 1) % 2, CHUNKS[c]
                m = slice(0, count)
                row = pay[:, first:first + count, :]
                dve.wait_ge(ln_ready, c + 1)
                dve.wait_ge(root_ready, 4 + 2 * c)
                link(V.reciprocal(mom[:, 4, m], ln[:, r, 4, m]))
                link(V.scalar_tensor_tensor(out=row[:, :, RSTD], in0=mom[:, 4, m], scalar=S64, in1=ln[:, r, 2, m],
                                            op0=ALU.mult, op1=ALU.mult))
                link(V.tensor_tensor(row[:, :, NBIAS], mom[:, 3, m], row[:, :, RSTD], ALU.mult))

            def over(v):
                return v.rearrange("p (n o) -> p n o", o=1).to_broadcast([128, v.shape[1], E])

            def top1(c):
                dve.wait_ge(logits_ready, FIRST4[c + 1])
                first, count = CHUNKS[c]
                m = slice(0, count)
                brbb = brb[:, :].rearrange("p (o e) -> p o e", o=1).to_broadcast([128, count, E])
                V.tensor_tensor(logit[:, m, :], bank[7][:, 0:count * E].rearrange("p (n e) -> p n e", e=E), brbb, ALU.add)\
                    .then_inc(logits_taken, 1)
                dve.wait_ge(logits_taken, c + 1)
                choice(c, 0)

            def choice(c, k):
                first, count = CHUNKS[c]
                m = slice(0, count)
                revb = rev[:, :].rearrange("p (o e) -> p o e", o=1).to_broadcast([128, count, E])
                link(V.tensor_reduce(small[:, k, m], logit[:, m, :], AX_X, ALU.max))
                link(V.tensor_tensor(pick[:, m, :], logit[:, m, :], over(small[:, k, m]), ALU.is_ge))
                link(V.tensor_tensor(score[:, m, :], pick[:, m, :], revb, ALU.mult))
                link(V.tensor_reduce(small[:, 2 + k, m], score[:, m, :], AX_X, ALU.max))
                if k == 0:
                    link(V.tensor_tensor(pick[:, m, :], revb, over(small[:, 2, m]), ALU.is_equal))
                    link(V.scalar_tensor_tensor(out=logit[:, m, :], in0=pick[:, m, :], scalar=NEG,
                                                in1=logit[:, m, :], op0=ALU.mult, op1=ALU.add))
                if k == 1:
                    V.tensor_tensor(small[:, 5, m], small[:, 1, m], small[:, 0, m], ALU.subtract).then_inc(gap_ready, 1)

            def pair(c):
                first, count = CHUNKS[c]
                m = slice(0, count)
                V.tensor_tensor(small[:, 7, m], small[:, 2, m], small[:, 3, m], ALU.max)
                V.tensor_tensor(small[:, 8, m], small[:, 2, m], small[:, 3, m], ALU.min)
                link(V.tensor_tensor(small[:, 9, m], small[:, 2, m], small[:, 3, m], ALU.is_gt))
                V.tensor_scalar(small[:, 10, m], small[:, 7, m], -0.5, E / 2.0, ALU.mult, ALU.add)
                link(V.tensor_tensor(small[:, 11, m], small[:, 7, m], small[:, 8, m], ALU.subtract))
                link(V.scalar_tensor_tensor(out=small[:, 12, m], in0=small[:, 7, m], scalar=E - 1.0,
                                            in1=small[:, 10, m], op0=ALU.add, op1=ALU.mult))
                link(V.scalar_tensor_tensor(out=small[:, 13, m], in0=small[:, 12, m], scalar=-1.0,
                                            in1=small[:, 11, m], op0=ALU.add, op1=ALU.add))
                link(V.tensor_tensor(
                    by_pair(onehot, count), small[:, 13, m].rearrange("p (o n) -> p o n", o=1).to_broadcast([128, PAIRS, count]),
                    pairs[:, :].rearrange("p (a o) -> p a o", o=1).to_broadcast([128, PAIRS, count]), ALU.is_equal))
                flat_size = PAIRS * count
                link(V.tensor_tensor_scan(running[:, 0:flat_size], restart[count][:, :], onehot[:, 0:flat_size], 0.0,
                                          ALU.mult, ALU.add))
                V.tensor_tensor(seen[:, c + 1, :], seen[:, c, :], by_pair(running, count)[:, :, count - 1], ALU.add).then_inc(seen_ready, 1)
                V.tensor_scalar(small[:, 14, m], small[:, 13, m], float(REGION * 128), None, ALU.mult).then_inc(hot_ready, 1)

            def weights(c):
                first, count = CHUNKS[c]
                m = slice(0, count)
                dve.wait_ge(exp_ready, c + 1)
                link(V.tensor_scalar(small[:, 10, m], small[:, 6, m], 1.0, S4096, ALU.add, ALU.mult))
                link(V.reciprocal(small[:, 11, m], small[:, 10, m]))
                link(V.tensor_tensor(small[:, 12, m], small[:, 6, m], small[:, 11, m], ALU.mult))
                link(V.tensor_tensor(small[:, 10, m], small[:, 11, m], small[:, 12, m], ALU.subtract))
                link(V.tensor_tensor(small[:, 15, m], small[:, 10, m], small[:, 9, m], ALU.mult))
                row = pay[:, first:first + count, :]
                V.tensor_tensor(row[:, :, WA], small[:, 12, m], small[:, 15, m], ALU.add)
                V.tensor_tensor(row[:, :, WB], small[:, 11, m], small[:, 15, m], ALU.subtract)

            def place(c):
                dve.wait_ge(rank_ready, c + 1)
                half = PAIRS // 2
                first, count = CHUNKS[c]
                m = slice(0, count)
                for b in range(2):
                    s = slice(b * half, (b + 1) * half)
                    last = V.tensor_tensor(by_pair(rank, count)[:, s, :], bank[5 + b][:, 0:half * count].rearrange("p (a n) -> p a n", n=count),
                                           by_pair(onehot, count)[:, s, :], ALU.mult)
                last.then_inc(rank_taken, 1)
                dve.wait_ge(rank_taken, c + 1)
                link(V.tensor_reduce(small[:, 12, m], by_pair(rank, count).rearrange("p a n -> p n a"), AX_X, ALU.add))
                V.tensor_tensor(slot[:, first:first + count], small[:, 12, m], small[:, 14, m], ALU.add)\
                    .then_inc(slots_ready, 1)

            dve.wait_ge(in_gw, 16 * 5)
            V.tensor_reduce(fstat[:, 0:1], fus[:, :], AX_X, ALU.max, negate=True).then_inc(fmax_ready, 1)
            stats(0, 0)
            stats(0, 1)
            dve.wait_ge(fexp_ready, 1)
            link(V.reciprocal(fstat[:, 2:3], fstat[:, 1:2]))
            link(V.tensor_scalar(fus[:, :], fus[:, :], fstat[:, 2:3], None, ALU.mult))
            link(V.tensor_tensor(wb2[:, :, :], wb2[:, :, :],
                                 fus[:, :].rearrange("p (g o) -> p g o", o=1).to_broadcast([128, 5, D]), ALU.mult))

            def blocks(i):
                g, q = QUADS[i]
                p, s, n = ROWS[g], SIZE[g], BATCHES[g]
                dve.wait_ge(in_pack[i % 2], 32 * (i // 2 + 1))
                if i >= 3:
                    dve.wait_ge(o_ready, i - 2)
                for k in range(4):
                    last = V.tensor_tensor(
                        bd[0:p, i % 3, k, 0:p].rearrange("p (b n) -> p b n", n=s),
                        npack[0:p, i % 2, k, 0:s].rearrange("p (o n) -> p o n", o=1).to_broadcast([p, n, s]),
                        mask[min(g, 3)][0:p, :].rearrange("p (b o) -> p b o", o=1).to_broadcast([p, n, s]), ALU.mult)
                last.then_inc(bd_ready, 1)

            def take_z(i):
                p4 = 4 * ROWS[QUADS[i][0]]
                dve.wait_ge(z_ready, i + 1)
                if i >= 2:
                    dve.wait_ge(h_ready, i - 1)
                V.tensor_copy(zs[:, i % 2, 0:p4], bank[0][:, 0:p4]).then_inc(zs_ready, 1)

            def take_s(i):
                p = ROWS[QUADS[i][0]]
                dve.wait_ge(s_ready, i + 1)
                if i >= 2:
                    dve.wait_ge(o_ready, i - 1)
                V.tensor_copy(ss[0:p, i % 2, :, :], bank[3][0:p, :].rearrange("p (k d) -> p k d", d=D)).then_inc(ss_ready, 1)

            def take_o(i):
                g = QUADS[i][0]
                p = ROWS[g]
                dve.wait_ge(o_ready, i + 1)
                if i >= 2:
                    dve.wait_ge(go_out[i % 2], 16 * (i // 2))
                V.scalar_tensor_tensor(
                    out=gpost[0:p, i % 2, :, :], in0=bank[4][0:p, :].rearrange("p (k d) -> p k d", d=D),
                    scalar=fus[0:p, g:g + 1],
                    in1=wb2[0:p, g, :].rearrange("p (o d) -> p o d", o=1).to_broadcast([p, 4, D]),
                    op0=ALU.mult, op1=ALU.add).then_inc(o_taken, 1)

            def mix_for(e):
                if e == 0:
                    dve.wait_ge(in_experts, 16 * (1 + HC + 3))
                    link(V.tensor_scalar(g64[:, :], lng[:, :], S64, None, ALU.mult))
                elif e >= 2:
                    dve.wait_ge(w1_ready, e - 1)
                V.tensor_scalar(pick64[:, e % 2, 0:1], ident[0:E, e:e + 1], S64, None, ALU.mult)
                link(V.tensor_scalar(mix[:, e % 2, :], ident[:, :], g64[:, e:e + 1], None, ALU.mult))
                link(V.tensor_scalar(mix[0:1, e % 2, :], ones64[0:1, :], lng[0:1, e:e + 1], -1.0, ALU.mult, ALU.mult))
                V.tensor_scalar(mix[:, e % 2, 0:1], lnb[:, e:e + 1], S64, None, ALU.mult).then_inc(mix_ready, 1)

            def low1(e):
                dve.wait_ge(w1_high, e + 1)
                V.tensor_tensor(w1s[:, e, 1, :], w_bank(e)[:, :], w1s[:, e, 0, :], ALU.subtract).then_inc(w1_low, 1)

            def low2(e):
                dve.wait_ge(w2_high, e + 1)
                V.scalar_tensor_tensor(out=w2s[:, e, :, 1, :], in0=w2f[:, e, :, :], scalar=S64,
                                       in1=w2s[:, e, :, 0, :], op0=ALU.mult, op1=ALU.subtract).then_inc(w2_low, 1)

            factors(0)
            blocks(0)
            blocks(1)
            take_z(0)
            take_z(1)
            row_factors(0)
            for i in range(NQ):
                take_s(i)
                if i + 2 < NQ:
                    blocks(i + 2)
                if i in STATS_AT:
                    stats(*STATS_AT[i])
                if i - 1 in FACTORS_AT:
                    row_factors(FACTORS_AT[i - 1])
                if i in TOP2_AT:
                    top1(TOP2_AT[i])
                if i in PAIR_AT:
                    pair(PAIR_AT[i])
                if i in PLACE_AT:
                    weights(PLACE_AT[i])
                    place(PLACE_AT[i])
                take_o(i)
                if i + 2 < NQ:
                    take_z(i + 2)
                if i in TOP2_AT:
                    choice(TOP2_AT[i], 1)
                if i in FACTORS_AT:
                    factors(FACTORS_AT[i])
                if SECOND_AT <= i < SECOND_AT + E - 1:
                    low2(i - SECOND_AT)
                if i >= FIRST_AT:
                    low1(i - FIRST_AT)
                if i >= FIRST_AT - 1:
                    mix_for(i - FIRST_AT + 1)
            mix_for(EARLY + 1)
            low1(EARLY)
            stats(NC - 1, 0)
            factors(NC - 1)
            normalise_last(0)
            normalise_last(1)
            row_factors(NC - 1)
            low1(EARLY + 1)
            mix_for(EARLY + 2)
            normalise_last(2)
            normalise_last(3)
            mix_for(EARLY + 3)
            top1(NC - 1)
            choice(NC - 1, 1)
            pair(NC - 1)
            weights(NC - 1)
            place(NC - 1)
            dve.wait_ge(cnt_ready, 1)
            V.tensor_tensor(padint[:, :], bank[2][0:1, 0:PAIRS], padrow[:, 0, :], ALU.add)
            link(V.tensor_scalar(tint[:, 0:1], bank[7][0:PAIRS, 0:1], 127.0, None, ALU.add))
            link(V.tensor_scalar(tint[:, 1:2], tint[:, 0:1], 7, None, ALU.arith_shift_right))
            V.tensor_copy(tcnt[:, 1:2], tint[:, 1:2]).then_inc(ntile_ready, 1)
            dve.wait_ge(tincl_ready, 1)
            link(V.tensor_copy(tcnt[:, 2:3], bank[3][0:PAIRS, 0:1]))
            link(V.tensor_tensor(tcnt[:, 3:4], tcnt[:, 2:3], tcnt[:, 1:2], ALU.subtract))
            V.tensor_copy(tcnt[:, 4:6], bank[3][0:PAIRS, 1:3])
            V.tensor_tensor(tcnt[:, 6:7], bank[3][0:PAIRS, 3:4], tcnt[:, 3:4], ALU.subtract)
            V.tensor_scalar(ahead[:, :], tline[:, :], tcnt[:, 3:4], None, ALU.is_ge)
            link(V.tensor_scalar(inpair[:, :], tline[:, :], tcnt[:, 2:3], None, ALU.is_ge))
            V.tensor_tensor(inpair[:, :], ahead[:, :], inpair[:, :], ALU.subtract).then_inc(member_ready, 1)
            dve.wait_ge(trow_ready, 1)
            V.tensor_copy(experts[:, :, :].rearrange("p t k -> p k t"),
                          bank[4][0:1, 0:2 * TABLE].rearrange("p (k t) -> p k t", k=2))
            link(V.scalar_tensor_tensor(out=ahead[0:1, :], in0=bank[4][0:1, 2 * TABLE:3 * TABLE], scalar=2.0 * DUMMY,
                                        in1=tline[0:1, :], op0=ALU.add, op1=ALU.add))
            V.tensor_scalar(place_of[:, :], ahead[0:1, :], float(DUMMY), None, ALU.min).then_inc(table_ready, 1)

            V.memset(b2s[:, :, :], 0.0).then_inc(b2_cleared, 1)
            for e in range(EARLY + 4, E):
                mix_for(e)
            for e in range(EARLY + 2, E):
                low1(e)
            low2(E - 1)
            dve.wait_ge(in_b2, 32)
            dve.wait_ge(b2_cleared, 1)
            by_e = (lambda v: v.rearrange("p (e d) -> p e d", e=E))
            V.tensor_scalar(b2s[0:1, :, :], by_e(b2f[0:1, :]), S64, None, ALU.mult)
            link(V.tensor_scalar(b2hi[32:33, 0:E * D], b2f[32:33, :], S64, None, ALU.mult))
            V.scalar_tensor_tensor(out=b2s[32:33, :, :], in0=by_e(b2f[32:33, :]), scalar=S64, in1=by_e(b2hi[32:33, 0:E * D]),
                                   op0=ALU.mult, op1=ALU.subtract).then_inc(b2_done, 1)

            def load_pair(t):
                return load_values(experts[0:1, bass.ds(t, 1), :].rearrange("p t k -> p (t k)"), mybir.EngineType.DVE, E - 1)

            def copy_weights(v, e):
                V.tensor_copy(wbuf[v % WRING], blocks_w[:, bass.ds(e, 1), :].rearrange("p e w -> p (e w)"))\
                    .then_inc(w_copied, 1)

            def low(v, n):
                dve.wait_ge(high_ready, n)
                V.scalar_tensor_tensor(out=hl[v % 4], in0=hid[v % 4], scalar=S64, in1=hh[v % 4], op0=ALU.mult,
                                       op1=ALU.subtract).then_inc(split_ready, 1)

            def combine_a(s):
                r, b = prow[s % RING], bank[6 + s % 2]
                V.scalar_tensor_tensor(out=orow[s % RING], in0=b[:, 0:D], scalar=r[:, WA:WA + 1], in1=r[:, 0:D],
                                       op0=ALU.mult, op1=ALU.add).then_inc(half_ready, 2)

            def combine_b(s, n):
                r, b = prow[s % RING], bank[6 + s % 2]
                dve.wait_ge(half_ready, n)
                V.scalar_tensor_tensor(out=orow[s % RING], in0=b[:, D:2 * D], scalar=r[:, WB:WB + 1], in1=orow[s % RING],
                                       op0=ALU.mult, op1=ALU.add).then_inc(row_ready, 2)

            dve.sem_inc(split_ready, 4)
            dve.sem_inc(half_ready, 5)
            dve.wait_ge(rows_out, 16 * N)
            dve.wait_ge(table_ready, 1)
            dve.wait_ge(b2_done, 1)
            dve.wait_ge(w1_low, E)
            dve.wait_ge(w2_low, E)
            for v, e in enumerate(load_pair(0)):
                copy_weights(v, e)
            for u in range(UNITS):
                t = u // 2
                if u % 2 == 0:
                    pair_ab = load_pair(t + 1)
                dve.wait_ge(e_ready, u + 1)
                if u % 2 == 0 and t >= 3:
                    combine_a(t - 3)
                copy_weights(u + 2, pair_ab[u % 2])
                if u % 2 == 0 and t >= 3:
                    combine_b(t - 3, u + 1)
                if u >= 2:
                    low(u - 2, u + 1)
            with dve.Fori(1, TILES // RING) as i:
                for v in range(UNITS):
                    n = dve.snap(i * UNITS + (v + 1))
                    if v % 2 == 0:
                        pair_ab = load_pair(i * RING + (v // 2 + 1))
                    dve.wait_ge(e_ready, n)
                    if v % 2 == 0:
                        combine_a(v // 2 - 3)
                    copy_weights(v + 2, pair_ab[v % 2])
                    if v % 2 == 0:
                        combine_b(v // 2 - 3, n)
                    low(v - 2, n)
            for u in range(2 * TILES, 2 * TILES + 5):
                t = u // 2
                dve.wait_ge(e_ready, u + 1)
                if u % 2 == 0:
                    combine_a(t - 3)
                    combine_b(t - 3, u + 1)
                if u < 2 * TILES + 2:
                    low(u - 2, u + 1)


_INS = ['x', 'adj', 'L0_gnn_W1', 'L0_gnn_b1', 'L0_gnn_W2', 'L0_gnn_b2', 'L0_gnn_fusion_w', 'L0_ffn_Wr', 'L0_ffn_br',
        'L0_ffn_ln_g', 'L0_ffn_ln_b', 'L0_ffn_W1', 'L0_ffn_b1', 'L0_ffn_W2', 'L0_ffn_b2']


def kernel(**inputs):
    import numpy as _np
    import concourse.bacc as _bacc
    from concourse import mybir as _mybir
    from concourse.bass_utils import run_bass_kernel_spmd as _run

    nc = _bacc.Bacc("TRN2", target_bir_lowering=False, num_devices=1)
    arrays, args = {}, []
    for name in _INS:
        a = _np.ascontiguousarray(inputs[name])
        arrays[f"in_{name}"] = a
        args.append(nc.dram_tensor(f"in_{name}", a.shape, _mybir.dt.from_np(a.dtype), kind="ExternalInput").ap())
    args.append(nc.dram_tensor("out_0", (B, N, D), _mybir.dt.float32, kind="ExternalOutput").ap())
    build(nc, *args)
    r = _run(nc, [arrays], core_ids=[0])
    return r.results[0]["out_0"]
```
